# Optimizing a Trainium2 kernel written in Bass

```python
import numpy as np
import jax
import jax.numpy as jnp

def _softmax(x, axis=-1):
    return jax.nn.softmax(x, axis=axis)

def _gelu(x):
    return jax.nn.gelu(x, approximate=True)

def _silu(x):
    return jax.nn.silu(x)

def _sigmoid(x):
    return jax.nn.sigmoid(x)

def _layernorm(x, axis=-1, eps=1e-05):
    m = jnp.mean(x, axis=axis, keepdims=True)
    v = jnp.var(x, axis=axis, keepdims=True)
    return (x - m) / jnp.sqrt(v + eps)

def _scatter_add(tgt, idx, src, axis=0):
    return tgt.at[idx].add(src)

def _segment_sum(src, seg, n):
    return jax.ops.segment_sum(src, seg, n)
kernel_name = 'mk_seq_postln_d1_jaxref_r8_a0b8cd'

def setup_inputs(seed: int=0):
    np.random.seed(seed)
    _w = jnp.asarray

    def _L0_attn_setup():
        import jax, jax.numpy as jnp
        import numpy as np
        B, N, D = (2, 256, 128)
        H, M = (8, 64)
        DK = D // H
        EPS = 1e-05

        def _gsa(q, k, v, s, g):
            b = q.shape[1]

            def step1(hk, t):
                q_t, k_t, s_t, g_t = t
                hk = hk * jnp.exp(g_t)[:, :, None, :] + k_t[..., :, None] * s_t[..., None, :]
                ok = jnp.einsum('bhk,bhkm->bhm', q_t, hk)
                return (hk, ok)
            hk0 = jnp.zeros((b, H, DK, M), q.dtype)
            _, ok = jax.lax.scan(step1, hk0, (q, k, s, g))
            qv = jax.nn.softmax(ok, axis=-1)

            def step2(hv, t):
                qv_t, s_t, v_t, g_t = t
                hv = hv * jnp.exp(g_t)[..., :, None] + s_t[..., :, None] * v_t[..., None, :]
                ov = jnp.einsum('bhm,bhmv->bhv', qv_t, hv)
                return (hv, ov)
            hv0 = jnp.zeros((b, H, M, DK), q.dtype)
            _, ov = jax.lax.scan(step2, hv0, (qv, s, v, g))
            return ov
        key = jax.random.key(seed)
        ks = jax.random.split(key, 9)
        std = 0.02
        return {'x': jax.random.normal(ks[0], (B, N, D), jnp.float32), 'Wq': jax.random.normal(ks[1], (D, D), jnp.float32) * std, 'Wk': jax.random.normal(ks[2], (D, D), jnp.float32) * std, 'Wv': jax.random.normal(ks[3], (D, D), jnp.float32) * std, 'Wf1': jax.random.normal(ks[4], (D, DK), jnp.float32) * std, 'Wf2': jax.random.normal(ks[5], (DK, H * M), jnp.float32) * std, 'Wg1': jax.random.normal(ks[6], (D, DK), jnp.float32) * std, 'Wg2': jax.random.normal(ks[7], (DK, D), jnp.float32) * std, 'Wo': jax.random.normal(ks[8], (D, D), jnp.float32) * std, 'norm_w': jnp.ones((D,), jnp.float32)}
    _L0_attn_in = _L0_attn_setup()

    def _L0_ffn_setup():
        import jax, jax.numpy as jnp
        import numpy as np
        D_MODEL = 128
        N_HEADS = 16
        HEAD_DIM = D_MODEL // N_HEADS
        FFN_DIM = 512
        N_EXPERTS = 8
        TOP_K = 2
        BATCH = 4
        SEQ = 128

        def _layernorm(x, w, b, eps=1e-05):
            mu = jnp.mean(x, axis=-1, keepdims=True)
            var = jnp.mean(jnp.square(x - mu), axis=-1, keepdims=True)
            return (x - mu) * jax.lax.rsqrt(var + eps) * w + b

        def _causal_attention(nx, Wqkv, bqkv, Wo, bo):
            B, S, D = nx.shape
            qkv = nx @ Wqkv + bqkv
            q, k, v = jnp.split(qkv, 3, axis=-1)
            q = q.reshape(B, S, N_HEADS, HEAD_DIM)
            k = k.reshape(B, S, N_HEADS, HEAD_DIM)
            v = v.reshape(B, S, N_HEADS, HEAD_DIM)
            scores = jnp.einsum('bqhd,bkhd->bhqk', q, k) / jnp.sqrt(jnp.float32(HEAD_DIM))
            causal = jnp.tril(jnp.ones((S, S), bool))
            scores = jnp.where(causal, scores, jnp.finfo(scores.dtype).min)
            attn = jax.nn.softmax(scores, axis=-1)
            out = jnp.einsum('bhqk,bkhd->bqhd', attn, v).reshape(B, S, D)
            return out @ Wo + bo

        def _moe_ffn(nx, gate_W, fc1_w, fc1_b, fc2_w, fc2_b):
            gate_logits = nx @ gate_W
            topk_vals, topk_idx = jax.lax.top_k(gate_logits, TOP_K)
            gate_w = jax.nn.softmax(topk_vals, axis=-1)
            dense_gates = jnp.sum(jax.nn.one_hot(topk_idx, N_EXPERTS, dtype=nx.dtype) * gate_w[..., None], axis=-2)
            moe_out = jnp.zeros_like(nx)
            for e in range(N_EXPERTS):
                h = jax.nn.gelu(jnp.einsum('bsd,fd->bsf', nx, fc1_w[e]) + fc1_b[e], approximate=False)
                y = jnp.einsum('bsf,df->bsd', h, fc2_w[e]) + fc2_b[e]
                moe_out = moe_out + y * dense_gates[..., e:e + 1]
            return moe_out
        key = jax.random.key(seed)
        ks = jax.random.split(key, 12)
        s = lambda k, shape, scale: jax.random.normal(k, shape, dtype=jnp.float32) * scale
        inp = {'x': s(ks[0], (BATCH, SEQ, D_MODEL), 1.0), 'ln1_w': jnp.ones((D_MODEL,), jnp.float32), 'ln1_b': jnp.zeros((D_MODEL,), jnp.float32), 'ln2_w': jnp.ones((D_MODEL,), jnp.float32), 'ln2_b': jnp.zeros((D_MODEL,), jnp.float32), 'Wqkv': s(ks[1], (D_MODEL, 3 * D_MODEL), 0.02), 'bqkv': jnp.zeros((3 * D_MODEL,), jnp.float32), 'Wo': s(ks[2], (D_MODEL, D_MODEL), 0.02), 'bo': jnp.zeros((D_MODEL,), jnp.float32), 'gate_W': s(ks[3], (D_MODEL, N_EXPERTS), 0.02), 'fc1_w': s(ks[4], (N_EXPERTS, FFN_DIM, D_MODEL), (2.0 / D_MODEL) ** 0.5), 'fc1_b': jnp.zeros((N_EXPERTS, FFN_DIM), jnp.float32), 'fc2_w': s(ks[5], (N_EXPERTS, D_MODEL, FFN_DIM), (1.0 / FFN_DIM) ** 0.5), 'fc2_b': jnp.zeros((N_EXPERTS, D_MODEL), jnp.float32)}
        return inp
    _L0_ffn_in = _L0_ffn_setup()
    _d = {'L0_attn_x': _L0_attn_in['x'], 'L0_attn_Wq': _L0_attn_in['Wq'], 'L0_attn_Wk': _L0_attn_in['Wk'], 'L0_attn_Wv': _L0_attn_in['Wv'], 'L0_attn_Wf1': _L0_attn_in['Wf1'], 'L0_attn_Wf2': _L0_attn_in['Wf2'], 'L0_attn_Wg1': _L0_attn_in['Wg1'], 'L0_attn_Wg2': _L0_attn_in['Wg2'], 'L0_attn_Wo': _L0_attn_in['Wo'], 'L0_attn_norm_w': _L0_attn_in['norm_w'], 'L0_ffn_ln1_w': _L0_ffn_in['ln1_w'], 'L0_ffn_ln1_b': _L0_ffn_in['ln1_b'], 'L0_ffn_ln2_w': _L0_ffn_in['ln2_w'], 'L0_ffn_ln2_b': _L0_ffn_in['ln2_b'], 'L0_ffn_Wqkv': _L0_ffn_in['Wqkv'], 'L0_ffn_bqkv': _L0_ffn_in['bqkv'], 'L0_ffn_Wo': _L0_ffn_in['Wo'], 'L0_ffn_bo': _L0_ffn_in['bo'], 'L0_ffn_gate_W': _L0_ffn_in['gate_W'], 'L0_ffn_fc1_w': _L0_ffn_in['fc1_w'], 'L0_ffn_fc1_b': _L0_ffn_in['fc1_b'], 'L0_ffn_fc2_w': _L0_ffn_in['fc2_w'], 'L0_ffn_fc2_b': _L0_ffn_in['fc2_b']}
    _x0 = _d['L0_attn_x']
    _d['L0_attn_x'] = jax.random.normal(jax.random.fold_in(jax.random.key(seed), 1), (32, 256, 128), dtype=_x0.dtype)
    del _x0
    return _d

def reference(L0_attn_x, L0_attn_Wq, L0_attn_Wk, L0_attn_Wv, L0_attn_Wf1, L0_attn_Wf2, L0_attn_Wg1, L0_attn_Wg2, L0_attn_Wo, L0_attn_norm_w, L0_ffn_ln1_w, L0_ffn_ln1_b, L0_ffn_ln2_w, L0_ffn_ln2_b, L0_ffn_Wqkv, L0_ffn_bqkv, L0_ffn_Wo, L0_ffn_bo, L0_ffn_gate_W, L0_ffn_fc1_w, L0_ffn_fc1_b, L0_ffn_fc2_w, L0_ffn_fc2_b):

    def _L0_attn_ref(x, Wq, Wk, Wv, Wf1, Wf2, Wg1, Wg2, Wo, norm_w):
        import jax, jax.numpy as jnp
        import numpy as np
        B, N, D = (2, 256, 128)
        H, M = (8, 64)
        DK = D // H
        EPS = 1e-05

        def _gsa(q, k, v, s, g):
            b = q.shape[1]

            def step1(hk, t):
                q_t, k_t, s_t, g_t = t
                hk = hk * jnp.exp(g_t)[:, :, None, :] + k_t[..., :, None] * s_t[..., None, :]
                ok = jnp.einsum('bhk,bhkm->bhm', q_t, hk)
                return (hk, ok)
            hk0 = jnp.zeros((b, H, DK, M), q.dtype)
            _, ok = jax.lax.scan(step1, hk0, (q, k, s, g))
            qv = jax.nn.softmax(ok, axis=-1)

            def step2(hv, t):
                qv_t, s_t, v_t, g_t = t
                hv = hv * jnp.exp(g_t)[..., :, None] + s_t[..., :, None] * v_t[..., None, :]
                ov = jnp.einsum('bhm,bhmv->bhv', qv_t, hv)
                return (hv, ov)
            hv0 = jnp.zeros((b, H, M, DK), q.dtype)
            _, ov = jax.lax.scan(step2, hv0, (qv, s, v, g))
            return ov
        b, n, d = x.shape
        q = jax.nn.silu(x @ Wq).reshape(b, n, H, DK)
        k = jax.nn.silu(x @ Wk).reshape(b, n, H, DK)
        v = (x @ Wv).reshape(b, n, H, DK)
        f = x @ Wf1 @ Wf2
        log_f = jax.nn.log_sigmoid(f).reshape(b, n, H, M)
        s = 1.0 - jnp.exp(log_f)
        tm = lambda a: jnp.swapaxes(a, 0, 1)
        ov = _gsa(tm(q), tm(k), tm(v), tm(s), tm(log_f))
        out = tm(ov).reshape(b, n, d)
        gate = x @ Wg1 @ Wg2
        out = out * jax.nn.sigmoid(gate)
        og = out.reshape(b, n, H, DK)
        og = og * jax.lax.rsqrt(jnp.mean(og * og, axis=-1, keepdims=True) + EPS)
        out = og.reshape(b, n, d) * norm_w
        return out @ Wo

    def _L0_ffn_ref(x, ln1_w, ln1_b, ln2_w, ln2_b, Wqkv, bqkv, Wo, bo, gate_W, fc1_w, fc1_b, fc2_w, fc2_b):
        import jax, jax.numpy as jnp
        import numpy as np
        D_MODEL = 128
        N_HEADS = 16
        HEAD_DIM = D_MODEL // N_HEADS
        FFN_DIM = 512
        N_EXPERTS = 8
        TOP_K = 2
        BATCH = 4
        SEQ = 128

        def _layernorm(x, w, b, eps=1e-05):
            mu = jnp.mean(x, axis=-1, keepdims=True)
            var = jnp.mean(jnp.square(x - mu), axis=-1, keepdims=True)
            return (x - mu) * jax.lax.rsqrt(var + eps) * w + b

        def _causal_attention(nx, Wqkv, bqkv, Wo, bo):
            B, S, D = nx.shape
            qkv = nx @ Wqkv + bqkv
            q, k, v = jnp.split(qkv, 3, axis=-1)
            q = q.reshape(B, S, N_HEADS, HEAD_DIM)
            k = k.reshape(B, S, N_HEADS, HEAD_DIM)
            v = v.reshape(B, S, N_HEADS, HEAD_DIM)
            scores = jnp.einsum('bqhd,bkhd->bhqk', q, k) / jnp.sqrt(jnp.float32(HEAD_DIM))
            causal = jnp.tril(jnp.ones((S, S), bool))
            scores = jnp.where(causal, scores, jnp.finfo(scores.dtype).min)
            attn = jax.nn.softmax(scores, axis=-1)
            out = jnp.einsum('bhqk,bkhd->bqhd', attn, v).reshape(B, S, D)
            return out @ Wo + bo

        def _moe_ffn(nx, gate_W, fc1_w, fc1_b, fc2_w, fc2_b):
            gate_logits = nx @ gate_W
            topk_vals, topk_idx = jax.lax.top_k(gate_logits, TOP_K)
            gate_w = jax.nn.softmax(topk_vals, axis=-1)
            dense_gates = jnp.sum(jax.nn.one_hot(topk_idx, N_EXPERTS, dtype=nx.dtype) * gate_w[..., None], axis=-2)
            moe_out = jnp.zeros_like(nx)
            for e in range(N_EXPERTS):
                h = jax.nn.gelu(jnp.einsum('bsd,fd->bsf', nx, fc1_w[e]) + fc1_b[e], approximate=False)
                y = jnp.einsum('bsf,df->bsd', h, fc2_w[e]) + fc2_b[e]
                moe_out = moe_out + y * dense_gates[..., e:e + 1]
            return moe_out
        nx = _layernorm(x, ln1_w, ln1_b)
        attn_out = _causal_attention(nx, Wqkv, bqkv, Wo, bo)
        x = x + attn_out
        nx2 = _layernorm(x, ln2_w, ln2_b)
        moe_out = _moe_ffn(nx2, gate_W, fc1_w, fc1_b, fc2_w, fc2_b)
        return x + moe_out
    x = L0_attn_x
    x = _layernorm(x + _L0_attn_ref(x, L0_attn_Wq, L0_attn_Wk, L0_attn_Wv, L0_attn_Wf1, L0_attn_Wf2, L0_attn_Wg1, L0_attn_Wg2, L0_attn_Wo, L0_attn_norm_w), axis=-1)
    x = _layernorm(x + _L0_ffn_ref(x, L0_ffn_ln1_w, L0_ffn_ln1_b, L0_ffn_ln2_w, L0_ffn_ln2_b, L0_ffn_Wqkv, L0_ffn_bqkv, L0_ffn_Wo, L0_ffn_bo, L0_ffn_gate_W, L0_ffn_fc1_w, L0_ffn_fc1_b, L0_ffn_fc2_w, L0_ffn_fc2_b), axis=-1)
    return x

_drawn_inputs = setup_inputs


def setup_inputs(seed=0):
    import zlib

    import numpy as np

    out = dict(_drawn_inputs(seed))
    spreads = {'L0_attn_norm_w': (1.0, 0.2),
     'L0_ffn_ln1_w': (1.0, 0.6),
     'L0_ffn_ln1_b': (0.0, 0.323),
     'L0_ffn_ln2_w': (1.0, 0.2),
     'L0_ffn_ln2_b': (0.0, 0.1),
     'L0_ffn_bqkv': (0.0, 0.1),
     'L0_ffn_bo': (0.0, 0.1),
     'L0_ffn_fc1_b': (0.0, 0.346),
     'L0_ffn_fc2_b': (0.0, 0.1)}
    factors = {'L0_attn_Wq': 8.0,
     'L0_attn_Wk': 8.0,
     'L0_attn_Wf1': 8.0,
     'L0_attn_Wf2': 6.795,
     'L0_attn_Wg1': 4.075,
     'L0_attn_Wg2': 3.691}
    for name, (base, spread) in spreads.items():
        noise = np.random.default_rng([zlib.crc32(name.encode()), seed]).standard_normal(out[name].shape)
        drawn = base * np.exp(spread * noise) if base else spread * noise
        out[name] = jnp.asarray(drawn.astype(out[name].dtype))
    for name, factor in factors.items():
        out[name] = (out[name] * factor).astype(out[name].dtype)
    return out
```

```python
from contextlib import ExitStack

import numpy as np

import concourse.bass as bass
from concourse import mybir

F32 = mybir.dt.float32
BF16 = mybir.dt.bfloat16
U32 = mybir.dt.uint32
ALU = mybir.AluOpType
ACT = mybir.ActivationFunctionType
AX_X = mybir.AxisListType.X

B, N, D = 32, 256, 128
T = N // 128
H, DK, M = 8, 16, 64
HM = H * M
HP = H // 2
C = 64
NC_STATES = N // C - 1
NH, HD = 16, 8
G4 = NH // 4
NE, F = 8, 512
FC = F // 128
EPS = 1e-5
PAIRS = [(0, 0), (0, 1), (0, 2), (1, 0), (1, 1), (2, 0)]
KS = 96
MAXROW = 96
BIG = -1e30
FMAX = 3e38


def build(nc, x_tok, x_T, w_qk, w_v, w_fg, w_f2, w_g2, w_o, norm_w, ln1, ln2, w2_qk, w2_v, b2_qk, bv, w2_o, bo,
          gate_w, fc1, fc1_b, fc2, fc2_b, c_ident, c_mid, c_win, c_wincol, c_causal, c_headmask, c_offhead,
          c_pairmask, c_negmask, c_negmaskT, c_identb, c_chunkmask, c_iota, out):
    ctx = ExitStack()
    with ctx:
        def sb(name, shape, dt=F32):
            return ctx.enter_context(nc.sbuf_tensor(name, shape, dt))

        def sem(name):
            return ctx.enter_context(nc.semaphore(name))

        ident = sb("ident", [128, 128])
        identb = sb("identb", [128, 128], BF16)
        mid = sb("mid", [128, 128])
        win = sb("win", [128, 4, 128])
        wincol = sb("wincol", [128, T, 4])
        causal = sb("causal", [128, 128])
        headmask = sb("headmask", [128, H])
        offhead = sb("offhead", [128, HM], BF16)
        pairmask = sb("pairmask", [128, 32])
        negmask = sb("negmask", [128, 2, 512], BF16)
        negmaskT = sb("negmaskT", [128, 2, 512], BF16)
        chunkmask = sb("chunkmask", [128, 2])
        iota = sb("iota", [128, NE])
        wqk = sb("wqk", [128, 2, 128])
        wv = sb("wv", [128, 128])
        wfg = sb("wfg", [128, 128])
        wf2 = sb("wf2", [128, HM])
        wg2 = sb("wg2", [128, 128])
        wo = sb("wo", [128, 128])
        nw = sb("nw", [128, 1])
        ln1c = sb("ln1c", [128, 2])
        ln2c = sb("ln2c", [128, 2])
        w2qk = sb("w2qk", [128, 2, 128])
        w2v = sb("w2v", [128, 128])
        b2qk = sb("b2qk", [128, 2])
        bvB = sb("bvB", [128, 128])
        w2o = sb("w2o", [128, 128])
        boB = sb("boB", [128, 128])
        gw = sb("gw", [128, NE])
        fc1s = sb("fc1s", [128, NE, F])
        fc1bs = sb("fc1bs", [128, NE * FC])
        fc2s = sb("fc2s", [128, NE, FC, 128])
        fc2bs = sb("fc2bs", [128, 128])
        neghalf = sb("neghalf", [128, 16])
        eps = sb("eps", [128, 16])
        epsdk = sb("epsdk", [128, 16])

        xT = sb("xT", [128, N])
        xt = sb("xt", [128, T, 128])
        qk2 = sb("qk2", [128, 2, N])
        ktm = sb("ktm", [128, T, 2, 128])
        vtok = sb("vtok", [128, T, 128])
        vtm = sb("vtm", [128, T, 2, 128])
        thg = sb("thg", [128, T, 128])
        thf = sb("thf", [128, T, HM])
        lf = sb("lf", [128, T, HM])
        E = sb("E", [128, T, HM])
        EY = sb("EY", [128, T, HM])
        Y = sb("Y", [128, T, HM])
        dm = sb("dm", [128, NC_STATES, HM])
        dv = sb("dv", [128, HP, 4])
        dvm = sb("dvm", [128, NC_STATES, HP, 32])
        state = sb("state", [128, NC_STATES, HM])
        vstate = sb("vstate", [128, NC_STATES, HP, 32])
        vtmp = sb("vtmp", [128, HP, 32])
        PTm = sb("PTm", [128, T, H, 128])
        YTbd = sb("YTbd", [128, T, HP, 2, 128])
        okE = EY
        mx = sb("mx", [128, T, H])
        sm = sb("sm", [128, T, H])
        rs = sb("rs", [128, T, H])
        QET = sb("QET", [128, T, HP, 128])
        og = sb("og", [128, T, 128])
        ms = sb("ms", [128, T, H])
        oT = sb("oT", [128, T, 128])
        r1 = sb("r1", [128, T, 128])
        bn = sb("bn", [128, T, 6])
        mv = sb("mv", [128, T, 2])
        rstd = sb("rstd", [128, 16])
        x1 = sb("x1", [128, T, 128])
        nh = sb("nh", [128, T, 128])
        nxT = sb("nxT", [128, N])
        qkf = sb("qkf", [128, 2, N])
        parts = sb("parts", [128, 3, 2, N], BF16)
        resid = sb("resid", [128, 2, N])
        Qst = sb("Qst", [MAXROW + 3, NH, N], BF16)
        Kst = sb("Kst", [MAXROW + 3, NH, N], BF16)
        vaug = sb("vaug", [128, T, NH, 32])
        nmax = sb("nmax", [128, T, NH])
        mparts = sb("mparts", [128, T, 128])
        mpb = sb("mpb", [128, T, NH], BF16)
        mres = sb("mres", [128, T, NH])
        mT = sb("mT", [3 * NH, N], BF16)
        pT = sb("pT", [128, 2, 3, 512])
        rec = sb("rec", [128, T, NH])
        at = sb("at", [128, T, 128])
        aT = sb("aT", [128, T, 128])
        x2 = sb("x2", [128, T, 128])
        qbd = pT[:].rearrange("p a b c -> p (a b c)")[:, 0:T * H * 128].rearrange("p (t h n) -> p t h n", t=T, h=H)
        thqk = resid
        stmp = resid[:].rearrange("p j n -> p (j n)")
        oT2 = Y[:].rearrange("p t n -> p (t n)").rearrange("p (g n) -> p g n", g=G4)
        fgT = nxT
        sq = at
        nx2T = sb("nx2T", [128, N])
        lg = sb("lg", [128, T, NE])
        top = sb("top", [128, T, 8])
        topi = sb("topi", [128, T, 8], U32)
        topf = sb("topf", [128, T, 8])
        gd = sb("gd", [128, T, 4])
        oh = sb("oh", [128, NE])
        gates = sb("gates", [128, T, 128])
        gatesm = sb("gatesm", [128, T, NE])
        gT = sb("gT", [128, T, 128])
        hx = sb("hx", [128, NE, FC, N])
        acc = sb("acc", [128, T, 128])
        xo = sb("xo", [128, T, 128])
        nop = sb("nop", [128, 1])
        bnm = sb("bnm", [128, T, 6])
        mvm = sb("mvm", [128, T, 2])
        rstdm = sb("rstdm", [128, T])

        psA = ctx.enter_context(nc.psum_tensor("psA", [128, 5, 512], F32))
        psM = ctx.enter_context(nc.psum_tensor("psM", [128, 3, 512], F32))
        scratch = nc.dram_tensor("scratch", (3, 2, 128, N), BF16, kind="Internal").ap()

        s_consts_in = sem("consts_in")
        s_zeroed = sem("zeroed")
        s_wo_scaled = sem("wo_scaled")
        s_x_in = sem("x_in")
        s_qk_ps = sem("qk_ps")
        s_th_qk = sem("th_qk")
        s_qk2_ready = sem("qk2_ready")
        s_fgv_ps = sem("fgv_ps")
        s_fgv_ready = sem("fgv_ready")
        s_vtm_ready = sem("vtm_ready")
        s_f_ps = sem("f_ps")
        s_th_g = sem("th_g")
        s_lnu_ready = sem("lnu_ready")
        s_ls_ready = sem("ls_ready")
        s_kt_ps = sem("kt_ps")
        s_kt_ready = sem("kt_ready")
        s_qbd_ready = sem("qbd_ready")
        s_pt_ps = sem("pt_ps")
        s_pt_ready = sem("pt_ready")
        s_g_ps = sem("g_ps")
        s_ey_ready = sem("ey_ready")
        s_dv_ps = sem("dv_ps")
        s_dv_ready = sem("dv_ready")
        s_dvm_ready = sem("dvm_ready")
        s_y_ready = sem("y_ready")
        s_d_ps = sem("d_ps")
        s_d_ready = sem("d_ready")
        s_yt_ps = sem("yt_ps")
        s_yt_lo = sem("yt_lo")
        s_yt_hi = sem("yt_hi")
        s_kty_ps = sem("kty_ps")
        s_state_ready = sem("state_ready")
        s_ok_ps = sem("ok_ps")
        s_oke_ready = sem("oke_ready")
        s_sub_ready = sem("sub_ready")
        s_exp_ready = sem("exp_ready")
        s_qe_ready = sem("qe_ready")
        s_qet_ps = sem("qet_ps")
        s_qet_ready = sem("qet_ready")
        s_r_ps = sem("r_ps")
        s_r_ready = sem("r_ready")
        s_yv_ps = sem("yv_ps")
        s_vstate_ready = sem("vstate_ready")
        s_ov_ps = sem("ov_ps")
        s_var_ready = sem("var_ready")
        s_rstd_ready = sem("rstd_ready")
        s_og_ready = sem("og_ready")
        s_ot_ps = sem("ot_ps")
        s_ot_ready = sem("ot_ready")
        s_pr_ps = sem("pr_ps")
        s_r1_ready = sem("r1_ready")
        s_nh_ready = sem("nh_ready")
        s_nht_ps = sem("nht_ps")
        s_nxt_ready = sem("nxt_ready")
        s_pqk_ps = sem("pqk_ps")
        s_qkf_ready = sem("qkf_ready")
        s_pv_ps = sem("pv_ps")
        s_vaug_ready = sem("vaug_ready")
        s_parts_ready = sem("parts_ready")
        s_parts_out = sem("parts_out")
        s_q_stack = sem("q_stack")
        s_k_stack = sem("k_stack")
        s_s_ps = sem("s_ps")
        s_s_max = sem("s_max")
        s_mt_in = sem("mt_in")
        s_mt_ps = sem("mt_ps")
        s_mt_ready = sem("mt_ready")
        s_mx_stack = sem("mx_stack")
        s_s2_ps = sem("s2_ps")
        s_p_ready = sem("p_ready")
        s_o2_ps = sem("o2_ps")
        s_o2_ready = sem("o2_ready")
        s_tr_ps = sem("tr_ps")
        s_at_ready = sem("at_ready")
        s_aat_ps = sem("aat_ps")
        s_aat_ready = sem("aat_ready")
        s_pr2_ps = sem("pr2_ps")
        s_x2_ready = sem("x2_ready")
        s_lg_ps = sem("lg_ps")
        s_gd_ready = sem("gd_ready")
        s_gexp_ready = sem("gexp_ready")
        s_gates_ready = sem("gates_ready")
        s_gt_ps = sem("gt_ps")
        s_gt_ready = sem("gt_ready")
        s_b2_ps = sem("b2_ps")
        s_acc_ready = sem("acc_ready")
        s_f1_ps = sem("f1_ps")
        s_h_raw = sem("h_raw")
        s_h_ready = sem("h_ready")
        s_y_ps = sem("y_ps")
        s_y_acc = sem("y_acc")
        s_varm_ready = sem("varm_ready")
        s_rstdm_ready = sem("rstdm_ready")
        s_out_ready = sem("out_ready")
        s_out_stored = sem("out_stored")
        s_dve_own = sem("dve_own")
        s_act_own = sem("act_own")
        s_pool_own = sem("pool_own")
        s_dve_m_own = sem("dve_m_own")
        s_pool_m_own = sem("pool_m_own")

        block = ctx.enter_context(nc.Block())

        CONSTS = [(ident, c_ident), (mid, c_mid), (win, c_win), (wincol, c_wincol), (causal, c_causal),
                  (headmask, c_headmask), (pairmask, c_pairmask), (iota, c_iota), (wqk, w_qk), (wv, w_v),
                  (wfg, w_fg), (wf2, w_f2), (wg2, w_g2), (wo, w_o), (nw, norm_w), (ln1c, ln1), (ln2c, ln2),
                  (w2qk, w2_qk), (w2v, w2_v), (b2qk, b2_qk), (bvB, bv.partition_broadcast(128)), (w2o, w2_o),
                  (boB, bo.partition_broadcast(128)), (gw, gate_w), (fc1s, fc1), (fc1bs, fc1_b), (fc2s, fc2),
                  (fc2bs, fc2_b), (identb, c_identb), (offhead, c_offhead), (negmask, c_negmask),
                  (negmaskT, c_negmaskT), (chunkmask, c_chunkmask)]
        N_CONSTS = len(CONSTS)

        UP = {"qk": (0, 1), "f": (2, 3, 4), "kt": (5, 6), "gp": (7, 8, 9), "d": (10, 11), "yt": (12, 13), "kty": (14, 15)}
        DOWN = {"ok": (0, 1), "qet": (2, 3), "ov": (4,), "ot": (5, 6), "nht": (7, 8), "pqk": (9, 10, 11), "mt": (12, 13),
                "tr": (14,), "nh2": (15,)}
        NU = 2 * NE

        def nth(i, per=1, k=1):
            return i * per + k

        def over_iterations(eng, body):
            body(0, None)
            body(1, 0)
            with eng.Fori(2, B) as i:
                body(i, i - 1)
            body(None, B - 1)

        def first(i):
            return isinstance(i, int) and i == 0

        @block.sync
        def _(sp):
            for dst, src in CONSTS:
                sp.dma_start(dst[:], src).then_inc(s_consts_in, 16)

            def load_x(a):
                sp.dma_start(xT[:], x_T[bass.ds(a, 1)].rearrange("o p n -> (o p) n")).then_inc(s_x_in, 16)
                sp.dma_start(xt[:], x_tok[bass.ds(a, 1)].rearrange("o (t p) d -> (o p) t d", p=128))\
                    .then_inc(s_x_in, 16)

            def body(a, m, more=True):
                if a is not None:
                    sp.wait_ge(s_parts_ready, nth(a))
                    if not first(a):
                        sp.wait_ge(s_q_stack, nth(a - 1, 96, 96))
                        sp.wait_ge(s_k_stack, nth(a - 1, 96, 96))
                    sp.dma_start(scratch.rearrange("j s p n -> p (j s) n"), parts[:].rearrange("p j s n -> p (j s) n")).then_inc(s_parts_out, 16)
                    sp.wait_ge(s_parts_out, nth(a, 16, 16))
                    row = 0
                    for p, n in ((0, 3), (1, 2), (2, 1)):
                        for r in range(n):
                            src = scratch[p, 0].rearrange("(h d) n -> d h n", d=HD)
                            sp.dma_start(Qst[row * HD:(row + 1) * HD, :, :], src).then_inc(s_q_stack, 16)
                            row += 1
                    row = 0
                    for n in (3, 2, 1):
                        for r in range(n):
                            src = scratch[r, 1].rearrange("(h d) n -> d h n", d=HD)
                            sp.dma_start(Kst[(row + r) * HD:(row + r + 1) * HD, :, :], src).then_inc(s_k_stack, 16)
                        row += n
                    sp.wait_ge(s_mt_ready, nth(a))
                    for p in range(3):
                        sp.dma_start(Qst[MAXROW + p:MAXROW + p + 1, :, :], mT[p * NH:(p + 1) * NH, :])\
                            .then_inc(s_mx_stack, 16)
                    if more:
                        load_x(a + 1)
                if m is not None:
                    sp.wait_ge(s_out_ready, nth(m))
                    sp.dma_start(out[bass.ds(m, 1)].rearrange("o (t p) d -> (o p) t d", p=128), xo[:])\
                        .then_inc(s_out_stored, 16)

            load_x(0)
            body(0, None)
            body(1, 0)
            with sp.Fori(2, B - 1) as i:
                body(i, i - 1)
            body(B - 1, B - 2, more=False)
            body(None, B - 1)
            sp.wait_ge(s_out_stored, 16 * B)

        A = [psA[:, k, :] for k in range(5)]

        @block.tensor
        def _(pe):
            def mm(o, l, r, start, stop, onto=False):
                return nc.tensor.matmul(o, l, r, start=start, stop=stop, skip_group_check=onto)

            def up(m, u):
                e, pair = divmod(u, 2)
                if u == 0:
                    pe.wait_ge(s_nxt_ready, nth(m, 2, 2))
                if u >= 3:
                    pe.wait_ge(s_h_raw, nth(m, NU, u - 2))
                elif u == 2:
                    pe.wait_ge(s_acc_ready, nth(m))
                for k in range(2):
                    f = 2 * pair + k
                    last = mm(psM[:, u % 3, k * N:(k + 1) * N], fc1s[:, e, f * 128:(f + 1) * 128], nx2T[:], True, True)
                last.then_inc(s_f1_ps, 1)

            def down(m, u):
                e, t = divmod(u, T)
                if t == 0:
                    pe.wait_ge(s_h_ready, nth(m, NE, e + 1))
                if u >= 3:
                    pe.wait_ge(s_y_acc, nth(m, NU, u - 2))
                else:
                    pe.wait_ge(s_h_raw, nth(m, NU, NU + u - 2))
                o = psM[:, (NU + u) % 3, 0:128]
                for f in range(FC):
                    last = mm(o, hx[:, e, f, t * 128:(t + 1) * 128], fc2s[:, e, f, :], f == 0, f == FC - 1)
                last.then_inc(s_y_ps, 1)

            def fill(m, name):
                if m is not None:
                    for u in UP.get(name, ()):
                        up(m, u)
                    for u in DOWN.get(name, ()):
                        down(m, u)

            def body(a, m):
                att = a is not None
                if m is not None:
                    pe.wait_ge(s_gt_ready, nth(m))
                    if not first(m):
                        pe.wait_ge(s_y_acc, nth(m - 1, NU, NU))
                    for t in range(T):
                        last = mm(psM[:, 2, t * 128:(t + 1) * 128], gT[:, t, :], fc2bs[:], True, True)
                    last.then_inc(s_b2_ps, 1)
                if att:
                    pe.wait_ge(s_x_in, 32 * a + 32)
                    if not first(a):
                        pe.wait_ge(s_gt_ready, nth(a - 1))
                    for j in range(2):
                        last = mm(psA[:, 0, j * N:(j + 1) * N], wqk[:, j, :], xT[:], True, True)
                    last.then_inc(s_qk_ps, 1)
                    mm(psA[:, 1, 0:N], wfg[:], xT[:], True, True)
                    for t in range(T):
                        last = mm(psA[:, 1, N + t * 128:N + (t + 1) * 128], xT[:, t * 128:(t + 1) * 128], wv[:], True, True)
                    last.then_inc(s_fgv_ps, 1)
                fill(m, "qk")
                if att:
                    pe.wait_ge(s_fgv_ready, nth(a))
                    for t in range(T):
                        last = mm(A[2 + t], fgT[:, t * 128:(t + 1) * 128], wf2[:], True, True)
                    last.then_inc(s_f_ps, 1)
                    for t in range(T):
                        last = mm(A[4][:, t * 128:(t + 1) * 128], fgT[:, t * 128:(t + 1) * 128], wg2[:], True, True)
                    last.then_inc(s_g_ps, 1)
                fill(m, "f")
                if att:
                    pe.wait_ge(s_qk2_ready, nth(a))
                    for t in range(T):
                        last = nc.tensor.transpose(A[0][:, t * 128:(t + 1) * 128], qk2[:, 1, t * 128:(t + 1) * 128], ident[:])
                    last.then_inc(s_kt_ps, 1)
                fill(m, "kt")
                if att:
                    pe.wait_ge(s_kt_ready, nth(a))
                    for t in range(T):
                        pe.wait_ge(s_qbd_ready, nth(a, T, t + 1))
                        if t:
                            pe.wait_ge(s_pt_ready, nth(a, T, t))
                        for g in range(2):
                            last = mm(A[g], qk2[:, 1, t * 128:(t + 1) * 128], qbd[:, t, 4 * g:4 * g + 4, :], True, True)
                        last.then_inc(s_pt_ps, 1)
                    pe.wait_ge(s_ls_ready, nth(a))
                    for t in range(T):
                        last = mm(A[2 + t], mid[:], lf[:, t, :], True, True)
                    last.then_inc(s_g_ps, 1)
                    for hp in range(HP):
                        for t in range(T):
                            last = mm(A[4][:, N + 4 * hp:N + 4 * hp + 4], lf[:, t, hp * 128:(hp + 1) * 128],
                                      wincol[:, t, :], t == 0, t == T - 1)
                    last.then_inc(s_dv_ps, 1)
                fill(m, "gp")
                if att:
                    pe.wait_ge(s_ey_ready, nth(a))
                    pe.wait_ge(s_dv_ready, nth(a))
                    for c in range(NC_STATES):
                        mm(A[2 + c], identb[:], offhead[:], True, False)
                        if c == 1:
                            mm(A[2 + c], win[:, 1, :], lf[:, 0, :], False, False)
                            last = mm(A[2 + c], win[:, 2, :], lf[:, 1, :], False, True)
                        else:
                            last = mm(A[2 + c], win[:, c // 2 * 3, :], lf[:, c // 2, :], False, True)
                        last.then_inc(s_d_ps, 1)
                fill(m, "d")
                if att:
                    for t in range(T):
                        pe.wait_ge(s_y_ready, nth(a, T, t + 1))
                        if t == 0:
                            pe.wait_ge(s_pt_ready, nth(a, T, T))
                        for hp in range(HP):
                            last = nc.tensor.transpose(A[t][:, hp * 128:(hp + 1) * 128], Y[:, t, hp * 128:(hp + 1) * 128],
                                                       ident[:])
                        last.then_inc(s_yt_ps, 1)
                fill(m, "yt")
                if att:
                    for c in range(NC_STATES):
                        if c < 2:
                            pe.wait_ge(s_d_ready, nth(a, NC_STATES, c + 1))
                        else:
                            pe.wait_ge(s_state_ready, nth(a, NC_STATES, 1))
                        last = mm(A[2 + c % 2], ktm[:, c // 2, c % 2, :], Y[:, c // 2, :], True, True)
                        last.then_inc(s_kty_ps, 1)
                    pe.wait_ge(s_d_ready, nth(a, NC_STATES, NC_STATES))
                    pe.wait_ge(s_vtm_ready, nth(a))
                    for c in range(NC_STATES):
                        for hp in range(HP):
                            last = mm(A[4][:, c * 128 + hp * 32:c * 128 + (hp + 1) * 32],
                                      Y[:, c // 2, hp * 128:(hp + 1) * 128],
                                      vtm[:, c // 2, c % 2, hp * 32:(hp + 1) * 32], True, True)
                    last.then_inc(s_yv_ps, 1)
                fill(m, "kty")
                if att:
                    pe.wait_ge(s_yt_lo, nth(a, T, T))
                    pe.wait_ge(s_yt_hi, nth(a, T, T))
                    for t in range(T):
                        for h in range(H):
                            mm(A[t][:, h * M:(h + 1) * M], PTm[:, t, h, :], Y[:, t, h * M:(h + 1) * M], h == 0, h == H - 1)
                        for c in range(max(2 * t, 1), 2 * t + 2):
                            pe.wait_ge(s_state_ready, nth(a, NC_STATES, c))
                            last = mm(A[t][c % 2 * C:(c % 2 + 1) * C, :], qk2[:, 0, c * C:(c + 1) * C],
                                      state[:, c - 1, :], False, True, onto=True)
                        last.then_inc(s_ok_ps, 1)
                fill(m, "ok")
                if att:
                    for t in range(T):
                        pe.wait_ge(s_qe_ready, nth(a, T, t + 1))
                        for hp in range(HP):
                            last = nc.tensor.transpose(A[2 + t][:, hp * 128:(hp + 1) * 128],
                                                       thf[:, t, hp * 128:(hp + 1) * 128], ident[:])
                        last.then_inc(s_qet_ps, 1)
                fill(m, "qet")
                if att:
                    pe.wait_ge(s_vstate_ready, nth(a, NC_STATES, NC_STATES))
                    for t in range(T):
                        pe.wait_ge(s_qet_ready, nth(a, T, t + 1))
                        if t == 0:
                            pe.wait_ge(s_oke_ready, nth(a, T, T))
                        else:
                            pe.wait_ge(s_r_ready, nth(a, T, t))
                        for h in range(H):
                            last = mm(A[h // 4][:, h % 4 * 128:(h % 4 + 1) * 128], YTbd[:, t, h // 2, h % 2, :],
                                      QET[:, t, h // 2, :], True, True)
                        last.then_inc(s_r_ps, 1)
                        o = A[4][:, t * 128:(t + 1) * 128]
                        pe.wait_ge(s_r_ready, nth(a, T, t + 1))
                        for h in range(H):
                            last = mm(o[:, h * DK:(h + 1) * DK], PTm[:, t, h, :], vtok[:, t, h * DK:(h + 1) * DK], h == 0, h == H - 1)
                        for c in range(max(2 * t, 1), 2 * t + 2):
                            for hp in range(HP):
                                last = mm(o[c % 2 * C:(c % 2 + 1) * C, hp * 32:(hp + 1) * 32],
                                          QET[:, t, hp, c % 2 * C:(c % 2 + 1) * C], vstate[:, c - 1, hp, :],
                                          False, True, onto=True)
                        last.then_inc(s_ov_ps, 1)
                        if t == 0:
                            fill(m, "ov")
                else:
                    fill(m, "ov")
                if att:
                    pe.wait_ge(s_og_ready, nth(a))
                    for t in range(T):
                        last = nc.tensor.transpose(A[2][:, t * 128:(t + 1) * 128], og[:, t, :], ident[:])
                    last.then_inc(s_ot_ps, 1)
                fill(m, "ot")
                if att:
                    pe.wait_ge(s_ot_ready, nth(a))
                    for t in range(T):
                        last = mm(A[3][:, t * 128:(t + 1) * 128], oT[:, t, :], wo[:], True, True)
                    last.then_inc(s_pr_ps, 1)
                    pe.wait_ge(s_nh_ready, nth(a, 2, 1))
                    for t in range(T):
                        last = nc.tensor.transpose(A[0][:, t * 128:(t + 1) * 128], nh[:, t, :], ident[:])
                    last.then_inc(s_nht_ps, 1)
                fill(m, "nht")
                if att:
                    pe.wait_ge(s_nxt_ready, nth(a, 2, 1))
                    for j in range(2):
                        last = mm(A[1][:, j * N:(j + 1) * N], w2qk[:, j, :], nxT[:], True, True)
                    last.then_inc(s_pqk_ps, 1)
                    for t in range(T):
                        last = mm(A[2][:, t * 128:(t + 1) * 128], nxT[:, t * 128:(t + 1) * 128], w2v[:], True, True)
                    last.then_inc(s_pv_ps, 1)
                fill(m, "pqk")
                if att:
                    pe.wait_ge(s_q_stack, nth(a, 96, 96))
                    pe.wait_ge(s_k_stack, nth(a, 96, 96))
                    pe.wait_ge(s_vaug_ready, nth(a))
                    for u in range(12):
                        if u >= 5:
                            pe.wait_ge(s_s_max, nth(a, 12, u - 4))
                        bank = A[(3 + u) % 5]
                        if u < 4:
                            mm(bank, identb[:], negmask[:, 0, :], True, False)
                            for j in range(4):
                                last = mm(bank[:, j * 128:(j + 1) * 128], Qst[0:KS, 4 * u + j, 0:128],
                                          Kst[0:KS, 4 * u + j, 0:128], False, j == 3)
                        else:
                            mm(bank, identb[:], negmask[:, 1, :], True, False)
                            for j in range(2):
                                last = mm(bank[:, j * N:(j + 1) * N], Qst[0:KS, 2 * (u - 4) + j, 128:N],
                                          Kst[0:KS, 2 * (u - 4) + j, :], False, j == 1)
                        last.then_inc(s_s_ps, 1)
                    pe.wait_ge(s_mt_in, nth(a))
                    for t in range(T):
                        last = nc.tensor.transpose(A[3][:, t * 128:(t + 1) * 128], mparts[:, t, :], ident[:])
                    last.then_inc(s_mt_ps, 1)
                fill(m, "mt")
                if att:
                    pe.wait_ge(s_mx_stack, nth(a, 48, 48))
                    pe.wait_ge(s_mt_ready, nth(a))

                    def scores(g):
                        for w in range(3):
                            u = 3 * g + w
                            if u >= 3:
                                pe.wait_ge(s_p_ready, nth(a, 12, u - 2))
                            bank = A[w]
                            mm(bank, identb[:], negmaskT[:, w // 2, :], True, False)
                            for j in range(2 if w < 2 else 4):
                                h = 4 * g + (2 * w + j if w < 2 else j)
                                n = N if w < 2 else 128
                                last = mm(bank[:, j * n:(j + 1) * n], Kst[:, h, w // 2 * 128:w // 2 * 128 + 128],
                                          Qst[:, h, N - n:N], False, j == (1 if w < 2 else 3))
                            last.then_inc(s_s2_ps, 1)

                    def values(g):
                        pe.wait_ge(s_p_ready, nth(a, 12, 3 * g + 3))
                        for j in range(4):
                            o = A[3 + g // 2][32 * j:32 * j + 32, g % 2 * N:(g % 2 + 1) * N]
                            mm(o, vaug[:, 0, 4 * g + j, :], pT[:, g % 2, j // 2, j % 2 * N:(j % 2 + 1) * N], True, False)
                            last = mm(o[:, 128:N], vaug[:, 1, 4 * g + j, :], pT[:, g % 2, 2, j * 128:(j + 1) * 128],
                                      False, True)
                        last.then_inc(s_o2_ps, 1)

                    scores(0)
                    for g in range(G4):
                        if g + 1 < G4:
                            scores(g + 1)
                        values(g)
                    for t in range(T):
                        for g in range(G4):
                            pe.wait_ge(s_o2_ready, nth(a, 2, g // 2 + 1))
                            last = nc.tensor.transpose(A[t][:, g * 128:(g + 1) * 128], oT2[:, g, t * 128:(t + 1) * 128],
                                                       ident[:])
                        last.then_inc(s_tr_ps, 1)
                fill(m, "tr")
                if att:
                    pe.wait_ge(s_at_ready, nth(a))
                    for t in range(T):
                        last = nc.tensor.transpose(A[2][:, t * 128:(t + 1) * 128], at[:, t, :], ident[:])
                    last.then_inc(s_aat_ps, 1)
                    pe.wait_ge(s_aat_ready, nth(a))
                    for t in range(T):
                        last = mm(A[3][:, t * 128:(t + 1) * 128], aT[:, t, :], w2o[:], True, True)
                    last.then_inc(s_pr2_ps, 1)
                fill(m, "nh2")
                if att:
                    pe.wait_ge(s_nh_ready, nth(a, 2, 2))
                    for t in range(T):
                        last = nc.tensor.transpose(A[0][:, t * 128:(t + 1) * 128], nh[:, t, :], ident[:])
                    last.then_inc(s_nht_ps, 1)
                    pe.wait_ge(s_nxt_ready, nth(a, 2, 2))
                    for t in range(T):
                        last = mm(A[4][:, t * NE:(t + 1) * NE], nx2T[:, t * 128:(t + 1) * 128], gw[:], True, True)
                    last.then_inc(s_lg_ps, 1)
                    pe.wait_ge(s_gates_ready, nth(a))
                    for t in range(T):
                        last = nc.tensor.transpose(A[1][:, t * 128:(t + 1) * 128], gates[:, t, :], ident[:])
                    last.then_inc(s_gt_ps, 1)

            pe.wait_ge(s_consts_in, N_CONSTS * 16)
            pe.wait_ge(s_zeroed, N_ZEROED)
            pe.wait_ge(s_wo_scaled, 1)
            over_iterations(pe, body)

        @block.vector
        def _(dve):
            V = nc.vector

            def body(a, m):
                att = a is not None
                step = {"a": 0, "m": 0}

                def own(ins):
                    step["a"] += 1
                    ins.then_inc(s_dve_own, 1)
                    dve.wait_ge(s_dve_own, nth(a, DVE_OWN, step["a"]))

                def own_m(ins):
                    step["m"] += 1
                    ins.then_inc(s_dve_m_own, 1)
                    dve.wait_ge(s_dve_m_own, nth(m, DVE_M_OWN, step["m"]))

                def raw(u):
                    e, pair = divmod(u, 2)
                    dve.wait_ge(s_f1_ps, nth(m, NU, u + 1))
                    if u == 0 and not first(m):
                        dve.wait_ge(s_y_ps, nth(m - 1, NU, NU))
                    for k in range(2):
                        f = 2 * pair + k
                        last = V.tensor_scalar(hx[:, e, f, :], psM[:, u % 3, k * N:(k + 1) * N],
                                               fc1bs[:, e * FC + f:e * FC + f + 1], None, ALU.add)
                    last.then_inc(s_h_raw, 1)

                def add_y(u):
                    e, t = divmod(u, T)
                    dve.wait_ge(s_y_ps, nth(m, NU, u + 1))
                    if u >= T:
                        dve.wait_ge(s_y_acc, nth(m, NU, u - T + 1))
                    o = psM[:, (NU + u) % 3, 0:128]
                    V.scalar_tensor_tensor(acc[:, t, :], o, gatesm[:, t, e:e + 1], acc[:, t, :], ALU.mult, ALU.add)\
                        .then_inc(s_y_acc, 1)

                def fill(name):
                    if m is not None:
                        for u in UP.get(name, ()):
                            raw(u)
                        for u in DOWN.get(name, ()):
                            add_y(u)

                def norm(x, o, k):
                    for t in range(T):
                        last = V.bn_stats(bn[:, t, :], x[:, t, :])
                    own(last)
                    V.tensor_copy(nop[:], neghalf[:, 0:1])
                    for t in range(T):
                        last = V.bn_aggr(mv[:, t, :], bn[:, t, :])
                    last.then_inc(s_var_ready, 1)
                    dve.wait_ge(s_rstd_ready, nth(a, 4, k))
                    for t in range(T):
                        last = V.tensor_scalar(o[:, t, :], x[:, t, :], mv[:, t, 0:1], rstd[:, t:t + 1], ALU.subtract, ALU.mult)
                    return last

                if m is not None:
                    dve.wait_ge(s_b2_ps, nth(m))
                    if not first(m):
                        dve.wait_ge(s_out_ready, nth(m - 1))
                    V.tensor_copy(gatesm[:], gates[:, :, 0:NE])
                    own_m(V.tensor_tensor(acc[:], x2[:], psM[:, 2, 0:N].rearrange("p (t d) -> p t d", t=T), ALU.add))
                    V.tensor_tensor(acc[:], acc[:], x1[:], ALU.add).then_inc(s_acc_ready, 1)
                    dve.wait_ge(s_acc_ready, nth(m))
                if att:
                    dve.wait_ge(s_fgv_ps, nth(a))
                    V.tensor_copy(fgT[:], A[1][:, 0:N])
                    V.tensor_copy(vtok[:], A[1][:, N:2 * N].rearrange("p (t d) -> p t d", t=T)).then_inc(s_fgv_ready, 1)
                    dve.wait_ge(s_th_qk, nth(a))
                    V.scalar_tensor_tensor(qk2[:], thqk[:], 1.0, A[0].rearrange("p (j n) -> p j n", j=2), ALU.add, ALU.mult)\
                        .then_inc(s_qk2_ready, 1)
                fill("qk")
                fill("f")
                if att:
                    dve.wait_ge(s_kt_ps, nth(a))
                    for t in range(T):
                        for c in range(2):
                            last = V.tensor_copy(ktm[c * C:(c + 1) * C, t, c, :], A[0][c * C:(c + 1) * C, t * 128:(t + 1) * 128])
                    last.then_inc(s_kt_ready, 1)
                if att:
                    dve.wait_ge(s_lnu_ready, nth(a))
                    V.scalar_tensor_tensor(lf[:], psA[:, 2:4, :], 0.0, lf[:], ALU.min, ALU.subtract).then_inc(s_ls_ready, 1)
                fill("kt")
                if att:
                    for t in range(T):
                        dve.wait_ge(s_pt_ps, nth(a, T, t + 1))
                        V.tensor_tensor(PTm[:, t], psA[:, 0:2, :].rearrange("p b (h n) -> p (b h) n", h=4),
                                        causal[:].unsqueeze(1).broadcast_to([128, H, 128]), ALU.mult).then_inc(s_pt_ready, 1)
                fill("gp")
                if att:
                    dve.wait_ge(s_ey_ready, nth(a))
                    for t in range(T):
                        V.scalar_tensor_tensor(Y[:, t, :], thf[:, t, :], 1.0, EY[:, t, :], ALU.subtract, ALU.mult)\
                            .then_inc(s_y_ready, 1)
                fill("d")
                if att:
                    for t in range(T):
                        dve.wait_ge(s_yt_ps, nth(a, T, t + 1))
                        V.tensor_copy(YTbd[64:128, t, :, 1, :], A[t][64:128, :].rearrange("p (h n) -> p h n", h=HP))\
                            .then_inc(s_yt_hi, 1)
                fill("yt")
                if att:
                    for c in range(NC_STATES):
                        dve.wait_ge(s_kty_ps, nth(a, NC_STATES, c + 1))
                        if c == 0:
                            dve.wait_ge(s_d_ready, nth(a, NC_STATES, NC_STATES))
                            V.tensor_tensor(state[:, 0, :], A[2], dm[:, 0, :], ALU.mult).then_inc(s_state_ready, 1)
                        else:
                            dve.wait_ge(s_state_ready, nth(a, NC_STATES, c))
                            own(V.tensor_tensor(stmp, A[2 + c % 2], state[:, c - 1, :], ALU.add))
                            V.tensor_tensor(state[:, c, :], stmp, dm[:, c, :], ALU.mult).then_inc(s_state_ready, 1)
                    dve.wait_ge(s_yv_ps, nth(a))
                    dve.wait_ge(s_dvm_ready, nth(a))
                    for c in range(NC_STATES):
                        yv = A[4][:, c * 128:(c + 1) * 128].rearrange("p (h v) -> p h v", h=HP)
                        if c == 0:
                            V.tensor_tensor(vstate[:, 0], yv, dvm[:, 0], ALU.mult).then_inc(s_vstate_ready, 1)
                        else:
                            dve.wait_ge(s_vstate_ready, nth(a, NC_STATES, c))
                            own(V.tensor_tensor(vtmp[:], yv, vstate[:, c - 1], ALU.add))
                            V.tensor_tensor(vstate[:, c], vtmp[:], dvm[:, c], ALU.mult).then_inc(s_vstate_ready, 1)
                fill("kty")
                if att:
                    for t in range(T):
                        dve.wait_ge(s_ok_ps, nth(a, T, t + 1))
                        V.scalar_tensor_tensor(okE[:, t, :], A[t], -0.125, E[:, t, :], ALU.mult, ALU.mult)\
                            .then_inc(s_oke_ready, 1)
                        dve.wait_ge(s_oke_ready, nth(a, T, t + 1))
                        okh = okE[:, t, :].rearrange("p (h m) -> p h m", h=H)
                        own(V.tensor_reduce(mx[:, t, :], okh, AX_X, ALU.max))
                        V.tensor_tensor(okh, okh, mx[:, t, :].unsqueeze(2).broadcast_to([128, H, M]), ALU.subtract)\
                            .then_inc(s_sub_ready, 1)
                    for t in range(T):
                        dve.wait_ge(s_exp_ready, nth(a, T, t + 1))
                        own(V.tensor_reduce(sm[:, t, :], okE[:, t, :].rearrange("p (h m) -> p h m", h=H), AX_X, ALU.add))
                    own(V.reciprocal(rs[:], sm[:]))
                fill("ok")
                fill("qet")
                if att:
                    for t in range(T):
                        dve.wait_ge(s_r_ps, nth(a, T, t + 1))
                        V.scalar_tensor_tensor(PTm[:, t], psA[:, 0:2, :].rearrange("p b (h n) -> p (b h) n", h=4), FMAX,
                                               causal[:].unsqueeze(1).broadcast_to([128, H, 128]), ALU.min, ALU.mult)\
                            .then_inc(s_r_ready, 1)
                        if t == 0:
                            fill("ov")
                elif m is not None:
                    fill("ov")
                if att:
                    dve.wait_ge(s_ov_ps, nth(a, T, T))
                    ov = A[4][:, 0:N].rearrange("p (t d) -> p t d", t=T)
                    dve.wait_ge(s_th_g, nth(a))
                    own(V.scalar_tensor_tensor(og[:], thg[:], 1.0, ov, ALU.add, ALU.mult))
                    ogh = og[:].rearrange("p t (h v) -> p (t h) v", h=H)
                    own(V.scalar_tensor_tensor(ogh, ogh, -0.25, rs[:].rearrange("p t h -> p (t h)").unsqueeze(2)
                                               .broadcast_to([128, T * H, DK]), ALU.mult, ALU.mult))
                    own(V.tensor_tensor(sq[:], og[:], og[:], ALU.mult))
                    V.tensor_reduce(ms[:].rearrange("p t h -> p (t h)"), sq[:].rearrange("p t (h v) -> p (t h) v", h=H),
                                    AX_X, ALU.add).then_inc(s_var_ready, 1)
                    dve.wait_ge(s_rstd_ready, nth(a, 4, 1))
                    V.tensor_tensor(ogh, ogh, rstd[:].unsqueeze(2).broadcast_to([128, T * H, DK]), ALU.mult)\
                        .then_inc(s_og_ready, 1)
                fill("ot")
                if att:
                    dve.wait_ge(s_pr_ps, nth(a))
                    V.tensor_tensor(r1[:], A[3][:, 0:N].rearrange("p (t d) -> p t d", t=T), xt[:], ALU.add)\
                        .then_inc(s_r1_ready, 1)
                    dve.wait_ge(s_r1_ready, nth(a))
                    own(norm(r1, x1, 2))
                    norm(x1, nh, 3).then_inc(s_nh_ready, 1)
                fill("nht")
                if att:
                    dve.wait_ge(s_pqk_ps, nth(a))
                    V.tensor_scalar(qkf[:, 0, :], A[1][:, 0:N], b2qk[:, 0:1], HD ** -0.5, ALU.add, ALU.mult)
                    V.tensor_scalar(qkf[:, 1, :], A[1][:, N:2 * N], b2qk[:, 1:2], None, ALU.add).then_inc(s_qkf_ready, 1)
                    dve.wait_ge(s_qkf_ready, nth(a))
                    if not first(a):
                        dve.wait_ge(s_parts_out, 16 * a)
                    own(V.tensor_copy(parts[:, 0], qkf[:]))
                    own(V.tensor_tensor(resid[:], qkf[:], parts[:, 0], ALU.subtract))
                    own(V.tensor_copy(parts[:, 1], resid[:]))
                    own(V.tensor_tensor(resid[:], resid[:], parts[:, 1], ALU.subtract))
                    V.tensor_copy(parts[:, 2], resid[:]).then_inc(s_parts_ready, 1)
                    dve.wait_ge(s_pv_ps, nth(a))
                    V.tensor_tensor(vaug[:, :, :, 0:HD], A[2][:, 0:N].rearrange("p (t h v) -> p t h v", t=T, h=NH),
                                    bvB[:].rearrange("p (h v) -> p h v", h=NH).unsqueeze(1).broadcast_to([128, T, NH, HD]),
                                    ALU.add).then_inc(s_vaug_ready, 1)
                fill("pqk")
                if att:
                    for u in range(12):
                        dve.wait_ge(s_s_ps, nth(a, 12, u + 1))
                        bank = A[(3 + u) % 5]
                        if u < 4:
                            o, n = nmax[:, 0, 4 * u:4 * u + 4], 4
                        else:
                            o, n = nmax[:, 1, 2 * (u - 4):2 * (u - 4) + 2], 2
                        V.tensor_reduce(o, bank.rearrange("p (h n) -> p h n", h=n), AX_X, ALU.max).then_inc(s_s_max, 1)
                    dve.wait_ge(s_s_max, nth(a, 12, 12))
                    own(V.tensor_scalar(mres[:], nmax[:], -1.0, None, ALU.mult))
                    for j in range(3):
                        own(V.tensor_copy(mpb[:], mres[:]))
                        last = V.tensor_copy(mparts[:, :, j * NH:(j + 1) * NH], mpb[:])
                        if j < 2:
                            own(V.tensor_tensor(mres[:], mres[:], mpb[:], ALU.subtract))
                    last.then_inc(s_mt_in, 1)
                fill("mt")
                if att:
                    for t in range(T):
                        dve.wait_ge(s_tr_ps, nth(a, T, t + 1))
                        o4 = A[t].rearrange("p (h w) -> p h w", h=NH)
                        own(V.reciprocal(rec[:, t, :].unsqueeze(2), o4[:, :, HD:HD + 1]))
                        last = V.tensor_tensor(at[:, t, :].rearrange("p (h v) -> p h v", h=NH), o4[:, :, 0:HD],
                                               rec[:, t, :].unsqueeze(2).broadcast_to([128, NH, HD]), ALU.mult)
                    last.then_inc(s_at_ready, 1)
                fill("tr")
                if att:
                    dve.wait_ge(s_pr2_ps, nth(a))
                    own(V.tensor_tensor(x2[:], A[3][:, 0:N].rearrange("p (t d) -> p t d", t=T),
                                        boB[:].unsqueeze(1).broadcast_to([128, T, 128]), ALU.add))
                    V.tensor_tensor(x2[:], x2[:], x1[:], ALU.add).then_inc(s_x2_ready, 1)
                    dve.wait_ge(s_x2_ready, nth(a))
                    norm(x2, nh, 4).then_inc(s_nh_ready, 1)
                fill("nh2")
                if att:
                    dve.wait_ge(s_lg_ps, nth(a))
                    own(V.tensor_copy(lg[:], A[4][:, 0:T * NE].rearrange("p (t e) -> p t e", t=T)))
                    V.tensor_copy(nop[:], neghalf[:, 0:1])
                    for t in range(T):
                        last = V.max(top[:, t, :], lg[:, t, :])
                    own(last)
                    V.tensor_copy(nop[:], neghalf[:, 0:1])
                    for t in range(T):
                        V.max_index(topi[:, t, :], top[:, t, :], lg[:, t, :])
                    own(V.tensor_tensor(gd[:, :, 0:1], top[:, :, 1:2], top[:, :, 0:1], ALU.subtract))
                    V.tensor_copy(topf[:], topi[:]).then_inc(s_gd_ready, 1)
                    dve.wait_ge(s_gexp_ready, nth(a))
                    own(V.tensor_scalar(gd[:, :, 2:3], gd[:, :, 1:2], 1.0, None, ALU.add))
                    own(V.reciprocal(gd[:, :, 0:1], gd[:, :, 2:3]))
                    own(V.tensor_tensor(gd[:, :, 3:4], gd[:, :, 0:1], gd[:, :, 1:2], ALU.mult))
                    for t in range(T):
                        own(V.tensor_scalar(gates[:, t, 0:NE], iota[:], topf[:, t, 0:1], gd[:, t, 0:1], ALU.is_equal, ALU.mult))
                        own(V.tensor_scalar(oh[:], iota[:], topf[:, t, 1:2], gd[:, t, 3:4], ALU.is_equal, ALU.mult))
                        last = V.tensor_tensor(gates[:, t, 0:NE], gates[:, t, 0:NE], oh[:], ALU.add)
                    last.then_inc(s_gates_ready, 1)
                    dve.wait_ge(s_gt_ps, nth(a))
                    V.tensor_copy(gT[:], A[1][:, 0:N].rearrange("p (t n) -> p t n", t=T)).then_inc(s_gt_ready, 1)
                if m is not None:
                    dve.wait_ge(s_y_acc, nth(m, NU, NU))
                    if not first(m):
                        dve.wait_ge(s_out_stored, 16 * m)
                    for t in range(T):
                        last = V.bn_stats(bnm[:, t, :], acc[:, t, :])
                    own_m(last)
                    V.tensor_copy(nop[:], neghalf[:, 0:1])
                    for t in range(T):
                        last = V.bn_aggr(mvm[:, t, :], bnm[:, t, :])
                    last.then_inc(s_varm_ready, 1)
                    dve.wait_ge(s_rstdm_ready, nth(m))
                    for t in range(T):
                        last = V.tensor_scalar(xo[:, t, :], acc[:, t, :], mvm[:, t, 0:1], rstdm[:, t:t + 1],
                                               ALU.subtract, ALU.mult)
                    last.then_inc(s_out_ready, 1)
                assert not att or step["a"] == DVE_OWN, step
                assert m is None or step["m"] == DVE_M_OWN, step

            dve.wait_ge(s_consts_in, N_CONSTS * 16)
            dve.wait_ge(s_zeroed, N_ZEROED)
            V.tensor_scalar(wo[:], wo[:], nw[:, 0:1], DK ** 0.5, ALU.mult, ALU.mult).then_inc(s_wo_scaled, 1)
            over_iterations(dve, body)

        @block.scalar
        def _(act):
            X = nc.scalar

            def body(a, m):
                att = a is not None
                if att:
                    act.wait_ge(s_qk_ps, nth(a))
                    X.activation(thqk[:].rearrange("p j n -> p (j n)"), A[0], ACT.Tanh, scale=0.5).then_inc(s_th_qk, 1)
                    act.wait_ge(s_f_ps, nth(a))
                    X.activation(thf[:], psA[:, 2:4, :], ACT.Tanh, scale=0.5)
                    act.wait_ge(s_g_ps, nth(a, 2, 1))
                    X.activation(thg[:].rearrange("p t n -> p (t n)"), A[4][:, 0:N], ACT.Tanh, scale=0.5).then_inc(s_th_g, 1)
                    X.activation(lf[:], psA[:, 2:4, :], ACT.Abs).then_inc(s_act_own, 1)
                    act.wait_ge(s_act_own, nth(a, 2, 1))
                    X.activation(lf[:], lf[:], ACT.Exp, scale=-1.0).then_inc(s_act_own, 1)
                    act.wait_ge(s_act_own, nth(a, 2, 2))
                    X.activation(lf[:], lf[:], ACT.Ln, bias=1.0).then_inc(s_lnu_ready, 1)
                    act.wait_ge(s_g_ps, nth(a, 2, 2))
                    X.activation(EY[:], psA[:, 2:4, :], ACT.Exp, scale=-1.0)
                    X.activation(E[:], psA[:, 2:4, :], ACT.Exp).then_inc(s_ey_ready, 1)
                    act.wait_ge(s_dv_ps, nth(a))
                    X.activation(dv[:].rearrange("p h c -> p (h c)"), A[4][:, N:N + 4 * HP], ACT.Exp).then_inc(s_dv_ready, 1)
                    for c in range(NC_STATES):
                        act.wait_ge(s_d_ps, nth(a, NC_STATES, c + 1))
                        X.activation(dm[:, c, :], A[2 + c], ACT.Exp).then_inc(s_d_ready, 1)
                    for t in range(T):
                        act.wait_ge(s_yt_ps, nth(a, T, t + 1))
                        X.activation(YTbd[0:64, t, :, 0, :], A[t][0:64, :].rearrange("p (h n) -> p h n", h=HP), ACT.Copy)\
                            .then_inc(s_yt_lo, 1)
                if m is not None:
                    for e in range(NE):
                        act.wait_ge(s_h_raw, nth(m, NU, 2 * e + 2))
                        X.activation(hx[:, e].rearrange("p f n -> p (f n)"), hx[:, e].rearrange("p f n -> p (f n)"), ACT.Gelu)\
                            .then_inc(s_h_ready, 1)
                if att:
                    for t in range(T):
                        act.wait_ge(s_sub_ready, nth(a, T, t + 1))
                        X.activation(okE[:, t, :], okE[:, t, :], ACT.Exp).then_inc(s_exp_ready, 1)
                    for t in range(T):
                        act.wait_ge(s_qet_ps, nth(a, T, t + 1))
                        X.activation(QET[:, t].rearrange("p h n -> p (h n)"), A[2 + t], ACT.Copy).then_inc(s_qet_ready, 1)
                    act.wait_ge(s_ot_ps, nth(a))
                    X.activation(oT[:].rearrange("p t n -> p (t n)"), A[2][:, 0:N], ACT.Copy).then_inc(s_ot_ready, 1)
                    act.wait_ge(s_nht_ps, nth(a, 2, 1))
                    X.activation(nxT[:], A[0][:, 0:N], ACT.Identity, bias=ln1c[:, 1:2], scale=ln1c[:, 0:1])\
                        .then_inc(s_nxt_ready, 1)
                    act.wait_ge(s_mt_ps, nth(a))
                    if not first(a):
                        act.wait_ge(s_mx_stack, nth(a - 1, 48, 48))
                    X.activation(mT[:], A[3][0:3 * NH, 0:N], ACT.Copy).then_inc(s_mt_ready, 1)
                    for u in range(12):
                        act.wait_ge(s_s2_ps, nth(a, 12, u + 1))
                        g, w = divmod(u, 3)
                        if g >= 2 and w == 0:
                            act.wait_ge(s_o2_ps, nth(a, G4, g - 1))
                        X.activation(pT[:, g % 2, w, :], A[w], ACT.Exp).then_inc(s_p_ready, 1)
                    for k in range(2):
                        act.wait_ge(s_o2_ps, nth(a, G4, 2 * k + 2))
                        X.activation(oT2[:, 2 * k:2 * k + 2, :].rearrange("p g n -> p (g n)"), A[3 + k], ACT.Copy)\
                            .then_inc(s_o2_ready, 1)
                    act.wait_ge(s_aat_ps, nth(a))
                    X.activation(aT[:].rearrange("p t n -> p (t n)"), A[2][:, 0:N], ACT.Copy).then_inc(s_aat_ready, 1)
                    act.wait_ge(s_nht_ps, nth(a, 2, 2))
                    X.activation(nx2T[:], A[0][:, 0:N], ACT.Identity, bias=ln2c[:, 1:2], scale=ln2c[:, 0:1])\
                        .then_inc(s_nxt_ready, 1)
                    act.wait_ge(s_gd_ready, nth(a))
                    X.activation(gd[:, :, 1:2], gd[:, :, 0:1], ACT.Exp).then_inc(s_gexp_ready, 1)

            act.wait_ge(s_consts_in, N_CONSTS * 16)
            act.wait_ge(s_zeroed, N_ZEROED)
            over_iterations(act, body)

        @block.gpsimd
        def _(pool):
            P = nc.gpsimd
            fills = [(ktm[:], 0.0), (vtm[:], 0.0), (YTbd[:], 0.0), (gates[:], 0.0), (Qst[:], 0.0), (Kst[:], 0.0),
                     (vaug[:], 0.0), (Kst[MAXROW:MAXROW + 3], 1.0), (vaug[:, :, :, HD:HD + 1], 1.0), (neghalf[:], -0.5),
                     (eps[:], EPS), (epsdk[:], EPS * DK), (mparts[:], 0.0)]
            for n, (z, value) in enumerate(fills):
                pool.memset(z, value).then_inc(s_zeroed, 1)
                pool.wait_ge(s_zeroed, n + 1)
            pool.wait_ge(s_consts_in, N_CONSTS * 16)

            def body(a, m):
                if a is not None:
                    pool.wait_ge(s_fgv_ready, nth(a))
                    for t in range(T):
                        for c in range(2):
                            last = P.tensor_tensor(vtm[:, t, c, :], vtok[:, t, :], chunkmask[:, c:c + 1].broadcast_to([128, 128]), ALU.mult)
                    last.then_inc(s_vtm_ready, 1)
                    pool.wait_ge(s_qk2_ready, nth(a))
                    for t in range(T):
                        P.tensor_tensor(qbd[:, t], qk2[:, 0, t * 128:(t + 1) * 128].unsqueeze(1).broadcast_to([128, H, 128]),
                                        headmask[:].unsqueeze(2).broadcast_to([128, H, 128]), ALU.mult)\
                            .then_inc(s_qbd_ready, 1)
                    pool.wait_ge(s_dv_ready, nth(a))
                    for c in range(NC_STATES):
                        last = P.tensor_tensor(dvm[:, c], pairmask[:].unsqueeze(1).broadcast_to([128, HP, 32]),
                                               dv[:, :, c:c + 1].broadcast_to([128, HP, 32]), ALU.mult)
                    last.then_inc(s_dvm_ready, 1)
                    for t in range(T):
                        pool.wait_ge(s_exp_ready, nth(a, T, t + 1))
                        P.tensor_tensor(thf[:, t, :], okE[:, t, :], E[:, t, :], ALU.mult).then_inc(s_qe_ready, 1)
                    pool.wait_ge(s_var_ready, nth(a, 4, 1))
                    P.tensor_tensor(rstd[:], ms[:].rearrange("p t h -> p (t h)"), epsdk[:], ALU.add).then_inc(s_pool_own, 1)
                    pool.wait_ge(s_pool_own, nth(a, 4, 1))
                    P.tensor_tensor(rstd[:], rstd[:], neghalf[:], ALU.pow).then_inc(s_rstd_ready, 1)
                    for k in (2, 3, 4):
                        pool.wait_ge(s_var_ready, nth(a, 4, k))
                        P.tensor_tensor(rstd[:, 0:T], mv[:, :, 1], eps[:, 0:T], ALU.add).then_inc(s_pool_own, 1)
                        pool.wait_ge(s_pool_own, nth(a, 4, k))
                        P.tensor_tensor(rstd[:, 0:T], rstd[:, 0:T], neghalf[:, 0:T], ALU.pow).then_inc(s_rstd_ready, 1)
                if m is not None:
                    pool.wait_ge(s_varm_ready, nth(m))
                    P.tensor_tensor(rstdm[:], mvm[:, :, 1], eps[:, 0:T], ALU.add).then_inc(s_pool_m_own, 1)
                    pool.wait_ge(s_pool_m_own, nth(m))
                    P.tensor_tensor(rstdm[:], rstdm[:], neghalf[:, 0:T], ALU.pow).then_inc(s_rstdm_ready, 1)

            over_iterations(pool, body)


N_ZEROED = 13
DVE_OWN = 39
DVE_M_OWN = 2


_OUTS = [((B, N, D), "float32")]


def _constants():
    s = np.arange(128)[:, None]
    t = np.arange(128)[None, :]
    c = {}
    f = np.float32
    c["c_ident"] = (s == t).astype(f)
    middle = t // C * C + C // 2 - 1
    same = s // C == t // C
    c["c_mid"] = (same * ((s > middle) & (s <= t)).astype(f) - same * ((s <= middle) & (s > t)).astype(f)).astype(f)
    inner = ((s >= C // 2) & (s < 128 - C // 2)).astype(f)
    late = (s >= 128 - C // 2).astype(f)
    early = (s < C // 2).astype(f)
    c["c_win"] = np.stack([np.repeat(x, 128, 1) for x in (inner, late, early, inner)], 1)
    zero = np.zeros((128, 1), f)
    c["c_wincol"] = np.stack([np.concatenate([inner, late, zero, zero], 1), np.concatenate([zero, early, inner, zero], 1)], 1)
    c["c_causal"] = (same & (s <= t)).astype(f)
    h = np.arange(H)[None, :]
    c["c_headmask"] = (s // DK == h).astype(f)
    c["c_offhead"] = np.where(s // DK == np.arange(HM)[None, :] // M, 0.0, BIG).astype(f)
    c["c_pairmask"] = (s // M == np.arange(32)[None, :] // DK).astype(f)
    up = np.where(t > s, BIG, 0.0).astype(f)
    none = np.zeros((128, 128), f)
    c["c_negmask"] = np.stack([np.tile(up, (1, 4)), np.tile(np.concatenate([none, up], 1), (1, 2))], 1)
    c["c_negmaskT"] = np.stack([np.tile(np.concatenate([up.T, none], 1), (1, 2)), np.tile(up.T, (1, 4))], 1)
    c["c_chunkmask"] = (s // C == np.arange(2)[None, :]).astype(f)
    c["c_iota"] = np.repeat(np.arange(NE, dtype=f)[None, :], 128, 0)
    return {k: np.ascontiguousarray(v) for k, v in c.items()}


def _padded(a, rows, cols, r0=0, c0=0):
    out = np.zeros((rows, cols), a.dtype)
    out[r0:r0 + a.shape[0], c0:c0 + a.shape[1]] = a
    return out


def kernel(**inputs):
    import ml_dtypes
    import concourse.bacc as _bacc
    from concourse.bass_utils import run_bass_kernel_spmd as _run

    g = {k: np.asarray(v) for k, v in inputs.items()}
    x = g["L0_attn_x"]
    wqkv, bqkv = g["L0_ffn_Wqkv"], g["L0_ffn_bqkv"]
    arrays = dict(
        x_tok=x,
        x_T=x.transpose(0, 2, 1),
        w_qk=np.stack([g["L0_attn_Wq"], g["L0_attn_Wk"]], 1),
        w_v=g["L0_attn_Wv"],
        w_fg=_padded(np.concatenate([g["L0_attn_Wf1"], g["L0_attn_Wg1"]], 1), 128, 128),
        w_f2=_padded(g["L0_attn_Wf2"], 128, HM),
        w_g2=_padded(g["L0_attn_Wg2"], 128, 128, DK),
        w_o=g["L0_attn_Wo"],
        norm_w=g["L0_attn_norm_w"][:, None],
        ln1=np.stack([g["L0_ffn_ln1_w"], g["L0_ffn_ln1_b"]], 1),
        ln2=np.stack([g["L0_ffn_ln2_w"], g["L0_ffn_ln2_b"]], 1),
        w2_qk=wqkv[:, :2 * D].reshape(D, 2, D),
        w2_v=wqkv[:, 2 * D:],
        b2_qk=bqkv[:2 * D].reshape(2, D).T,
        bv=bqkv[2 * D:],
        w2_o=g["L0_ffn_Wo"],
        bo=g["L0_ffn_bo"],
        gate_w=g["L0_ffn_gate_W"],
        fc1=g["L0_ffn_fc1_w"].transpose(2, 0, 1),
        fc1_b=g["L0_ffn_fc1_b"].reshape(NE * FC, 128).T,
        fc2=g["L0_ffn_fc2_w"].reshape(NE, D, FC, 128).transpose(3, 0, 2, 1),
        fc2_b=_padded(g["L0_ffn_fc2_b"], 128, 128),
    )
    arrays.update(_constants())
    arrays["c_identb"] = arrays["c_ident"].astype(ml_dtypes.bfloat16)
    for k in ("c_offhead", "c_negmask", "c_negmaskT"):
        arrays[k] = arrays[k].astype(ml_dtypes.bfloat16)

    nc = _bacc.Bacc("TRN2", target_bir_lowering=False, num_devices=1)
    feeds, args = {}, {}
    for name, a in arrays.items():
        a = np.ascontiguousarray(a)
        feeds[f"in_{name}"] = a
        args[name] = nc.dram_tensor(f"in_{name}", a.shape, mybir.dt.from_np(a.dtype), kind="ExternalInput").ap()
    o = nc.dram_tensor("out_0_dram", _OUTS[0][0], F32, kind="ExternalOutput").ap()
    build(nc, out=o, **args)
    r = _run(nc, [feeds], core_ids=[0])
    return r.results[0]["out_0_dram"]
```

```python
from contextlib import ExitStack

import numpy as np

import concourse.bass as bass
from concourse import mybir

F32 = mybir.dt.float32
BF16 = mybir.dt.bfloat16
U32 = mybir.dt.uint32
ALU = mybir.AluOpType
ACT = mybir.ActivationFunctionType
AX_X = mybir.AxisListType.X

B, N, D = 32, 256, 128
T = N // 128
H, DK, M = 8, 16, 64
HM = H * M
HP = H // 2
C = 64
NC_STATES = N // C - 1
NH, HD = 16, 8
G4 = NH // 4
NE, F = 8, 512
FC = F // 128
EPS = 1e-5
PAIRS = [(0, 0), (0, 1), (0, 2), (1, 0), (1, 1), (2, 0)]
KS = 96
MAXROW = 96
BIG = -1e30
FMAX = 3e38


def build(nc, x_tok, x_T, w_qk, w_v, w_fg, w_f2, w_g2, w_o, norm_w, ln1, ln2, w2_qk, w2_v, b2_qk, bv, w2_o, bo,
          gate_w, fc1, fc1_b, fc2, fc2_b, c_ident, c_mid, c_win, c_wincol, c_causal, c_headmask, c_offhead,
          c_pairmask, c_negmask, c_negmaskT, c_identb, c_chunkmask, c_iota, out):
    ctx = ExitStack()
    with ctx:
        def sb(name, shape, dt=F32):
            return ctx.enter_context(nc.sbuf_tensor(name, shape, dt))

        def sem(name):
            return ctx.enter_context(nc.semaphore(name))

        ident = sb("ident", [128, 128])
        identb = sb("identb", [128, 128], BF16)
        mid = sb("mid", [128, 128])
        win = sb("win", [128, 4, 128])
        wincol = sb("wincol", [128, T, 4])
        causal = sb("causal", [128, 128])
        headmask = sb("headmask", [128, H])
        offhead = sb("offhead", [128, HM], BF16)
        pairmask = sb("pairmask", [128, 32])
        negmask = sb("negmask", [128, 2, 512], BF16)
        negmaskT = sb("negmaskT", [128, 2, 512], BF16)
        chunkmask = sb("chunkmask", [128, 2])
        iota = sb("iota", [128, NE])
        wqk = sb("wqk", [128, 2, 128])
        wv = sb("wv", [128, 128])
        wfg = sb("wfg", [128, 128])
        wf2 = sb("wf2", [128, HM])
        wg2 = sb("wg2", [128, 128])
        wo = sb("wo", [128, 128])
        nw = sb("nw", [128, 1])
        ln1c = sb("ln1c", [128, 2])
        ln2c = sb("ln2c", [128, 2])
        w2qk = sb("w2qk", [128, 2, 128])
        w2v = sb("w2v", [128, 128])
        b2qk = sb("b2qk", [128, 2])
        bvB = sb("bvB", [128, 128])
        w2o = sb("w2o", [128, 128])
        boB = sb("boB", [128, 128])
        gw = sb("gw", [128, NE])
        fc1s = sb("fc1s", [128, NE, F])
        fc1bs = sb("fc1bs", [128, NE * FC])
        fc2s = sb("fc2s", [128, NE, FC, 128])
        fc2bs = sb("fc2bs", [128, 128])
        neghalf = sb("neghalf", [128, 16])
        eps = sb("eps", [128, 16])
        epsdk = sb("epsdk", [128, 16])
        nop = sb("nop", [128, 2])


        xT = sb("xT", [128, N])
        xt = sb("xt", [128, T, 128])
        fgT = sb("fgT", [128, N])
        thqk = sb("thqk", [128, 2, N])
        stmp = thqk[:].rearrange("p j n -> p (j n)")
        qk2 = sb("qk2", [128, 2, N])
        qbd = sb("qbd", [128, 2, 4, 128])
        ktm = sb("ktm", [128, T, 2, 128])
        vtok = sb("vtok", [128, T, 128])
        vtm = sb("vtm", [128, T, 2, 128])
        thg = sb("thg", [128, T, 128])
        thf = sb("thf", [128, T, HM])
        lf = sb("lf", [128, T, HM])
        E = sb("E", [128, T, HM])
        EY = sb("EY", [128, T, HM])
        okE = EY
        Y = sb("Y", [128, T, HM])
        dm = sb("dm", [128, NC_STATES, HM])
        state = dm
        dv = sb("dv", [128, HP, 4])
        dvm = sb("dvm", [128, NC_STATES, HP, 32])
        vstate = dvm
        vtmp = sb("vtmp", [128, HP, 32])
        PTm = sb("PTm", [128, T, H, 128])
        YTbd = sb("YTbd", [128, T, HP, 2, 128])
        mx = sb("mx", [128, T, H])
        sm = sb("sm", [128, T, H])
        rs = sb("rs", [128, T, H])
        QET = lf[:].rearrange("p t (h n) -> p t h n", h=HP)
        og = sb("og", [128, T, 128])
        sq = sb("sq", [128, T, 128])
        ms = sb("ms", [128, T, H])
        oT = sb("oT", [128, T, 128])
        r1 = sb("r1", [128, T, 128])
        bng = sb("bng", [128, T, 6])
        mvg = sb("mvg", [128, T, 2])
        rstdg = sb("rstdg", [128, T * H])
        x1 = sb("x1", [128, T, 128])
        x1c = sb("x1c", [128, T, 128])
        nh = sb("nh", [128, T, 128])
        nxT = sb("nxT", [128, N])
        bn = sb("bn", [128, T, 6])
        mv = sb("mv", [128, T, 2])
        rstd = sb("rstd", [128, T])
        qkf = sb("qkf", [128, 2, N])
        parts = sb("parts", [128, 3, 2, N], BF16)
        resid = sb("resid", [128, 2, N])
        Qst = sb("Qst", [MAXROW + 3, NH, N], BF16)
        Kst = sb("Kst", [MAXROW + 3, NH, N], BF16)
        vaug = sb("vaug", [128, T, NH, 32])
        nmax = sb("nmax", [128, T, NH])
        mparts = sb("mparts", [128, T, 128])
        mpb = sb("mpb", [128, T, NH], BF16)
        mres = sb("mres", [128, T, NH])
        mT = sb("mT", [3 * NH, N], BF16)
        pT = sb("pT", [128, 2, 3, 512])
        oT2 = sb("oT2", [128, G4, N])
        rec = sb("rec", [128, T, NH])
        at = sb("at", [128, T, 128])
        aT = sb("aT", [128, T, 128])
        x2 = sb("x2", [128, T, 128])
        x12 = sb("x12", [128, T, 128])
        lg = sb("lg", [128, T, NE])
        top = sb("top", [128, T, 8])
        topi = sb("topi", [128, T, 8], U32)
        topf = sb("topf", [128, T, 8])
        gd = sb("gd", [128, T, 4])
        oh = sb("oh", [128, NE])
        gates = sb("gates", [128, T, 128])
        gT = sb("gT", [128, T, 128])
        nx2T = sb("nx2T", [128, N])
        gatesm = sb("gatesm", [128, T, NE])
        hx = sb("hx", [128, NE, FC, N])
        acc = sb("acc", [128, T, 128])
        xo = sb("xo", [128, T, 128])
        bnm = sb("bnm", [128, T, 6])
        mvm = sb("mvm", [128, T, 2])
        rstdm = sb("rstdm", [128, T])

        ps = ctx.enter_context(nc.psum_tensor("ps", [128, 8, 512], F32))
        bank = [ps[:, k, :] for k in range(8)]
        scratch = nc.dram_tensor("scratch", (3, 2, 128, N), BF16, kind="Internal").ap()

        s_consts_in = sem("consts_in")
        s_zeroed = sem("zeroed")
        s_wo_scaled = sem("wo_scaled")
        s_xT_in = sem("xT_in")
        s_xt_in = sem("xt_in")
        s_fgv_ps = sem("fgv_ps")
        s_fgv_ready = sem("fgv_ready")
        s_qk_ps = sem("qk_ps")
        s_th_qk = sem("th_qk")
        s_qk2_ready = sem("qk2_ready")
        s_vtm_ready = sem("vtm_ready")
        s_g_ps = sem("g_ps")
        s_th_g = sem("th_g")
        s_f_ps = sem("f_ps")
        s_lnu_ready = sem("lnu_ready")
        s_ls_ready = sem("ls_ready")
        s_kt_ps = sem("kt_ps")
        s_kt_ready = sem("kt_ready")
        s_qbd_ready = sem("qbd_ready")
        s_pt_ps = sem("pt_ps")
        s_pt_ready = sem("pt_ready")
        s_gp_ps = sem("gp_ps")
        s_ey_ready = sem("ey_ready")
        s_dv_ps = sem("dv_ps")
        s_dv_ready = sem("dv_ready")
        s_dvm_ready = sem("dvm_ready")
        s_y_ready = sem("y_ready")
        s_d_ps = sem("d_ps")
        s_d_ready = sem("d_ready")
        s_yt_ps = sem("yt_ps")
        s_yt_lo = sem("yt_lo")
        s_yt_hi = sem("yt_hi")
        s_kty_ps = sem("kty_ps")
        s_state_ready = sem("state_ready")
        s_yv_ps = sem("yv_ps")
        s_vstate_ready = sem("vstate_ready")
        s_ok_ps = sem("ok_ps")
        s_oke_ready = sem("oke_ready")
        s_sub_ready = sem("sub_ready")
        s_exp_ready = sem("exp_ready")
        s_qe_ready = sem("qe_ready")
        s_qet_ps = sem("qet_ps")
        s_qet_ready = sem("qet_ready")
        s_r_ps = sem("r_ps")
        s_r_ready = sem("r_ready")
        s_ov_ps = sem("ov_ps")
        s_gvar_ready = sem("gvar_ready")
        s_grstd_ready = sem("grstd_ready")
        s_og_ready = sem("og_ready")
        s_ot_ps = sem("ot_ps")
        s_ot_ready = sem("ot_ready")
        s_pr_ps = sem("pr_ps")
        s_r1_ready = sem("r1_ready")
        s_x1_ready = sem("x1_ready")
        s_x1c_ready = sem("x1c_ready")
        s_nh_ready = sem("nh_ready")
        s_nht_ps = sem("nht_ps")
        s_nxt_ready = sem("nxt_ready")
        s_pqk_ps = sem("pqk_ps")
        s_qkf_ready = sem("qkf_ready")
        s_pv_ps = sem("pv_ps")
        s_vaug_ready = sem("vaug_ready")
        s_parts_ready = sem("parts_ready")
        s_parts_out = sem("parts_out")
        s_q_stack = sem("q_stack")
        s_k_stack = sem("k_stack")
        s_s_ps = sem("s_ps")
        s_s_max = sem("s_max")
        s_mt_in = sem("mt_in")
        s_mt_ps = sem("mt_ps")
        s_mt_ready = sem("mt_ready")
        s_mx_stack = sem("mx_stack")
        s_s2_ps = sem("s2_ps")
        s_p_ready = sem("p_ready")
        s_o2_ps = sem("o2_ps")
        s_o2_ready = sem("o2_ready")
        s_tr_ps = sem("tr_ps")
        s_at_ready = sem("at_ready")
        s_aat_ps = sem("aat_ps")
        s_aat_ready = sem("aat_ready")
        s_pr2_ps = sem("pr2_ps")
        s_x2_ready = sem("x2_ready")
        s_var_ready = sem("var_ready")
        s_rstd_ready = sem("rstd_ready")
        s_lg_ps = sem("lg_ps")
        s_gd_ready = sem("gd_ready")
        s_gexp_ready = sem("gexp_ready")
        s_gates_ready = sem("gates_ready")
        s_gt_ps = sem("gt_ps")
        s_gt_ready = sem("gt_ready")
        s_b2_ps = sem("b2_ps")
        s_acc_ready = sem("acc_ready")
        s_f1_ps = sem("f1_ps")
        s_h_raw = sem("h_raw")
        s_h_ready = sem("h_ready")
        s_y_ps = sem("y_ps")
        s_y_acc = sem("y_acc")
        s_varm_ready = sem("varm_ready")
        s_rstdm_ready = sem("rstdm_ready")
        s_out_ready = sem("out_ready")
        s_out_stored = sem("out_stored")
        s_dve_a_own = sem("dve_a_own")
        s_dve_b_own = sem("dve_b_own")
        s_dve_m_own = sem("dve_m_own")
        s_act_own = sem("act_own")
        s_pool_a_own = sem("pool_a_own")
        s_pool_b_own = sem("pool_b_own")
        s_pool_m_own = sem("pool_m_own")

        block = ctx.enter_context(nc.Block())

        CONSTS = [(ident, c_ident), (mid, c_mid), (win, c_win), (wincol, c_wincol), (causal, c_causal),
                  (headmask, c_headmask), (pairmask, c_pairmask), (iota, c_iota), (wqk, w_qk), (wv, w_v),
                  (wfg, w_fg), (wf2, w_f2), (wg2, w_g2), (wo, w_o), (nw, norm_w), (ln1c, ln1), (ln2c, ln2),
                  (w2qk, w2_qk), (w2v, w2_v), (b2qk, b2_qk), (bvB, bv.partition_broadcast(128)), (w2o, w2_o),
                  (boB, bo.partition_broadcast(128)), (gw, gate_w), (fc1s, fc1), (fc1bs, fc1_b), (fc2s, fc2),
                  (fc2bs, fc2_b), (identb, c_identb), (offhead, c_offhead), (negmask, c_negmask),
                  (negmaskT, c_negmaskT), (chunkmask, c_chunkmask)]
        N_CONSTS = len(CONSTS)

        ORDER = """b2 x1c proj up0 up1 nht gf up2 up3 pqk up4 kt pt0 up5 up6 pt1 up7 gp up8 up9 d up10 up11 yt sc0 up12
            kty sc1 up13 sc2 up14 mt ok up15 gelu st0 down0 st1 down1 softmax st2 down2 qet down3 st3 down4 r tr down5 ov at
            down6 og down7 pr2 down8 ot down9 nh2 down10 pr down11 lg down12 gate down13 x1 down14 gt down15 end""".split()
        NU = 2 * NE

        def nth(i, per=1, k=1):
            return i * per + k

        def first(i):
            return isinstance(i, int) and i == 0

        def over_iterations(eng, steps):
            def iteration(a, b, m):
                for step in ORDER:
                    if step.startswith("up") or step.startswith("down"):
                        name = step.rstrip("0123456789")
                        if m is not None and name in steps:
                            steps[name](m, int(step[len(name):]))
                    elif step in steps:
                        part, program = steps[step]
                        i = {"a": a, "b": b, "m": m}[part]
                        if i is not None:
                            program(i)

            iteration(0, None, None)
            iteration(1, 0, None)
            iteration(2, 1, 0)
            with eng.Fori(3, B) as i:
                iteration(i, i - 1, i - 2)
            iteration(None, B - 1, B - 2)
            iteration(None, None, B - 1)

        @block.sync
        def _(sp):
            for dst, src in CONSTS:
                sp.dma_start(dst[:], src).then_inc(s_consts_in, 16)

            def load_xT(a):
                sp.dma_start(xT[:], x_T[bass.ds(a, 1)].rearrange("o p n -> (o p) n")).then_inc(s_xT_in, 16)

            def load_xt(a):
                sp.dma_start(xt[:], x_tok[bass.ds(a, 1)].rearrange("o (t p) d -> (o p) t d", p=128)).then_inc(s_xt_in, 16)

            def iteration(a, b, m, more=True):
                if a is not None and more:
                    sp.wait_ge(s_qk_ps, nth(a))
                    load_xT(a + 1)
                if b is not None:
                    sp.wait_ge(s_parts_ready, nth(b))
                    if not first(b):
                        sp.wait_ge(s_q_stack, nth(b - 1, 96, 96))
                        sp.wait_ge(s_k_stack, nth(b - 1, 96, 96))
                    sp.dma_start(scratch.rearrange("j s p n -> p (j s) n"), parts[:].rearrange("p j s n -> p (j s) n"))\
                        .then_inc(s_parts_out, 16)
                    sp.wait_ge(s_parts_out, nth(b, 16, 16))
                    row = 0
                    for p, n in ((0, 3), (1, 2), (2, 1)):
                        for r in range(n):
                            src = scratch[p, 0].rearrange("(h d) n -> d h n", d=HD)
                            sp.dma_start(Qst[row * HD:(row + 1) * HD, :, :], src).then_inc(s_q_stack, 16)
                            row += 1
                    row = 0
                    for n in (3, 2, 1):
                        for r in range(n):
                            src = scratch[r, 1].rearrange("(h d) n -> d h n", d=HD)
                            sp.dma_start(Kst[(row + r) * HD:(row + r + 1) * HD, :, :], src).then_inc(s_k_stack, 16)
                        row += n
                    sp.wait_ge(s_mt_ready, nth(b))
                    for p in range(3):
                        sp.dma_start(Qst[MAXROW + p:MAXROW + p + 1, :, :], mT[p * NH:(p + 1) * NH, :])\
                            .then_inc(s_mx_stack, 16)
                if a is not None and more:
                    sp.wait_ge(s_r1_ready, nth(a))
                    load_xt(a + 1)
                if m is not None:
                    sp.wait_ge(s_out_ready, nth(m))
                    sp.dma_start(out[bass.ds(m, 1)].rearrange("o (t p) d -> (o p) t d", p=128), xo[:])\
                        .then_inc(s_out_stored, 16)

            load_xT(0)
            load_xt(0)
            iteration(0, None, None)
            iteration(1, 0, None)
            iteration(2, 1, 0)
            with sp.Fori(3, B - 1) as i:
                iteration(i, i - 1, i - 2)
            iteration(B - 1, B - 2, B - 3, more=False)
            iteration(None, B - 1, B - 2)
            iteration(None, None, B - 1)
            sp.wait_ge(s_out_stored, 16 * B)

        @block.tensor
        def _(pe):
            def mm(o, l, r, start=True, stop=True, onto=False):
                return nc.tensor.matmul(o, l, r, start=start, stop=stop, skip_group_check=onto)

            def tiles(x, t):
                return x[:, t * 128:(t + 1) * 128]

            def proj(a):
                pe.wait_ge(s_xT_in, nth(a, 16, 16))
                if not first(a):
                    pe.wait_ge(s_r1_ready, nth(a - 1))
                mm(bank[0][:, 0:N], wfg[:], xT[:])
                for t in range(T):
                    last = mm(bank[0][:, N + t * 128:N + (t + 1) * 128], tiles(xT, t), wv[:])
                last.then_inc(s_fgv_ps, 1)
                for j in range(2):
                    last = mm(bank[1][:, j * N:(j + 1) * N], wqk[:, j, :], xT[:])
                last.then_inc(s_qk_ps, 1)

            def gf(a):
                pe.wait_ge(s_fgv_ready, nth(a))
                for t in range(T):
                    last = mm(tiles(bank[0], t), tiles(fgT, t), wg2[:])
                last.then_inc(s_g_ps, 1)
                pe.wait_ge(s_qk2_ready, nth(a))
                for t in range(T):
                    last = mm(bank[1 + t], tiles(fgT, t), wf2[:])
                last.then_inc(s_f_ps, 1)

            def kt(a):
                pe.wait_ge(s_th_g, nth(a))
                for t in range(T):
                    last = nc.tensor.transpose(tiles(bank[0], t), tiles(qk2[:, 1, :], t), ident[:])
                last.then_inc(s_kt_ps, 1)

            def pt(a, t):
                for g in range(2):
                    n = 2 * t + g
                    pe.wait_ge(s_qbd_ready, nth(a, 2 * T, n + 1))
                    if n == 0:
                        pe.wait_ge(s_kt_ready, nth(a))
                    else:
                        pe.wait_ge(s_pt_ready, nth(a, 2 * T, n))
                    mm(bank[0], tiles(qk2[:, 1, :], t), qbd[:, g, :, :]).then_inc(s_pt_ps, 1)

            def gp(a):
                pe.wait_ge(s_ls_ready, nth(a))
                for t in range(T):
                    last = mm(bank[1 + t], mid[:], lf[:, t, :])
                last.then_inc(s_gp_ps, 1)
                pe.wait_ge(s_pt_ready, nth(a, 2 * T, 2 * T))
                for hp in range(HP):
                    for t in range(T):
                        last = mm(bank[0][:, 4 * hp:4 * hp + 4], lf[:, t, hp * 128:(hp + 1) * 128], wincol[:, t, :],
                                  t == 0, t == T - 1)
                last.then_inc(s_dv_ps, 1)

            def d(a):
                for c in range(NC_STATES):
                    if c == 0:
                        pe.wait_ge(s_ey_ready, nth(a))
                    if c == 2:
                        pe.wait_ge(s_dv_ready, nth(a))
                    o = bank[(1 + c) % 3]
                    mm(o, identb[:], offhead[:], True, False)
                    if c == 1:
                        mm(o, win[:, 1, :], lf[:, 0, :], False, False)
                        last = mm(o, win[:, 2, :], lf[:, 1, :], False, True)
                    else:
                        last = mm(o, win[:, c // 2 * 3, :], lf[:, c // 2, :], False, True)
                    last.then_inc(s_d_ps, 1)

            def yt(a):
                for t in range(T):
                    pe.wait_ge(s_y_ready, nth(a, T, t + 1))
                    pe.wait_ge(s_d_ready, nth(a, NC_STATES, t + 1))
                    for hp in range(HP):
                        last = nc.tensor.transpose(tiles(bank[1 + t], hp), tiles(Y[:, t, :], hp), ident[:])
                    last.then_inc(s_yt_ps, 1)

            def kty(a):
                for c in range(NC_STATES):
                    if c == 0:
                        pe.wait_ge(s_d_ready, nth(a, NC_STATES, NC_STATES))
                    else:
                        pe.wait_ge(s_yt_lo, nth(a, T, c))
                        pe.wait_ge(s_yt_hi, nth(a, T, c))
                    mm(bank[c], ktm[:, c // 2, c % 2, :], Y[:, c // 2, :]).then_inc(s_kty_ps, 1)
                pe.wait_ge(s_state_ready, nth(a, NC_STATES, 1))
                pe.wait_ge(s_vtm_ready, nth(a))
                for c in range(NC_STATES):
                    for hp in range(HP):
                        last = mm(bank[0][:, c * 128 + hp * 32:c * 128 + (hp + 1) * 32], tiles(Y[:, c // 2, :], hp),
                                  vtm[:, c // 2, c % 2, hp * 32:(hp + 1) * 32])
                last.then_inc(s_yv_ps, 1)

            def ok(a):
                for t in range(T):
                    pe.wait_ge(s_state_ready, nth(a, NC_STATES, t + 2))
                    for h in range(H):
                        mm(bank[1 + t][:, h * M:(h + 1) * M], PTm[:, t, h, :], Y[:, t, h * M:(h + 1) * M],
                           h == 0, h == H - 1)
                    for c in range(max(2 * t, 1), 2 * t + 2):
                        last = mm(bank[1 + t][c % 2 * C:(c % 2 + 1) * C, :], qk2[:, 0, c * C:(c + 1) * C],
                                  state[:, c - 1, :], False, True, onto=True)
                    last.then_inc(s_ok_ps, 1)

            def qet(a):
                pe.wait_ge(s_vstate_ready, nth(a, NC_STATES, NC_STATES))
                for t in range(T):
                    pe.wait_ge(s_qe_ready, nth(a, T, t + 1))
                    for hp in range(HP):
                        last = nc.tensor.transpose(tiles(bank[t], hp), tiles(thf[:, t, :], hp), ident[:])
                    last.then_inc(s_qet_ps, 1)

            def r(a):
                for n in range(2 * T):
                    t, g = divmod(n, 2)
                    pe.wait_ge(s_qet_ready, nth(a, T, t + 1))
                    if n == 0:
                        pe.wait_ge(s_oke_ready, nth(a, T, T))
                    if n >= 2:
                        pe.wait_ge(s_r_ready, nth(a, 2 * T, n - 1))
                    for h in range(4 * g, 4 * g + 4):
                        last = mm(tiles(bank[(2, 0)[g]], h % 4), YTbd[:, t, h // 2, h % 2, :], QET[:, t, h // 2, :])
                    last.then_inc(s_r_ps, 1)

            def ov(a):
                pe.wait_ge(s_qet_ready, nth(a, T, T))
                for t in range(T):
                    o = tiles(bank[1], t)
                    pe.wait_ge(s_r_ready, nth(a, 2 * T, 2 * t + 2))
                    for h in range(H):
                        last = mm(o[:, h * DK:(h + 1) * DK], PTm[:, t, h, :], vtok[:, t, h * DK:(h + 1) * DK],
                                  h == 0, h == H - 1)
                    for c in range(max(2 * t, 1), 2 * t + 2):
                        for hp in range(HP):
                            last = mm(o[c % 2 * C:(c % 2 + 1) * C, hp * 32:(hp + 1) * 32],
                                      QET[:, t, hp, c % 2 * C:(c % 2 + 1) * C], vstate[:, c - 1, hp, :],
                                      False, True, onto=True)
                last.then_inc(s_ov_ps, 1)

            def ot(a):
                pe.wait_ge(s_og_ready, nth(a))
                for t in range(T):
                    last = nc.tensor.transpose(tiles(bank[2], t), og[:, t, :], ident[:])
                last.then_inc(s_ot_ps, 1)

            def pr(a):
                pe.wait_ge(s_ot_ready, nth(a))
                for t in range(T):
                    last = mm(tiles(bank[0], t), oT[:, t, :], wo[:])
                last.then_inc(s_pr_ps, 1)

            def nht(b):
                if not first(b):
                    pe.wait_ge(s_gt_ready, nth(b - 1))
                pe.wait_ge(s_nh_ready, nth(b, 2, 1))
                for t in range(T):
                    last = nc.tensor.transpose(tiles(bank[3], t), nh[:, t, :], ident[:])
                last.then_inc(s_nht_ps, 1)

            def pqk(b):
                pe.wait_ge(s_nxt_ready, nth(b, 2, 1))
                for j in range(2):
                    last = mm(bank[4][:, j * N:(j + 1) * N], w2qk[:, j, :], nxT[:])
                last.then_inc(s_pqk_ps, 1)
                for t in range(T):
                    last = mm(tiles(bank[5], t), tiles(nxT, t), w2v[:])
                last.then_inc(s_pv_ps, 1)

            def sc(b, part):
                if part == 0:
                    pe.wait_ge(s_q_stack, nth(b, 96, 96))
                    pe.wait_ge(s_k_stack, nth(b, 96, 96))
                    pe.wait_ge(s_vaug_ready, nth(b))
                for u in range(4 * part, 4 * part + 4):
                    if u >= 3:
                        pe.wait_ge(s_s_max, nth(b, 12, u - 2))
                    o = bank[3 + u % 3]
                    if u < 4:
                        mm(o, identb[:], negmask[:, 0, :], True, False)
                        for j in range(4):
                            last = mm(tiles(o, j), Qst[0:KS, 4 * u + j, 0:128], Kst[0:KS, 4 * u + j, 0:128], False, j == 3)
                    else:
                        mm(o, identb[:], negmask[:, 1, :], True, False)
                        for j in range(2):
                            last = mm(o[:, j * N:(j + 1) * N], Qst[0:KS, 2 * (u - 4) + j, 128:N],
                                      Kst[0:KS, 2 * (u - 4) + j, :], False, j == 1)
                    last.then_inc(s_s_ps, 1)

            def mt(b):
                pe.wait_ge(s_mt_in, nth(b))
                for t in range(T):
                    last = nc.tensor.transpose(tiles(bank[3], t), mparts[:, t, :], ident[:])
                last.then_inc(s_mt_ps, 1)

            def scores(b, g):
                for w in range(3):
                    u = 3 * g + w
                    if u >= 2:
                        pe.wait_ge(s_p_ready, nth(b, 12, u - 1))
                    o = bank[3 + u % 2]
                    mm(o, identb[:], negmaskT[:, w // 2, :], True, False)
                    for j in range(2 if w < 2 else 4):
                        h = 4 * g + (2 * w + j if w < 2 else j)
                        n = N if w < 2 else 128
                        last = mm(o[:, j * n:(j + 1) * n], Kst[:, h, w // 2 * 128:w // 2 * 128 + 128],
                                  Qst[:, h, N - n:N], False, j == (1 if w < 2 else 3))
                    last.then_inc(s_s2_ps, 1)

            def st(b, g):
                if g == 0:
                    pe.wait_ge(s_mx_stack, nth(b, 48, 48))
                    pe.wait_ge(s_mt_ready, nth(b))
                    scores(b, 0)
                if g + 1 < G4:
                    scores(b, g + 1)
                pe.wait_ge(s_p_ready, nth(b, 12, 3 * g + 3))
                if g == 2:
                    pe.wait_ge(s_o2_ready, nth(b, 2, 1))
                for j in range(4):
                    o = bank[5][32 * j:32 * j + 32, g % 2 * N:(g % 2 + 1) * N]
                    mm(o, vaug[:, 0, 4 * g + j, :], pT[:, g % 2, j // 2, j % 2 * N:(j % 2 + 1) * N], True, False)
                    last = mm(o[:, 128:N], vaug[:, 1, 4 * g + j, :], pT[:, g % 2, 2, j * 128:(j + 1) * 128], False, True)
                last.then_inc(s_o2_ps, 1)

            def tr(b):
                pe.wait_ge(s_p_ready, nth(b, 12, 12))
                for t in range(T):
                    for g in range(G4):
                        pe.wait_ge(s_o2_ready, nth(b, 2, g // 2 + 1))
                        last = nc.tensor.transpose(tiles(bank[3 + t], g), oT2[:, g, t * 128:(t + 1) * 128], ident[:])
                    last.then_inc(s_tr_ps, 1)

            def at_(b):
                pe.wait_ge(s_at_ready, nth(b))
                for t in range(T):
                    last = nc.tensor.transpose(tiles(bank[5], t), at[:, t, :], ident[:])
                last.then_inc(s_aat_ps, 1)

            def pr2(b):
                pe.wait_ge(s_aat_ready, nth(b))
                for t in range(T):
                    last = mm(tiles(bank[3], t), aT[:, t, :], w2o[:])
                last.then_inc(s_pr2_ps, 1)

            def nh2(b):
                pe.wait_ge(s_nh_ready, nth(b, 2, 2))
                for t in range(T):
                    last = nc.tensor.transpose(tiles(bank[4], t), nh[:, t, :], ident[:])
                last.then_inc(s_nht_ps, 1)

            def lgs(b):
                pe.wait_ge(s_nxt_ready, nth(b, 2, 2))
                for t in range(T):
                    last = mm(bank[5][:, t * NE:(t + 1) * NE], tiles(nx2T, t), gw[:])
                last.then_inc(s_lg_ps, 1)

            def gt(b):
                pe.wait_ge(s_gates_ready, nth(b))
                for t in range(T):
                    last = nc.tensor.transpose(tiles(bank[3], t), gates[:, t, :], ident[:])
                last.then_inc(s_gt_ps, 1)

            def b2(m):
                pe.wait_ge(s_gt_ready, nth(m))
                if not first(m):
                    pe.wait_ge(s_y_acc, nth(m - 1, NU, NU))
                for t in range(T):
                    last = mm(tiles(bank[6], t), gT[:, t, :], fc2bs[:])
                last.then_inc(s_b2_ps, 1)

            def up(m, u):
                e, pair = divmod(u, 2)
                if u == 0:
                    pe.wait_ge(s_nxt_ready, nth(m, 2, 2))
                elif u == 1:
                    pe.wait_ge(s_acc_ready, nth(m))
                else:
                    pe.wait_ge(s_h_raw, nth(m, NU, u - 1))
                for k in range(2):
                    f = 2 * pair + k
                    last = mm(bank[6 + (u + 1) % 2][:, k * N:(k + 1) * N], fc1s[:, e, f * 128:(f + 1) * 128], nx2T[:])
                last.then_inc(s_f1_ps, 1)

            def down(m, u):
                e, t = divmod(u, T)
                if t == 0:
                    pe.wait_ge(s_h_ready, nth(m, NE, e + 1))
                if u >= 2:
                    pe.wait_ge(s_y_acc, nth(m, NU, u - 1))
                else:
                    pe.wait_ge(s_h_raw, nth(m, NU, NU + u - 1))
                for f in range(FC):
                    last = mm(bank[6 + (u + 1) % 2][:, 0:128], hx[:, e, f, t * 128:(t + 1) * 128], fc2s[:, e, f, :],
                              f == 0, f == FC - 1)
                last.then_inc(s_y_ps, 1)

            pe.wait_ge(s_consts_in, N_CONSTS * 16)
            pe.wait_ge(s_zeroed, N_ZEROED)
            pe.wait_ge(s_wo_scaled, 1)
            over_iterations(pe, {
                "proj": ("a", proj), "gf": ("a", gf), "kt": ("a", kt), "pt0": ("a", lambda a: pt(a, 0)),
                "pt1": ("a", lambda a: pt(a, 1)), "gp": ("a", gp), "d": ("a", d), "yt": ("a", yt), "kty": ("a", kty),
                "ok": ("a", ok), "qet": ("a", qet), "r": ("a", r), "ov": ("a", ov), "ot": ("a", ot), "pr": ("a", pr),
                "nht": ("b", nht), "pqk": ("b", pqk), "sc0": ("b", lambda b: sc(b, 0)), "sc1": ("b", lambda b: sc(b, 1)),
                "sc2": ("b", lambda b: sc(b, 2)), "mt": ("b", mt), "st0": ("b", lambda b: st(b, 0)),
                "st1": ("b", lambda b: st(b, 1)), "st2": ("b", lambda b: st(b, 2)), "st3": ("b", lambda b: st(b, 3)),
                "tr": ("b", tr), "at": ("b", at_), "pr2": ("b", pr2), "nh2": ("b", nh2), "lg": ("b", lgs), "gt": ("b", gt),
                "b2": ("m", b2), "up": up, "down": down})

        @block.vector
        def _(dve):
            V = nc.vector
            step = {"a": 0, "b": 0, "m": 0}

            def own_a(a, ins):
                step["a"] = step["a"] % DVE_A_OWN + 1
                ins.then_inc(s_dve_a_own, 1)
                dve.wait_ge(s_dve_a_own, nth(a, DVE_A_OWN, step["a"]))

            def own_b(b, ins):
                step["b"] = step["b"] % DVE_B_OWN + 1
                ins.then_inc(s_dve_b_own, 1)
                dve.wait_ge(s_dve_b_own, nth(b, DVE_B_OWN, step["b"]))

            def own_m(m, ins):
                step["m"] = step["m"] % DVE_M_OWN + 1
                ins.then_inc(s_dve_m_own, 1)
                dve.wait_ge(s_dve_m_own, nth(m, DVE_M_OWN, step["m"]))

            def by_tile(x):
                return x.rearrange("p (t d) -> p t d", t=T)

            def centre(o, x, stats, root):
                for t in range(T):
                    last = V.tensor_scalar(o[:, t, :], x[:, t, :], stats[:, t, 0:1], root[:, t:t + 1], ALU.subtract, ALU.mult)
                return last

            def proj(a):
                dve.wait_ge(s_fgv_ps, nth(a))
                V.tensor_copy(fgT[:], bank[0][:, 0:N])
                V.tensor_copy(vtok[:], by_tile(bank[0][:, N:2 * N])).then_inc(s_fgv_ready, 1)
                dve.wait_ge(s_th_qk, nth(a))
                V.scalar_tensor_tensor(qk2[:], thqk[:], 1.0, bank[1].rearrange("p (j n) -> p j n", j=2), ALU.add, ALU.mult)\
                    .then_inc(s_qk2_ready, 1)

            def kt(a):
                dve.wait_ge(s_kt_ps, nth(a))
                for t in range(T):
                    for c in range(2):
                        last = V.tensor_copy(ktm[c * C:(c + 1) * C, t, c, :], bank[0][c * C:(c + 1) * C, t * 128:(t + 1) * 128])
                last.then_inc(s_kt_ready, 1)

            def pt(a, t):
                for g in range(2):
                    dve.wait_ge(s_pt_ps, nth(a, 2 * T, 2 * t + g + 1))
                    V.tensor_tensor(PTm[:, t, 4 * g:4 * g + 4], bank[0].rearrange("p (h n) -> p h n", h=4),
                                    causal[:].unsqueeze(1).broadcast_to([128, 4, 128]), ALU.mult).then_inc(s_pt_ready, 1)

            def gp(a):
                dve.wait_ge(s_lnu_ready, nth(a))
                V.scalar_tensor_tensor(lf[:], ps[:, 1:3, :], 0.0, lf[:], ALU.min, ALU.subtract).then_inc(s_ls_ready, 1)

            def d(a):
                dve.wait_ge(s_ey_ready, nth(a))
                for t in range(T):
                    V.scalar_tensor_tensor(Y[:, t, :], thf[:, t, :], 1.0, EY[:, t, :], ALU.subtract, ALU.mult)\
                        .then_inc(s_y_ready, 1)

            def yt(a):
                for t in range(T):
                    dve.wait_ge(s_yt_ps, nth(a, T, t + 1))
                    dve.wait_ge(s_yt_lo, nth(a, T, t + 1))
                    V.tensor_copy(YTbd[64:128, t, :, 1, :], bank[1 + t][64:128, :].rearrange("p (h n) -> p h n", h=HP))\
                        .then_inc(s_yt_hi, 1)

            def kty(a):
                dve.wait_ge(s_d_ready, nth(a, NC_STATES, NC_STATES))
                for c in range(NC_STATES):
                    dve.wait_ge(s_kty_ps, nth(a, NC_STATES, c + 1))
                    if c == 0:
                        V.tensor_tensor(state[:, 0, :], bank[0], dm[:, 0, :], ALU.mult).then_inc(s_state_ready, 1)
                    else:
                        dve.wait_ge(s_state_ready, nth(a, NC_STATES, c))
                        own_a(a, V.tensor_tensor(stmp, bank[c], state[:, c - 1, :], ALU.add))
                        V.tensor_tensor(state[:, c, :], stmp, dm[:, c, :], ALU.mult).then_inc(s_state_ready, 1)
                dve.wait_ge(s_yv_ps, nth(a))
                dve.wait_ge(s_dvm_ready, nth(a))
                for c in range(NC_STATES):
                    yv = bank[0][:, c * 128:(c + 1) * 128].rearrange("p (h v) -> p h v", h=HP)
                    if c == 0:
                        V.tensor_tensor(vstate[:, 0], yv, dvm[:, 0], ALU.mult).then_inc(s_vstate_ready, 1)
                    else:
                        dve.wait_ge(s_vstate_ready, nth(a, NC_STATES, c))
                        own_a(a, V.tensor_tensor(vtmp[:], yv, vstate[:, c - 1], ALU.add))
                        V.tensor_tensor(vstate[:, c], vtmp[:], dvm[:, c], ALU.mult).then_inc(s_vstate_ready, 1)

            def ok(a):
                for t in range(T):
                    dve.wait_ge(s_ok_ps, nth(a, T, t + 1))
                    V.scalar_tensor_tensor(okE[:, t, :], bank[1 + t], -0.125, E[:, t, :], ALU.mult, ALU.mult)\
                        .then_inc(s_oke_ready, 1)
                    dve.wait_ge(s_oke_ready, nth(a, T, t + 1))
                    okh = okE[:, t, :].rearrange("p (h m) -> p h m", h=H)
                    own_a(a, V.tensor_reduce(mx[:, t, :], okh, AX_X, ALU.max))
                    V.tensor_tensor(okh, okh, mx[:, t, :].unsqueeze(2).broadcast_to([128, H, M]), ALU.subtract)\
                        .then_inc(s_sub_ready, 1)

            def softmax(a):
                for t in range(T):
                    dve.wait_ge(s_exp_ready, nth(a, T, t + 1))
                    last = V.tensor_reduce(sm[:, t, :], okE[:, t, :].rearrange("p (h m) -> p h m", h=H), AX_X, ALU.add)
                own_a(a, last)
                own_a(a, V.reciprocal(rs[:], sm[:]))

            def r(a):
                for n in range(2 * T):
                    t, g = divmod(n, 2)
                    dve.wait_ge(s_r_ps, nth(a, 2 * T, n + 1))
                    V.scalar_tensor_tensor(PTm[:, t, 4 * g:4 * g + 4], bank[(2, 0)[g]].rearrange("p (h n) -> p h n", h=4), FMAX,
                                           causal[:].unsqueeze(1).broadcast_to([128, 4, 128]), ALU.min, ALU.mult)\
                        .then_inc(s_r_ready, 1)

            def og_(a):
                dve.wait_ge(s_ov_ps, nth(a))
                own_a(a, V.scalar_tensor_tensor(og[:], thg[:], 1.0, by_tile(bank[1][:, 0:N]), ALU.add, ALU.mult))
                ogh = og[:].rearrange("p t (h v) -> p (t h) v", h=H)
                own_a(a, V.scalar_tensor_tensor(ogh, ogh, -0.25, rs[:].rearrange("p t h -> p (t h)").unsqueeze(2)
                                                .broadcast_to([128, T * H, DK]), ALU.mult, ALU.mult))
                own_a(a, V.tensor_tensor(sq[:], og[:], og[:], ALU.mult))
                V.tensor_reduce(ms[:].rearrange("p t h -> p (t h)"), sq[:].rearrange("p t (h v) -> p (t h) v", h=H),
                                AX_X, ALU.add).then_inc(s_gvar_ready, 1)

            def ot(a):
                dve.wait_ge(s_grstd_ready, nth(a, 2, 1))
                V.tensor_tensor(og[:].rearrange("p t (h v) -> p (t h) v", h=H), og[:].rearrange("p t (h v) -> p (t h) v", h=H),
                                rstdg[:].unsqueeze(2).broadcast_to([128, T * H, DK]), ALU.mult).then_inc(s_og_ready, 1)

            def pr(a):
                dve.wait_ge(s_pr_ps, nth(a))
                dve.wait_ge(s_xt_in, nth(a, 16, 16))
                V.tensor_tensor(r1[:], by_tile(bank[0][:, 0:N]), xt[:], ALU.add).then_inc(s_r1_ready, 1)
                dve.wait_ge(s_r1_ready, nth(a))
                for t in range(T):
                    last = V.bn_stats(bng[:, t, :], r1[:, t, :])
                own_a(a, last)
                V.tensor_copy(nop[:, 0:1], neghalf[:, 0:1])
                for t in range(T):
                    last = V.bn_aggr(mvg[:, t, :], bng[:, t, :])
                last.then_inc(s_gvar_ready, 1)

            def x1_(a):
                dve.wait_ge(s_grstd_ready, nth(a, 2, 2))
                centre(x1, r1, mvg, rstdg).then_inc(s_x1_ready, 1)

            def stats_b(b, x):
                for t in range(T):
                    last = V.bn_stats(bn[:, t, :], x[:, t, :])
                own_b(b, last)
                V.tensor_copy(nop[:, 0:1], neghalf[:, 0:1])
                for t in range(T):
                    last = V.bn_aggr(mv[:, t, :], bn[:, t, :])
                last.then_inc(s_var_ready, 1)

            def x1c_(b):
                dve.wait_ge(s_x1_ready, nth(b))
                V.tensor_copy(x1c[:], x1[:]).then_inc(s_x1c_ready, 1)
                dve.wait_ge(s_x1c_ready, nth(b))
                stats_b(b, x1c)

            def nht(b):
                dve.wait_ge(s_rstd_ready, nth(b, 2, 1))
                centre(nh, x1c, mv, rstd).then_inc(s_nh_ready, 1)

            def pqk(b):
                dve.wait_ge(s_pqk_ps, nth(b))
                V.tensor_scalar(qkf[:, 0, :], bank[4][:, 0:N], b2qk[:, 0:1], HD ** -0.5, ALU.add, ALU.mult)
                V.tensor_scalar(qkf[:, 1, :], bank[4][:, N:2 * N], b2qk[:, 1:2], None, ALU.add).then_inc(s_qkf_ready, 1)
                dve.wait_ge(s_qkf_ready, nth(b))
                if not first(b):
                    dve.wait_ge(s_parts_out, nth(b - 1, 16, 16))
                own_b(b, V.tensor_copy(parts[:, 0], qkf[:]))
                own_b(b, V.tensor_tensor(resid[:], qkf[:], parts[:, 0], ALU.subtract))
                own_b(b, V.tensor_copy(parts[:, 1], resid[:]))
                own_b(b, V.tensor_tensor(resid[:], resid[:], parts[:, 1], ALU.subtract))
                V.tensor_copy(parts[:, 2], resid[:]).then_inc(s_parts_ready, 1)
                dve.wait_ge(s_pv_ps, nth(b))
                V.tensor_tensor(vaug[:, :, :, 0:HD], bank[5][:, 0:N].rearrange("p (t h v) -> p t h v", t=T, h=NH),
                                bvB[:].rearrange("p (h v) -> p h v", h=NH).unsqueeze(1).broadcast_to([128, T, NH, HD]),
                                ALU.add).then_inc(s_vaug_ready, 1)

            def sc(b, part):
                for u in range(4 * part, 4 * part + 4):
                    dve.wait_ge(s_s_ps, nth(b, 12, u + 1))
                    if u < 4:
                        o, n = nmax[:, 0, 4 * u:4 * u + 4], 4
                    else:
                        o, n = nmax[:, 1, 2 * (u - 4):2 * (u - 4) + 2], 2
                    V.tensor_reduce(o, bank[3 + u % 3].rearrange("p (h n) -> p h n", h=n), AX_X, ALU.max).then_inc(s_s_max, 1)
                if part == 2:
                    dve.wait_ge(s_s_max, nth(b, 12, 12))
                    own_b(b, V.tensor_scalar(mres[:], nmax[:], -1.0, None, ALU.mult))
                    for j in range(3):
                        own_b(b, V.tensor_copy(mpb[:], mres[:]))
                        last = V.tensor_copy(mparts[:, :, j * NH:(j + 1) * NH], mpb[:])
                        if j < 2:
                            own_b(b, V.tensor_tensor(mres[:], mres[:], mpb[:], ALU.subtract))
                    last.then_inc(s_mt_in, 1)

            def tr(b):
                for t in range(T):
                    dve.wait_ge(s_tr_ps, nth(b, T, t + 1))
                    o4 = bank[3 + t].rearrange("p (h w) -> p h w", h=NH)
                    own_b(b, V.reciprocal(rec[:, t, :].unsqueeze(2), o4[:, :, HD:HD + 1]))
                    last = V.tensor_tensor(at[:, t, :].rearrange("p (h v) -> p h v", h=NH), o4[:, :, 0:HD],
                                           rec[:, t, :].unsqueeze(2).broadcast_to([128, NH, HD]), ALU.mult)
                last.then_inc(s_at_ready, 1)

            def pr2(b):
                dve.wait_ge(s_pr2_ps, nth(b))
                own_b(b, V.tensor_tensor(x2[:], by_tile(bank[3][:, 0:N]), boB[:].unsqueeze(1).broadcast_to([128, T, 128]),
                                         ALU.add))
                V.tensor_tensor(x2[:], x2[:], x1c[:], ALU.add).then_inc(s_x2_ready, 1)
                dve.wait_ge(s_x2_ready, nth(b))
                stats_b(b, x2)

            def nh2(b):
                V.tensor_tensor(x12[:], x2[:], x1c[:], ALU.add)
                dve.wait_ge(s_rstd_ready, nth(b, 2, 2))
                centre(nh, x2, mv, rstd).then_inc(s_nh_ready, 1)

            def lgs(b):
                dve.wait_ge(s_lg_ps, nth(b))
                own_b(b, V.tensor_copy(lg[:], bank[5][:, 0:T * NE].rearrange("p (t e) -> p t e", t=T)))
                V.tensor_copy(nop[:, 0:1], neghalf[:, 0:1])
                for t in range(T):
                    last = V.max(top[:, t, :], lg[:, t, :])
                own_b(b, last)
                V.tensor_copy(nop[:, 0:1], neghalf[:, 0:1])
                for t in range(T):
                    V.max_index(topi[:, t, :], top[:, t, :], lg[:, t, :])
                own_b(b, V.tensor_tensor(gd[:, :, 0:1], top[:, :, 1:2], top[:, :, 0:1], ALU.subtract))
                V.tensor_copy(topf[:], topi[:]).then_inc(s_gd_ready, 1)

            def gate(b):
                dve.wait_ge(s_gexp_ready, nth(b))
                own_b(b, V.tensor_scalar(gd[:, :, 2:3], gd[:, :, 1:2], 1.0, None, ALU.add))
                own_b(b, V.reciprocal(gd[:, :, 0:1], gd[:, :, 2:3]))
                own_b(b, V.tensor_tensor(gd[:, :, 3:4], gd[:, :, 0:1], gd[:, :, 1:2], ALU.mult))
                for t in range(T):
                    own_b(b, V.tensor_scalar(gates[:, t, 0:NE], iota[:], topf[:, t, 0:1], gd[:, t, 0:1], ALU.is_equal, ALU.mult))
                    own_b(b, V.tensor_scalar(oh[:], iota[:], topf[:, t, 1:2], gd[:, t, 3:4], ALU.is_equal, ALU.mult))
                    last = V.tensor_tensor(gates[:, t, 0:NE], gates[:, t, 0:NE], oh[:], ALU.add)
                last.then_inc(s_gates_ready, 1)

            def gt(b):
                dve.wait_ge(s_gt_ps, nth(b))
                V.tensor_copy(gT[:], by_tile(bank[3][:, 0:N])).then_inc(s_gt_ready, 1)

            def b2(m):
                dve.wait_ge(s_b2_ps, nth(m))
                if not first(m):
                    dve.wait_ge(s_out_ready, nth(m - 1))
                V.tensor_copy(gatesm[:], gates[:, :, 0:NE])
                V.tensor_tensor(acc[:], x12[:], by_tile(bank[6][:, 0:N]), ALU.add).then_inc(s_acc_ready, 1)

            def up(m, u):
                e, pair = divmod(u, 2)
                dve.wait_ge(s_f1_ps, nth(m, NU, u + 1))
                if u == 0 and not first(m):
                    dve.wait_ge(s_y_ps, nth(m - 1, NU, NU))
                for k in range(2):
                    f = 2 * pair + k
                    last = V.tensor_scalar(hx[:, e, f, :], bank[6 + (u + 1) % 2][:, k * N:(k + 1) * N],
                                           fc1bs[:, e * FC + f:e * FC + f + 1], None, ALU.add)
                last.then_inc(s_h_raw, 1)

            def down(m, u):
                e, t = divmod(u, T)
                dve.wait_ge(s_y_ps, nth(m, NU, u + 1))
                if u >= T:
                    dve.wait_ge(s_y_acc, nth(m, NU, u - T + 1))
                else:
                    dve.wait_ge(s_acc_ready, nth(m))
                V.scalar_tensor_tensor(acc[:, t, :], bank[6 + (u + 1) % 2][:, 0:128], gatesm[:, t, e:e + 1], acc[:, t, :],
                                       ALU.mult, ALU.add).then_inc(s_y_acc, 1)

            def end(m):
                dve.wait_ge(s_y_acc, nth(m, NU, NU))
                if not first(m):
                    dve.wait_ge(s_out_stored, nth(m - 1, 16, 16))
                for t in range(T):
                    last = V.bn_stats(bnm[:, t, :], acc[:, t, :])
                own_m(m, last)
                V.tensor_copy(nop[:, 0:1], neghalf[:, 0:1])
                for t in range(T):
                    last = V.bn_aggr(mvm[:, t, :], bnm[:, t, :])
                last.then_inc(s_varm_ready, 1)
                dve.wait_ge(s_rstdm_ready, nth(m))
                centre(xo, acc, mvm, rstdm).then_inc(s_out_ready, 1)

            dve.wait_ge(s_consts_in, N_CONSTS * 16)
            dve.wait_ge(s_zeroed, N_ZEROED)
            V.tensor_scalar(wo[:], wo[:], nw[:, 0:1], DK ** 0.5, ALU.mult, ALU.mult).then_inc(s_wo_scaled, 1)
            over_iterations(dve, {
                "proj": ("a", proj), "kt": ("a", kt), "pt0": ("a", lambda a: pt(a, 0)), "pt1": ("a", lambda a: pt(a, 1)),
                "gp": ("a", gp), "d": ("a", d), "yt": ("a", yt), "kty": ("a", kty), "ok": ("a", ok), "softmax": ("a", softmax),
                "r": ("a", r), "og": ("a", og_), "ot": ("a", ot), "pr": ("a", pr), "x1": ("a", x1_),
                "x1c": ("b", x1c_), "nht": ("b", nht), "pqk": ("b", pqk), "sc0": ("b", lambda b: sc(b, 0)),
                "sc1": ("b", lambda b: sc(b, 1)), "sc2": ("b", lambda b: sc(b, 2)), "tr": ("b", tr), "pr2": ("b", pr2),
                "nh2": ("b", nh2), "lg": ("b", lgs), "gate": ("b", gate), "gt": ("b", gt),
                "b2": ("m", b2), "up": up, "down": down, "end": ("m", end)})
            assert not any(step[k] % n for k, n in (("a", DVE_A_OWN), ("b", DVE_B_OWN), ("m", DVE_M_OWN))), step

        @block.scalar
        def _(act):
            X = nc.scalar

            def proj(a):
                act.wait_ge(s_qk_ps, nth(a))
                X.activation(thqk[:].rearrange("p j n -> p (j n)"), bank[1], ACT.Tanh, scale=0.5).then_inc(s_th_qk, 1)

            def gf(a):
                act.wait_ge(s_g_ps, nth(a))
                X.activation(thg[:].rearrange("p t n -> p (t n)"), bank[0][:, 0:N], ACT.Tanh, scale=0.5).then_inc(s_th_g, 1)
                act.wait_ge(s_f_ps, nth(a))
                X.activation(thf[:], ps[:, 1:3, :], ACT.Tanh, scale=0.5)
                X.activation(lf[:], ps[:, 1:3, :], ACT.Abs).then_inc(s_act_own, 1)
                act.wait_ge(s_act_own, nth(a, 2, 1))
                X.activation(lf[:], lf[:], ACT.Exp, scale=-1.0).then_inc(s_act_own, 1)
                act.wait_ge(s_act_own, nth(a, 2, 2))
                X.activation(lf[:], lf[:], ACT.Ln, bias=1.0).then_inc(s_lnu_ready, 1)

            def gp(a):
                act.wait_ge(s_gp_ps, nth(a))
                X.activation(EY[:], ps[:, 1:3, :], ACT.Exp, scale=-1.0)
                X.activation(E[:], ps[:, 1:3, :], ACT.Exp).then_inc(s_ey_ready, 1)
                act.wait_ge(s_dv_ps, nth(a))
                X.activation(dv[:].rearrange("p h c -> p (h c)"), bank[0][:, 0:4 * HP], ACT.Exp).then_inc(s_dv_ready, 1)

            def d(a):
                for c in range(NC_STATES):
                    act.wait_ge(s_d_ps, nth(a, NC_STATES, c + 1))
                    X.activation(dm[:, c, :], bank[(1 + c) % 3], ACT.Exp).then_inc(s_d_ready, 1)

            def yt(a):
                for t in range(T):
                    act.wait_ge(s_yt_ps, nth(a, T, t + 1))
                    X.activation(YTbd[0:64, t, :, 0, :], bank[1 + t][0:64, :].rearrange("p (h n) -> p h n", h=HP), ACT.Copy)\
                        .then_inc(s_yt_lo, 1)

            def softmax(a):
                for t in range(T):
                    act.wait_ge(s_sub_ready, nth(a, T, t + 1))
                    X.activation(okE[:, t, :], okE[:, t, :], ACT.Exp).then_inc(s_exp_ready, 1)

            def qet(a):
                for t in range(T):
                    act.wait_ge(s_qet_ps, nth(a, T, t + 1))
                    X.activation(QET[:, t].rearrange("p h n -> p (h n)"), bank[t], ACT.Copy).then_inc(s_qet_ready, 1)

            def ot(a):
                act.wait_ge(s_ot_ps, nth(a))
                X.activation(oT[:].rearrange("p t n -> p (t n)"), bank[2][:, 0:N], ACT.Copy).then_inc(s_ot_ready, 1)

            def nht(b):
                act.wait_ge(s_nht_ps, nth(b, 2, 1))
                X.activation(nxT[:], bank[3][:, 0:N], ACT.Identity, bias=ln1c[:, 1:2], scale=ln1c[:, 0:1])\
                    .then_inc(s_nxt_ready, 1)

            def mt(b):
                act.wait_ge(s_mt_ps, nth(b))
                if not first(b):
                    act.wait_ge(s_mx_stack, nth(b - 1, 48, 48))
                X.activation(mT[:], bank[3][0:3 * NH, 0:N], ACT.Copy).then_inc(s_mt_ready, 1)

            def exps(b, units):
                for u in units:
                    act.wait_ge(s_s2_ps, nth(b, 12, u + 1))
                    g, w = divmod(u, 3)
                    if g >= 2 and w == 0:
                        act.wait_ge(s_o2_ps, nth(b, G4, g - 1))
                    X.activation(pT[:, g % 2, w, :], bank[3 + u % 2], ACT.Exp).then_inc(s_p_ready, 1)

            def o2(b, k):
                act.wait_ge(s_o2_ps, nth(b, G4, 2 * k + 2))
                X.activation(oT2[:, 2 * k:2 * k + 2, :].rearrange("p g n -> p (g n)"), bank[5], ACT.Copy)\
                    .then_inc(s_o2_ready, 1)

            def st(b, g):
                if g == 0:
                    exps(b, range(0, 6))
                elif g < 3:
                    exps(b, range(3 * g + 3, 3 * g + 6))
                if g % 2:
                    o2(b, g // 2)

            def at_(b):
                act.wait_ge(s_aat_ps, nth(b))
                X.activation(aT[:].rearrange("p t n -> p (t n)"), bank[5][:, 0:N], ACT.Copy).then_inc(s_aat_ready, 1)

            def nh2(b):
                act.wait_ge(s_nht_ps, nth(b, 2, 2))
                if not first(b):
                    act.wait_ge(s_f1_ps, nth(b - 1, NU, NU))
                X.activation(nx2T[:], bank[4][:, 0:N], ACT.Identity, bias=ln2c[:, 1:2], scale=ln2c[:, 0:1])\
                    .then_inc(s_nxt_ready, 1)

            def lgs(b):
                act.wait_ge(s_gd_ready, nth(b))
                X.activation(gd[:, :, 1:2], gd[:, :, 0:1], ACT.Exp).then_inc(s_gexp_ready, 1)

            def gelu(m):
                for e in range(NE):
                    act.wait_ge(s_h_raw, nth(m, NU, 2 * e + 2))
                    X.activation(hx[:, e].rearrange("p f n -> p (f n)"), hx[:, e].rearrange("p f n -> p (f n)"), ACT.Gelu)\
                        .then_inc(s_h_ready, 1)

            act.wait_ge(s_consts_in, N_CONSTS * 16)
            act.wait_ge(s_zeroed, N_ZEROED)
            over_iterations(act, {
                "proj": ("a", proj), "gf": ("a", gf), "gp": ("a", gp), "d": ("a", d), "yt": ("a", yt),
                "softmax": ("a", softmax), "qet": ("a", qet), "ot": ("a", ot),
                "nht": ("b", nht), "mt": ("b", mt), "st0": ("b", lambda b: st(b, 0)), "st1": ("b", lambda b: st(b, 1)),
                "st2": ("b", lambda b: st(b, 2)), "st3": ("b", lambda b: st(b, 3)), "at": ("b", at_), "nh2": ("b", nh2),
                "lg": ("b", lgs), "gelu": ("m", gelu)})

        @block.gpsimd
        def _(pool):
            P = nc.gpsimd
            fills = [(ktm[:], 0.0), (YTbd[:], 0.0), (gates[:], 0.0), (Qst[:], 0.0), (Kst[:], 0.0), (vaug[:], 0.0),
                     (Kst[MAXROW:MAXROW + 3], 1.0), (vaug[:, :, :, HD:HD + 1], 1.0), (neghalf[:], -0.5), (eps[:], EPS),
                     (epsdk[:], EPS * DK), (mparts[:], 0.0)]
            assert len(fills) == N_ZEROED
            for n, (z, value) in enumerate(fills):
                pool.memset(z, value).then_inc(s_zeroed, 1)
                pool.wait_ge(s_zeroed, n + 1)
            pool.wait_ge(s_consts_in, N_CONSTS * 16)

            def proj(a):
                pool.wait_ge(s_qk2_ready, nth(a))
                for n in range(2):
                    qbd_unit(a, n)
                for t in range(T):
                    for c in range(2):
                        last = P.tensor_tensor(vtm[:, t, c, :], vtok[:, t, :], chunkmask[:, c:c + 1].broadcast_to([128, 128]),
                                               ALU.mult)
                last.then_inc(s_vtm_ready, 1)

            def qbd_unit(a, n):
                t, g = divmod(n, 2)
                if n >= 2:
                    pool.wait_ge(s_pt_ps, nth(a, 2 * T, n - 1))
                P.tensor_tensor(qbd[:, g], qk2[:, 0, t * 128:(t + 1) * 128].unsqueeze(1).broadcast_to([128, 4, 128]),
                                headmask[:, 4 * g:4 * g + 4].unsqueeze(2).broadcast_to([128, 4, 128]), ALU.mult)\
                    .then_inc(s_qbd_ready, 1)

            def pt0(a):
                for n in range(2, 4):
                    qbd_unit(a, n)

            def gp(a):
                pool.wait_ge(s_dv_ready, nth(a))
                for c in range(NC_STATES):
                    last = P.tensor_tensor(dvm[:, c], pairmask[:].unsqueeze(1).broadcast_to([128, HP, 32]),
                                           dv[:, :, c:c + 1].broadcast_to([128, HP, 32]), ALU.mult)
                last.then_inc(s_dvm_ready, 1)

            def softmax(a):
                for t in range(T):
                    pool.wait_ge(s_exp_ready, nth(a, T, t + 1))
                    P.tensor_tensor(thf[:, t, :], okE[:, t, :], E[:, t, :], ALU.mult).then_inc(s_qe_ready, 1)

            def og_(a):
                pool.wait_ge(s_gvar_ready, nth(a, 2, 1))
                P.tensor_tensor(rstdg[:], ms[:].rearrange("p t h -> p (t h)"), epsdk[:], ALU.add).then_inc(s_pool_a_own, 1)
                pool.wait_ge(s_pool_a_own, nth(a, 2, 1))
                P.tensor_tensor(rstdg[:], rstdg[:], neghalf[:], ALU.pow).then_inc(s_grstd_ready, 1)

            def pr(a):
                pool.wait_ge(s_gvar_ready, nth(a, 2, 2))
                P.tensor_tensor(rstdg[:, 0:T], mvg[:, :, 1], eps[:, 0:T], ALU.add).then_inc(s_pool_a_own, 1)
                pool.wait_ge(s_pool_a_own, nth(a, 2, 2))
                P.tensor_tensor(rstdg[:, 0:T], rstdg[:, 0:T], neghalf[:, 0:T], ALU.pow).then_inc(s_grstd_ready, 1)

            def root_b(b, k):
                pool.wait_ge(s_var_ready, nth(b, 2, k))
                P.tensor_tensor(rstd[:], mv[:, :, 1], eps[:, 0:T], ALU.add).then_inc(s_pool_b_own, 1)
                pool.wait_ge(s_pool_b_own, nth(b, 2, k))
                P.tensor_tensor(rstd[:], rstd[:], neghalf[:, 0:T], ALU.pow).then_inc(s_rstd_ready, 1)

            def end(m):
                pool.wait_ge(s_varm_ready, nth(m))
                P.tensor_tensor(rstdm[:], mvm[:, :, 1], eps[:, 0:T], ALU.add).then_inc(s_pool_m_own, 1)
                pool.wait_ge(s_pool_m_own, nth(m))
                P.tensor_tensor(rstdm[:], rstdm[:], neghalf[:, 0:T], ALU.pow).then_inc(s_rstdm_ready, 1)

            over_iterations(pool, {
                "proj": ("a", proj), "pt0": ("a", pt0), "gp": ("a", gp), "softmax": ("a", softmax), "og": ("a", og_),
                "pr": ("a", pr), "x1c": ("b", lambda b: root_b(b, 1)), "pr2": ("b", lambda b: root_b(b, 2)), "end": ("m", end)})


N_ZEROED = 12
DVE_A_OWN = 12
DVE_B_OWN = 25
DVE_M_OWN = 1


_OUTS = [((B, N, D), "float32")]


def _constants():
    s = np.arange(128)[:, None]
    t = np.arange(128)[None, :]
    c = {}
    f = np.float32
    c["c_ident"] = (s == t).astype(f)
    middle = t // C * C + C // 2 - 1
    same = s // C == t // C
    c["c_mid"] = (same * ((s > middle) & (s <= t)).astype(f) - same * ((s <= middle) & (s > t)).astype(f)).astype(f)
    inner = ((s >= C // 2) & (s < 128 - C // 2)).astype(f)
    late = (s >= 128 - C // 2).astype(f)
    early = (s < C // 2).astype(f)
    c["c_win"] = np.stack([np.repeat(x, 128, 1) for x in (inner, late, early, inner)], 1)
    zero = np.zeros((128, 1), f)
    c["c_wincol"] = np.stack([np.concatenate([inner, late, zero, zero], 1), np.concatenate([zero, early, inner, zero], 1)], 1)
    c["c_causal"] = (same & (s <= t)).astype(f)
    h = np.arange(H)[None, :]
    c["c_headmask"] = (s // DK == h).astype(f)
    c["c_offhead"] = np.where(s // DK == np.arange(HM)[None, :] // M, 0.0, BIG).astype(f)
    c["c_pairmask"] = (s // M == np.arange(32)[None, :] // DK).astype(f)
    up = np.where(t > s, BIG, 0.0).astype(f)
    none = np.zeros((128, 128), f)
    c["c_negmask"] = np.stack([np.tile(up, (1, 4)), np.tile(np.concatenate([none, up], 1), (1, 2))], 1)
    c["c_negmaskT"] = np.stack([np.tile(np.concatenate([up.T, none], 1), (1, 2)), np.tile(up.T, (1, 4))], 1)
    c["c_chunkmask"] = (s // C == np.arange(2)[None, :]).astype(f)
    c["c_iota"] = np.repeat(np.arange(NE, dtype=f)[None, :], 128, 0)
    return {k: np.ascontiguousarray(v) for k, v in c.items()}


def _padded(a, rows, cols, r0=0, c0=0):
    out = np.zeros((rows, cols), a.dtype)
    out[r0:r0 + a.shape[0], c0:c0 + a.shape[1]] = a
    return out


def kernel(**inputs):
    import ml_dtypes
    import concourse.bacc as _bacc
    from concourse.bass_utils import run_bass_kernel_spmd as _run

    g = {k: np.asarray(v) for k, v in inputs.items()}
    x = g["L0_attn_x"]
    wqkv, bqkv = g["L0_ffn_Wqkv"], g["L0_ffn_bqkv"]
    arrays = dict(
        x_tok=x,
        x_T=x.transpose(0, 2, 1),
        w_qk=np.stack([g["L0_attn_Wq"], g["L0_attn_Wk"]], 1),
        w_v=g["L0_attn_Wv"],
        w_fg=_padded(np.concatenate([g["L0_attn_Wf1"], g["L0_attn_Wg1"]], 1), 128, 128),
        w_f2=_padded(g["L0_attn_Wf2"], 128, HM),
        w_g2=_padded(g["L0_attn_Wg2"], 128, 128, DK),
        w_o=g["L0_attn_Wo"],
        norm_w=g["L0_attn_norm_w"][:, None],
        ln1=np.stack([g["L0_ffn_ln1_w"], g["L0_ffn_ln1_b"]], 1),
        ln2=np.stack([g["L0_ffn_ln2_w"], g["L0_ffn_ln2_b"]], 1),
        w2_qk=wqkv[:, :2 * D].reshape(D, 2, D),
        w2_v=wqkv[:, 2 * D:],
        b2_qk=bqkv[:2 * D].reshape(2, D).T,
        bv=bqkv[2 * D:],
        w2_o=g["L0_ffn_Wo"],
        bo=g["L0_ffn_bo"],
        gate_w=g["L0_ffn_gate_W"],
        fc1=g["L0_ffn_fc1_w"].transpose(2, 0, 1),
        fc1_b=g["L0_ffn_fc1_b"].reshape(NE * FC, 128).T,
        fc2=g["L0_ffn_fc2_w"].reshape(NE, D, FC, 128).transpose(3, 0, 2, 1),
        fc2_b=_padded(g["L0_ffn_fc2_b"], 128, 128),
    )
    arrays.update(_constants())
    arrays["c_identb"] = arrays["c_ident"].astype(ml_dtypes.bfloat16)
    for k in ("c_offhead", "c_negmask", "c_negmaskT"):
        arrays[k] = arrays[k].astype(ml_dtypes.bfloat16)

    nc = _bacc.Bacc("TRN2", target_bir_lowering=False, num_devices=1)
    feeds, args = {}, {}
    for name, a in arrays.items():
        a = np.ascontiguousarray(a)
        feeds[f"in_{name}"] = a
        args[name] = nc.dram_tensor(f"in_{name}", a.shape, mybir.dt.from_np(a.dtype), kind="ExternalInput").ap()
    o = nc.dram_tensor("out_0_dram", _OUTS[0][0], F32, kind="ExternalOutput").ap()
    build(nc, out=o, **args)
    r = _run(nc, [feeds], core_ids=[0])
    return r.results[0]["out_0_dram"]
```

```python
from contextlib import ExitStack

import numpy as np

import concourse.bass as bass
from concourse import mybir

F32 = mybir.dt.float32
BF16 = mybir.dt.bfloat16
U32 = mybir.dt.uint32
ALU = mybir.AluOpType
ACT = mybir.ActivationFunctionType
AX_X = mybir.AxisListType.X

B, N, D = 32, 256, 128
T = N // 128
H, DK, M = 8, 16, 64
HM = H * M
HP = H // 2
C = 64
NC_STATES = N // C - 1
NH, HD = 16, 8
G4 = NH // 4
NE, F = 8, 512
FC = F // 128
EPS = 1e-5
PAIRS = [(0, 0), (0, 1), (0, 2), (1, 0), (1, 1), (2, 0)]
KS = 96
MAXROW = 96
BIG = -1e30
FMAX = 3e38


def build(nc, x_tok, x_T, w_qk, w_v, w_fg, w_f2, w_g2, w_o, norm_w, ln1, ln2, w2_qk, w2_v, b2_qk, bv, w2_o, bo,
          gate_w, fc1, fc1_b, fc2, fc2_b, c_ident, c_mid, c_wincol, c_causal, c_headmask, c_blockmask,
          c_pairmask, c_negmask, c_negmaskT, c_identb, c_chunkmask, c_iota, out):
    ctx = ExitStack()
    with ctx:
        def sb(name, shape, dt=F32):
            return ctx.enter_context(nc.sbuf_tensor(name, shape, dt))

        def sem(name):
            return ctx.enter_context(nc.semaphore(name))

        ident = sb("ident", [128, 128])
        identb = sb("identb", [128, 128], BF16)
        mid = sb("mid", [128, 128])
        wincol = sb("wincol", [128, T, 4])
        causal = sb("causal", [128, 128])
        headmask = sb("headmask", [128, H])
        blockmask = sb("blockmask", [128, HP])
        pairmask = sb("pairmask", [128, 32])
        negmask = sb("negmask", [128, 512], BF16)
        negmaskT = sb("negmaskT", [128, 512], BF16)
        chunkmask = sb("chunkmask", [128, 2])
        iota = sb("iota", [128, NE])
        wqk = sb("wqk", [128, 2, 128])
        wv = sb("wv", [128, 128])
        wfg = sb("wfg", [128, 128])
        wf2 = sb("wf2", [128, HM])
        wg2 = sb("wg2", [128, 128])
        wo = sb("wo", [128, 128])
        nw = sb("nw", [128, 1])
        ln1c = sb("ln1c", [128, 2])
        ln2c = sb("ln2c", [128, 2])
        w2qk = sb("w2qk", [128, 2, 128])
        w2v = sb("w2v", [128, 128])
        b2qk = sb("b2qk", [128, 2])
        bvB = sb("bvB", [128, 128])
        w2o = sb("w2o", [128, 128])
        boB = sb("boB", [128, 128])
        gw = sb("gw", [128, NE])
        fc1s = sb("fc1s", [128, NE, F])
        fc1bs = sb("fc1bs", [128, NE * FC])
        fc2s = sb("fc2s", [128, NE, FC, 128])
        fc2bs = sb("fc2bs", [128, 128])
        neghalf = sb("neghalf", [128, 16])
        eps = sb("eps", [128, 16])
        epsdk = sb("epsdk", [128, 16])
        nop = sb("nop", [128, 2])


        xT = sb("xT", [128, N])
        xt = sb("xt", [128, T, 128])
        fgT = sb("fgT", [128, N])
        thqk = sb("thqk", [128, 2, N])
        qk2 = sb("qk2", [128, 2, N])
        qbd = sb("qbd", [128, 2, 4, 128])
        kvm = sb("kvm", [128, T, 2, 2, HP, 32])
        vtok = sb("vtok", [128, T, 128])
        thg = sb("thg", [128, T, 128])
        thf = sb("thf", [128, T, HM])
        lf = sb("lf", [128, T, HM])
        E = sb("E", [128, T, HM])
        EY = sb("EY", [128, T, HM])
        okE = EY
        Y = sb("Y", [128, T, HM])
        kstate = sb("kstate", [128, NC_STATES, HP, 128])
        dv = sb("dv", [128, HP, 4])
        dvm = sb("dvm", [128, NC_STATES, 2, HP, 32])
        state = dvm
        stmp = sb("stmp", [128, 2 * HP * 32])
        PTm = sb("PTm", [128, T, H, 128])
        YTbd = sb("YTbd", [128, T, HP, 2, 128])
        mx = sb("mx", [128, T, H])
        sm = sb("sm", [128, T, H])
        rs = sb("rs", [128, T, H])
        QET = lf[:].rearrange("p t (h n) -> p t h n", h=HP)
        og = sb("og", [128, T, 128])
        sq = sb("sq", [128, T, 128])
        ms = sb("ms", [128, T, H])
        oT = sb("oT", [128, T, 128])
        r1 = sb("r1", [128, T, 128])
        bng = sb("bng", [128, T, 6])
        mvg = sb("mvg", [128, T, 2])
        rstdg = sb("rstdg", [128, T * H])
        x1 = sb("x1", [128, T, 128])
        x1c = sb("x1c", [128, T, 128])
        nh = sb("nh", [128, T, 128])
        nxT = sb("nxT", [128, N])
        bn = sb("bn", [128, T, 6])
        mv = sb("mv", [128, T, 2])
        rstd = sb("rstd", [128, T])
        qkf = sb("qkf", [128, 2, N])
        parts = sb("parts", [128, 3, 2, N], BF16)
        resid = sb("resid", [128, 2, N])
        Qst = sb("Qst", [MAXROW + 3, NH, N], BF16)
        Kst = sb("Kst", [MAXROW + 3, NH, N], BF16)
        vaug = sb("vaug", [128, T, NH, 32])
        nmax = sb("nmax", [128, T, NH])
        mparts = sb("mparts", [128, T, 128])
        mpb = sb("mpb", [128, T, NH], BF16)
        mres = sb("mres", [128, T, NH])
        mT = sb("mT", [3 * NH, N], BF16)
        pT = sb("pT", [128, 2, 3, 512])
        oT2 = sb("oT2", [128, G4, N])
        rec = sb("rec", [128, T, NH])
        at = sb("at", [128, T, 128])
        aT = sb("aT", [128, T, 128])
        x2 = sb("x2", [128, T, 128])
        x12 = sb("x12", [128, T, 128])
        lg = sb("lg", [128, T, NE])
        top = sb("top", [128, T, 8])
        topi = sb("topi", [128, T, 8], U32)
        topf = sb("topf", [128, T, 8])
        gd = sb("gd", [128, T, 4])
        oh = sb("oh", [128, NE])
        gates = sb("gates", [128, T, 128])
        gT = sb("gT", [128, T, 128])
        nx2T = sb("nx2T", [128, N])
        gatesm = sb("gatesm", [128, T, NE])
        hx = sb("hx", [128, NE, FC, N])
        acc = sb("acc", [128, T, 128])
        xo = sb("xo", [128, T, 128])
        bnm = sb("bnm", [128, T, 6])
        mvm = sb("mvm", [128, T, 2])
        rstdm = sb("rstdm", [128, T])

        ps = ctx.enter_context(nc.psum_tensor("ps", [128, 8, 512], F32))
        bank = [ps[:, k, :] for k in range(8)]
        scratch = nc.dram_tensor("scratch", (3, 2, 128, N), BF16, kind="Internal").ap()

        s_consts_in = sem("consts_in")
        s_expert_consts_in = sem("expert_consts_in")
        s_zeroed = sem("zeroed")
        s_wo_scaled = sem("wo_scaled")
        s_xT_in = sem("xT_in")
        s_xt_in = sem("xt_in")
        s_fgv_ps = sem("fgv_ps")
        s_fgv_ready = sem("fgv_ready")
        s_qk_ps = sem("qk_ps")
        s_th_qk = sem("th_qk")
        s_qk2_ready = sem("qk2_ready")
        s_v_masked = sem("v_masked")
        s_g_ps = sem("g_ps")
        s_th_g = sem("th_g")
        s_f_ps = sem("f_ps")
        s_lnu_ready = sem("lnu_ready")
        s_ls_ready = sem("ls_ready")
        s_kt_ps = sem("kt_ps")
        s_kt_ready = sem("kt_ready")
        s_qbd_ready = sem("qbd_ready")
        s_pt_ps = sem("pt_ps")
        s_pt_ready = sem("pt_ready")
        s_gp_ps = sem("gp_ps")
        s_ey_ready = sem("ey_ready")
        s_dv_ps = sem("dv_ps")
        s_dv_ready = sem("dv_ready")
        s_dvm_ready = sem("dvm_ready")
        s_y_ready = sem("y_ready")
        s_yt_ps = sem("yt_ps")
        s_yt_lo = sem("yt_lo")
        s_yt_hi = sem("yt_hi")
        s_kty_ps = sem("kty_ps")
        s_state_ready = sem("state_ready")
        s_ht_ps = sem("ht_ps")
        s_kstate_ready = sem("kstate_ready")
        s_ok_ps = sem("ok_ps")
        s_oke_ready = sem("oke_ready")
        s_sub_ready = sem("sub_ready")
        s_exp_ready = sem("exp_ready")
        s_qe_ready = sem("qe_ready")
        s_qet_ps = sem("qet_ps")
        s_qet_ready = sem("qet_ready")
        s_r_ps = sem("r_ps")
        s_r_ready = sem("r_ready")
        s_ov_ps = sem("ov_ps")
        s_gvar_ready = sem("gvar_ready")
        s_grstd_ready = sem("grstd_ready")
        s_og_ready = sem("og_ready")
        s_ot_ps = sem("ot_ps")
        s_ot_ready = sem("ot_ready")
        s_pr_ps = sem("pr_ps")
        s_r1_ready = sem("r1_ready")
        s_x1_ready = sem("x1_ready")
        s_x1c_ready = sem("x1c_ready")
        s_nh_ready = sem("nh_ready")
        s_nht_ps = sem("nht_ps")
        s_nxt_ready = sem("nxt_ready")
        s_pqk_ps = sem("pqk_ps")
        s_qkf_ready = sem("qkf_ready")
        s_pv_ps = sem("pv_ps")
        s_vaug_ready = sem("vaug_ready")
        s_parts_ready = sem("parts_ready")
        s_parts_out = sem("parts_out")
        s_q_stack = sem("q_stack")
        s_k_stack = sem("k_stack")
        s_s_ps = sem("s_ps")
        s_s_max = sem("s_max")
        s_mt_in = sem("mt_in")
        s_mt_ps = sem("mt_ps")
        s_mt_ready = sem("mt_ready")
        s_mx_stack = sem("mx_stack")
        s_s2_ps = sem("s2_ps")
        s_p_ready = sem("p_ready")
        s_o2_ps = sem("o2_ps")
        s_o2_ready = sem("o2_ready")
        s_tr_ps = sem("tr_ps")
        s_at_ready = sem("at_ready")
        s_aat_ps = sem("aat_ps")
        s_aat_ready = sem("aat_ready")
        s_pr2_ps = sem("pr2_ps")
        s_x2_ready = sem("x2_ready")
        s_var_ready = sem("var_ready")
        s_rstd_ready = sem("rstd_ready")
        s_lg_ps = sem("lg_ps")
        s_gd_ready = sem("gd_ready")
        s_gexp_ready = sem("gexp_ready")
        s_gates_ready = sem("gates_ready")
        s_gt_ps = sem("gt_ps")
        s_gt_ready = sem("gt_ready")
        s_b2_ps = sem("b2_ps")
        s_acc_ready = sem("acc_ready")
        s_f1_ps = sem("f1_ps")
        s_h_raw = sem("h_raw")
        s_h_ready = sem("h_ready")
        s_y_ps = sem("y_ps")
        s_y_acc = sem("y_acc")
        s_varm_ready = sem("varm_ready")
        s_rstdm_ready = sem("rstdm_ready")
        s_out_ready = sem("out_ready")
        s_out_stored = sem("out_stored")
        s_dve_a_own = sem("dve_a_own")
        s_dve_b_own = sem("dve_b_own")
        s_dve_m_own = sem("dve_m_own")
        s_act_own = sem("act_own")
        s_pool_a_own = sem("pool_a_own")
        s_pool_b_own = sem("pool_b_own")
        s_pool_m_own = sem("pool_m_own")

        block = ctx.enter_context(nc.Block())

        CONSTS = [(ident, c_ident), (mid, c_mid), (wincol, c_wincol), (causal, c_causal),
                  (headmask, c_headmask), (pairmask, c_pairmask), (iota, c_iota), (wqk, w_qk), (wv, w_v),
                  (wfg, w_fg), (wf2, w_f2), (wg2, w_g2), (wo, w_o), (nw, norm_w), (ln1c, ln1), (ln2c, ln2),
                  (w2qk, w2_qk), (w2v, w2_v), (b2qk, b2_qk), (bvB, bv.partition_broadcast(128)), (w2o, w2_o),
                  (boB, bo.partition_broadcast(128)), (gw, gate_w), (identb, c_identb), (blockmask, c_blockmask), (negmask, c_negmask),
                  (negmaskT, c_negmaskT), (chunkmask, c_chunkmask)]
        N_CONSTS = len(CONSTS)
        EXPERT_CONSTS = [(fc1s, fc1), (fc1bs, fc1_b), (fc2s, fc2), (fc2bs, fc2_b)]
        N_EXPERT_CONSTS = len(EXPERT_CONSTS)

        ORDER = """x1c proj b2 nht up0 pqk up1 gf up2 kt gelu0 up3 up4 pt0 gelu1 up5 up6 pt1 gp sc0 sc1 sc2 y0 sc3 up7 up8
            y1 pt2 sc4 sc5 sc6 sc7 up9 sc8 sc9 sc10 gelu2 up10 up11 pt3 sc11 gelu3 gelu4 up12 gelu5 up13 dv yt0 yt1
            mt up14 kty0 up15 kty1 gelu6 down0 kty2 s0 ht0 s1 gelu7 ht1 down1 ht2 s2 s3 ok0 ok1 softmax0 s4 av0 s5
            softmax1 down2 s6 qet0 s7 down3 s8 av1 r0 s9 qet1 s10 av2 s11 r1 av3 down4 tr0 tr1 r2 r3 at down5 down6
            pr2 down7 down8 ov0 ov1 nh2 og down9 lg down10 down11 down12 ot gate down13 pr down14 down15 end0 gt x1
            end1""".split()
        NU = 2 * NE

        def nth(i, per=1, k=1):
            return i * per + k

        def first(i):
            return isinstance(i, int) and i == 0

        def over_iterations(eng, steps):
            def iteration(a, b, m):
                for step in ORDER:
                    name = step.rstrip("0123456789")
                    name, unit = (step, ()) if step in steps else (name, (int(step[len(name):] or 0),))
                    part, program = steps.get(name, ("a", None))
                    i = {"a": a, "b": b, "m": m}[part]
                    if program is not None and i is not None:
                        program(i, *unit)

            iteration(0, None, None)
            iteration(1, 0, None)
            iteration(2, 1, 0)
            with eng.Fori(3, B) as i:
                iteration(i, i - 1, i - 2)
            iteration(None, B - 1, B - 2)
            iteration(None, None, B - 1)

        @block.sync
        def _(sp):
            def load_xT(a):
                sp.dma_start(xT[:], x_T[bass.ds(a, 1)].rearrange("o p n -> (o p) n")).then_inc(s_xT_in, 16)

            def load_xt(a):
                sp.dma_start(xt[:], x_tok[bass.ds(a, 1)].rearrange("o (t p) d -> (o p) t d", p=128)).then_inc(s_xt_in, 16)

            def iteration(a, b, m, more=True):
                if a is not None and more:
                    sp.wait_ge(s_qk_ps, nth(a))
                    load_xT(a + 1)
                if b is not None:
                    sp.wait_ge(s_parts_ready, nth(b))
                    if not first(b):
                        sp.wait_ge(s_q_stack, nth(b - 1, 96, 96))
                        sp.wait_ge(s_k_stack, nth(b - 1, 96, 96))
                    sp.dma_start(scratch.rearrange("j s p n -> p (j s) n"), parts[:].rearrange("p j s n -> p (j s) n"))\
                        .then_inc(s_parts_out, 16)
                    sp.wait_ge(s_parts_out, nth(b, 16, 16))
                    row = 0
                    for p, n in ((0, 3), (1, 2), (2, 1)):
                        for r in range(n):
                            src = scratch[p, 0].rearrange("(h d) n -> d h n", d=HD)
                            sp.dma_start(Qst[row * HD:(row + 1) * HD, :, :], src).then_inc(s_q_stack, 16)
                            row += 1
                    row = 0
                    for n in (3, 2, 1):
                        for r in range(n):
                            src = scratch[r, 1].rearrange("(h d) n -> d h n", d=HD)
                            sp.dma_start(Kst[(row + r) * HD:(row + r + 1) * HD, :, :], src).then_inc(s_k_stack, 16)
                        row += n
                    sp.wait_ge(s_mt_ready, nth(b))
                    for p in range(3):
                        sp.dma_start(Qst[MAXROW + p:MAXROW + p + 1, :, :], mT[p * NH:(p + 1) * NH, :])\
                            .then_inc(s_mx_stack, 16)
                if a is not None and more:
                    sp.wait_ge(s_r1_ready, nth(a))
                    load_xt(a + 1)
                if m is not None:
                    sp.wait_ge(s_out_ready, nth(m))
                    sp.dma_start(out[bass.ds(m, 1)].rearrange("o (t p) d -> (o p) t d", p=128), xo[:])\
                        .then_inc(s_out_stored, 16)

            load_xT(0)
            for dst, src in CONSTS:
                sp.dma_start(dst[:], src).then_inc(s_consts_in, 16)
            load_xt(0)
            for dst, src in EXPERT_CONSTS:
                sp.dma_start(dst[:], src).then_inc(s_expert_consts_in, 16)
            iteration(0, None, None)
            iteration(1, 0, None)
            iteration(2, 1, 0)
            with sp.Fori(3, B - 1) as i:
                iteration(i, i - 1, i - 2)
            iteration(B - 1, B - 2, B - 3, more=False)
            iteration(None, B - 1, B - 2)
            iteration(None, None, B - 1)
            sp.wait_ge(s_out_stored, 16 * B)

        @block.tensor
        def _(pe):
            def mm(o, l, r, start=True, stop=True, onto=False):
                return nc.tensor.matmul(o, l, r, start=start, stop=stop, skip_group_check=onto)

            def tiles(x, t):
                return x[:, t * 128:(t + 1) * 128]

            def proj(a):
                pe.wait_ge(s_xT_in, nth(a, 16, 16))
                if not first(a):
                    pe.wait_ge(s_r1_ready, nth(a - 1))
                mm(bank[0][:, 0:N], wfg[:], xT[:])
                for t in range(T):
                    last = mm(bank[0][:, N + t * 128:N + (t + 1) * 128], tiles(xT, t), wv[:])
                last.then_inc(s_fgv_ps, 1)
                for j in range(2):
                    last = mm(bank[1][:, j * N:(j + 1) * N], wqk[:, j, :], xT[:])
                last.then_inc(s_qk_ps, 1)

            def gf(a):
                pe.wait_ge(s_fgv_ready, nth(a))
                for t in range(T):
                    last = mm(tiles(bank[0], t), tiles(fgT, t), wg2[:])
                last.then_inc(s_g_ps, 1)
                pe.wait_ge(s_qk2_ready, nth(a))
                for t in range(T):
                    last = mm(bank[1 + t], tiles(fgT, t), wf2[:])
                last.then_inc(s_f_ps, 1)

            def kt(a):
                pe.wait_ge(s_th_g, nth(a))
                for t in range(T):
                    last = nc.tensor.transpose(tiles(bank[0], t), tiles(qk2[:, 1, :], t), ident[:])
                last.then_inc(s_kt_ps, 1)

            def pt(a, n):
                t, g = divmod(n, 2)
                pe.wait_ge(s_qbd_ready, nth(a, 2 * T, n + 1))
                if n == 0:
                    pe.wait_ge(s_kt_ready, nth(a))
                else:
                    pe.wait_ge(s_pt_ready, nth(a, 2 * T, n))
                mm(bank[0], tiles(qk2[:, 1, :], t), qbd[:, g, :, :]).then_inc(s_pt_ps, 1)

            def gp(a):
                pe.wait_ge(s_ls_ready, nth(a))
                for t in range(T):
                    last = mm(bank[1 + t], mid[:], lf[:, t, :])
                last.then_inc(s_gp_ps, 1)

            def dv_(a):
                pe.wait_ge(s_pt_ready, nth(a, 2 * T, 2 * T))
                for hp in range(HP):
                    for t in range(T):
                        last = mm(bank[0][:, 4 * hp:4 * hp + 4], lf[:, t, hp * 128:(hp + 1) * 128], wincol[:, t, :],
                                  t == 0, t == T - 1)
                last.then_inc(s_dv_ps, 1)

            def yt(a, t):
                pe.wait_ge(s_y_ready, nth(a, T, t + 1))
                for hp in range(HP):
                    last = nc.tensor.transpose(tiles(bank[1 + t], hp), tiles(Y[:, t, :], hp), ident[:])
                last.then_inc(s_yt_ps, 1)

            def kty(a, c):
                if c == 0:
                    pe.wait_ge(s_dv_ready, nth(a))
                    pe.wait_ge(s_v_masked, nth(a))
                else:
                    pe.wait_ge(s_yt_lo, nth(a, T, c))
                    pe.wait_ge(s_yt_hi, nth(a, T, c))
                for hp in range(HP):
                    last = mm(bank[c][:, 0:N].rearrange("p (j h n) -> p j h n", j=2, h=HP)[:, :, hp, :], tiles(Y[:, c // 2, :], hp),
                              kvm[:, c // 2, c % 2, :, hp, :])
                last.then_inc(s_kty_ps, 1)

            def ht(a, c):
                pe.wait_ge(s_state_ready, nth(a, NC_STATES, c + 1))
                nc.tensor.transpose(bank[c][:, 0:128], state[:, c, 0].rearrange("p h n -> p (h n)"), ident[:]).then_inc(s_ht_ps, 1)

            def ok(a, t):
                pe.wait_ge(s_kstate_ready, nth(a, NC_STATES, t + 2))
                for h in range(H):
                    mm(bank[1 + t][:, h * M:(h + 1) * M], PTm[:, t, h, :], Y[:, t, h * M:(h + 1) * M],
                       h == 0, h == H - 1)
                for c in range(max(2 * t, 1), 2 * t + 2):
                    last = mm(bank[1 + t][c % 2 * C:(c % 2 + 1) * C, :], qk2[:, 0, c * C:(c + 1) * C],
                              kstate[:, c - 1, :, :], False, True, onto=True)
                last.then_inc(s_ok_ps, 1)

            def qet(a, t):
                pe.wait_ge(s_qe_ready, nth(a, T, t + 1))
                for hp in range(HP):
                    last = nc.tensor.transpose(tiles(bank[t], hp), tiles(thf[:, t, :], hp), ident[:])
                last.then_inc(s_qet_ps, 1)

            def r(a, n):
                t, g = divmod(n, 2)
                pe.wait_ge(s_qet_ready, nth(a, T, T if g else t + 1))
                if n == 0:
                    pe.wait_ge(s_oke_ready, nth(a, T, T))
                if n >= 2:
                    pe.wait_ge(s_r_ready, nth(a, 2 * T, n - 1))
                for h in range(4 * g, 4 * g + 4):
                    last = mm(tiles(bank[(2, 0)[g]], h % 4), YTbd[:, t, h // 2, h % 2, :], QET[:, t, h // 2, :])
                last.then_inc(s_r_ps, 1)

            def ov(a, t):
                pe.wait_ge(s_qet_ready, nth(a, T, T))
                o = tiles(bank[1], t)
                pe.wait_ge(s_r_ready, nth(a, 2 * T, 2 * t + 2))
                for h in range(H):
                    last = mm(o[:, h * DK:(h + 1) * DK], PTm[:, t, h, :], vtok[:, t, h * DK:(h + 1) * DK],
                              h == 0, h == H - 1)
                for c in range(max(2 * t, 1), 2 * t + 2):
                    for hp in range(HP):
                        last = mm(o[c % 2 * C:(c % 2 + 1) * C, hp * 32:(hp + 1) * 32],
                                  QET[:, t, hp, c % 2 * C:(c % 2 + 1) * C], state[:, c - 1, 1, hp, :],
                                  False, True, onto=True)
                if t == T - 1:
                    last.then_inc(s_ov_ps, 1)

            def ot(a):
                pe.wait_ge(s_og_ready, nth(a))
                for t in range(T):
                    last = nc.tensor.transpose(tiles(bank[2], t), og[:, t, :], ident[:])
                last.then_inc(s_ot_ps, 1)

            def pr(a):
                pe.wait_ge(s_ot_ready, nth(a))
                for t in range(T):
                    last = mm(tiles(bank[0], t), oT[:, t, :], wo[:])
                last.then_inc(s_pr_ps, 1)

            def nht(b):
                if not first(b):
                    pe.wait_ge(s_gt_ready, nth(b - 1))
                pe.wait_ge(s_nh_ready, nth(b, 2, 1))
                for t in range(T):
                    last = nc.tensor.transpose(tiles(bank[3], t), nh[:, t, :], ident[:])
                last.then_inc(s_nht_ps, 1)

            def pqk(b):
                pe.wait_ge(s_nxt_ready, nth(b, 2, 1))
                for j in range(2):
                    last = mm(bank[4][:, j * N:(j + 1) * N], w2qk[:, j, :], nxT[:])
                last.then_inc(s_pqk_ps, 1)
                for t in range(T):
                    last = mm(tiles(bank[5], t), tiles(nxT, t), w2v[:])
                last.then_inc(s_pv_ps, 1)

            def sc(b, u):
                if u == 0:
                    pe.wait_ge(s_q_stack, nth(b, 96, 96))
                    pe.wait_ge(s_k_stack, nth(b, 96, 96))
                    pe.wait_ge(s_vaug_ready, nth(b))
                if u >= 3:
                    pe.wait_ge(s_s_max, nth(b, 12, u - 2))
                o = bank[3 + u % 3]
                if u < 4:
                    for j in range(4):
                        mm(tiles(o, j), Qst[0:KS, 4 * u + j, 0:128], Kst[0:KS, 4 * u + j, 0:128], j == 0, False)
                    last = mm(o, identb[:], negmask[:], False, True)
                else:
                    for j in range(2):
                        mm(o[:, j * N:(j + 1) * N], Qst[0:KS, 2 * (u - 4) + j, 128:N], Kst[0:KS, 2 * (u - 4) + j, :],
                           j == 0, False)
                    last = mm(o.rearrange("p (j n) -> p j n", j=2)[:, :, 128:N], identb[:], negmask[:, 0:N], False, True)
                last.then_inc(s_s_ps, 1)

            def mt(b):
                pe.wait_ge(s_mt_in, nth(b))
                for t in range(T):
                    last = nc.tensor.transpose(tiles(bank[3], t), mparts[:, t, :], ident[:])
                last.then_inc(s_mt_ps, 1)

            def scores(b, u):
                g, w = divmod(u, 3)
                if u == 0:
                    pe.wait_ge(s_mx_stack, nth(b, 48, 48))
                    pe.wait_ge(s_mt_ready, nth(b))
                if u >= 2:
                    pe.wait_ge(s_p_ready, nth(b, 12, u - 1))
                o = bank[3 + u % 2]
                for j in range(2 if w < 2 else 4):
                    h = 4 * g + (2 * w + j if w < 2 else j)
                    n = N if w < 2 else 128
                    mm(o[:, j * n:(j + 1) * n], Kst[:, h, w // 2 * 128:w // 2 * 128 + 128], Qst[:, h, N - n:N], j == 0, False)
                if w < 2:
                    last = mm(o.rearrange("p (j n) -> p j n", j=2)[:, :, 0:128], identb[:], negmaskT[:, 0:N], False, True)
                else:
                    last = mm(o, identb[:], negmaskT[:], False, True)
                last.then_inc(s_s2_ps, 1)

            def av(b, g):
                pe.wait_ge(s_p_ready, nth(b, 12, 3 * g + 3))
                if g == 2:
                    pe.wait_ge(s_o2_ready, nth(b, 2, 1))
                for j in range(4):
                    o = bank[5][32 * j:32 * j + 32, g % 2 * N:(g % 2 + 1) * N]
                    mm(o, vaug[:, 0, 4 * g + j, :], pT[:, g % 2, j // 2, j % 2 * N:(j % 2 + 1) * N], True, False)
                    last = mm(o[:, 128:N], vaug[:, 1, 4 * g + j, :], pT[:, g % 2, 2, j * 128:(j + 1) * 128], False, True)
                last.then_inc(s_o2_ps, 1)

            def tr(b, t):
                pe.wait_ge(s_p_ready, nth(b, 12, 12))
                for g in range(G4):
                    pe.wait_ge(s_o2_ready, nth(b, 2, g // 2 + 1))
                    last = nc.tensor.transpose(tiles(bank[3 + t], g), oT2[:, g, t * 128:(t + 1) * 128], ident[:])
                last.then_inc(s_tr_ps, 1)

            def at_(b):
                pe.wait_ge(s_at_ready, nth(b, T, T))
                for t in range(T):
                    last = nc.tensor.transpose(tiles(bank[5], t), at[:, t, :], ident[:])
                last.then_inc(s_aat_ps, 1)

            def pr2(b):
                pe.wait_ge(s_aat_ready, nth(b))
                for t in range(T):
                    last = mm(tiles(bank[3], t), aT[:, t, :], w2o[:])
                last.then_inc(s_pr2_ps, 1)

            def nh2(b):
                pe.wait_ge(s_nh_ready, nth(b, 2, 2))
                for t in range(T):
                    last = nc.tensor.transpose(tiles(bank[4], t), nh[:, t, :], ident[:])
                last.then_inc(s_nht_ps, 1)

            def lgs(b):
                pe.wait_ge(s_nxt_ready, nth(b, 2, 2))
                for t in range(T):
                    last = mm(bank[5][:, t * NE:(t + 1) * NE], tiles(nx2T, t), gw[:])
                last.then_inc(s_lg_ps, 1)

            def gt(b):
                pe.wait_ge(s_gates_ready, nth(b))
                for t in range(T):
                    last = nc.tensor.transpose(tiles(bank[3], t), gates[:, t, :], ident[:])
                last.then_inc(s_gt_ps, 1)

            def b2(m):
                if first(m):
                    pe.wait_ge(s_expert_consts_in, 16 * N_EXPERT_CONSTS)
                pe.wait_ge(s_gt_ready, nth(m))
                if not first(m):
                    pe.wait_ge(s_y_acc, nth(m - 1, NU, NU))
                for t in range(T):
                    last = mm(tiles(bank[6], t), gT[:, t, :], fc2bs[:])
                last.then_inc(s_b2_ps, 1)

            def up(m, u):
                e, pair = divmod(u, 2)
                if u == 0:
                    pe.wait_ge(s_nxt_ready, nth(m, 2, 2))
                elif u == 1:
                    pe.wait_ge(s_acc_ready, nth(m))
                else:
                    pe.wait_ge(s_h_raw, nth(m, NU, u - 1))
                for k in range(2):
                    f = 2 * pair + k
                    last = mm(bank[6 + (u + 1) % 2][:, k * N:(k + 1) * N], fc1s[:, e, f * 128:(f + 1) * 128], nx2T[:])
                last.then_inc(s_f1_ps, 1)

            def down(m, u):
                e, t = divmod(u, T)
                if t == 0:
                    pe.wait_ge(s_h_ready, nth(m, NE, e + 1))
                if u >= 2:
                    pe.wait_ge(s_y_acc, nth(m, NU, u - 1))
                else:
                    pe.wait_ge(s_h_raw, nth(m, NU, NU + u - 1))
                for f in range(FC):
                    last = mm(bank[6 + (u + 1) % 2][:, 0:128], hx[:, e, f, t * 128:(t + 1) * 128], fc2s[:, e, f, :],
                              f == 0, f == FC - 1)
                last.then_inc(s_y_ps, 1)

            pe.wait_ge(s_consts_in, N_CONSTS * 16)
            pe.wait_ge(s_zeroed, N_ZEROED)
            pe.wait_ge(s_wo_scaled, 1)
            over_iterations(pe, {
                "proj": ("a", proj), "gf": ("a", gf), "kt": ("a", kt), "pt": ("a", pt), "gp": ("a", gp), "dv": ("a", dv_),
                "yt": ("a", yt), "kty": ("a", kty), "ht": ("a", ht), "ok": ("a", ok), "qet": ("a", qet),
                "r": ("a", r), "ov": ("a", ov), "ot": ("a", ot), "pr": ("a", pr),
                "nht": ("b", nht), "pqk": ("b", pqk), "sc": ("b", sc), "mt": ("b", mt), "s": ("b", scores), "av": ("b", av),
                "tr": ("b", tr), "at": ("b", at_), "pr2": ("b", pr2), "nh2": ("b", nh2), "lg": ("b", lgs), "gt": ("b", gt),
                "b2": ("m", b2), "up": ("m", up), "down": ("m", down)})

        @block.vector
        def _(dve):
            V = nc.vector
            step = {"a": 0, "b": 0, "m": 0}

            def own_a(a, ins):
                step["a"] = step["a"] % DVE_A_OWN + 1
                ins.then_inc(s_dve_a_own, 1)
                dve.wait_ge(s_dve_a_own, nth(a, DVE_A_OWN, step["a"]))

            def own_b(b, ins):
                step["b"] = step["b"] % DVE_B_OWN + 1
                ins.then_inc(s_dve_b_own, 1)
                dve.wait_ge(s_dve_b_own, nth(b, DVE_B_OWN, step["b"]))

            def own_m(m, ins):
                step["m"] = step["m"] % DVE_M_OWN + 1
                ins.then_inc(s_dve_m_own, 1)
                dve.wait_ge(s_dve_m_own, nth(m, DVE_M_OWN, step["m"]))

            def by_tile(x):
                return x.rearrange("p (t d) -> p t d", t=T)

            def centre(o, x, stats, root):
                for t in range(T):
                    last = V.tensor_scalar(o[:, t, :], x[:, t, :], stats[:, t, 0:1], root[:, t:t + 1], ALU.subtract, ALU.mult)
                return last

            def proj(a):
                dve.wait_ge(s_fgv_ps, nth(a))
                V.tensor_copy(fgT[:], bank[0][:, 0:N])
                V.tensor_copy(vtok[:], by_tile(bank[0][:, N:2 * N])).then_inc(s_fgv_ready, 1)
                dve.wait_ge(s_th_qk, nth(a))
                V.scalar_tensor_tensor(qk2[:], thqk[:], 1.0, bank[1].rearrange("p (j n) -> p j n", j=2), ALU.add, ALU.mult)\
                    .then_inc(s_qk2_ready, 1)

            def kt(a):
                dve.wait_ge(s_kt_ps, nth(a))
                for t in range(T):
                    for c in range(2):
                        last = V.tensor_copy(kvm[c * C:(c + 1) * C, t, c, 0, :, :],
                                             bank[0][c * C:(c + 1) * C, t * 128:(t + 1) * 128]
                                             .rearrange("p (h n) -> p h n", h=HP))
                last.then_inc(s_kt_ready, 1)

            def pt(a, n):
                t, g = divmod(n, 2)
                dve.wait_ge(s_pt_ps, nth(a, 2 * T, n + 1))
                V.tensor_tensor(PTm[:, t, 4 * g:4 * g + 4], bank[0].rearrange("p (h n) -> p h n", h=4),
                                causal[:].unsqueeze(1).broadcast_to([128, 4, 128]), ALU.mult).then_inc(s_pt_ready, 1)

            def gp(a):
                dve.wait_ge(s_lnu_ready, nth(a))
                V.scalar_tensor_tensor(lf[:], ps[:, 1:3, :], 0.0, lf[:], ALU.min, ALU.subtract).then_inc(s_ls_ready, 1)

            def y_(a, t):
                dve.wait_ge(s_ey_ready, nth(a))
                V.scalar_tensor_tensor(Y[:, t, :], thf[:, t, :], 1.0, EY[:, t, :], ALU.subtract, ALU.mult)\
                    .then_inc(s_y_ready, 1)

            def yt(a, t):
                dve.wait_ge(s_yt_ps, nth(a, T, t + 1))
                dve.wait_ge(s_yt_lo, nth(a, T, t + 1))
                V.tensor_copy(YTbd[64:128, t, :, 1, :], bank[1 + t][64:128, :].rearrange("p (h n) -> p h n", h=HP))\
                    .then_inc(s_yt_hi, 1)

            def kty(a, c):
                if c == 0:
                    dve.wait_ge(s_dvm_ready, nth(a))
                dve.wait_ge(s_kty_ps, nth(a, NC_STATES, c + 1))
                kv = bank[c][:, 0:2 * HP * 32]

                def flat(x):
                    return x[:, c].rearrange("p j h n -> p (j h n)")

                if c == 0:
                    V.tensor_tensor(flat(state), kv, flat(dvm), ALU.mult).then_inc(s_state_ready, 1)
                else:
                    dve.wait_ge(s_state_ready, nth(a, NC_STATES, c))
                    own_a(a, V.tensor_tensor(stmp[:], kv, state[:, c - 1].rearrange("p j h n -> p (j h n)"), ALU.add))
                    V.tensor_tensor(flat(state), stmp[:], flat(dvm), ALU.mult).then_inc(s_state_ready, 1)

            def ht(a, c):
                dve.wait_ge(s_ht_ps, nth(a, NC_STATES, c + 1))
                V.tensor_tensor(kstate[:, c], bank[c][:, 0:128].unsqueeze(1).broadcast_to([128, HP, 128]),
                                blockmask[:].unsqueeze(2).broadcast_to([128, HP, 128]), ALU.mult).then_inc(s_kstate_ready, 1)

            def ok(a, t):
                dve.wait_ge(s_ok_ps, nth(a, T, t + 1))
                V.scalar_tensor_tensor(okE[:, t, :], bank[1 + t], -0.125, E[:, t, :], ALU.mult, ALU.mult)\
                    .then_inc(s_oke_ready, 1)
                dve.wait_ge(s_oke_ready, nth(a, T, t + 1))
                okh = okE[:, t, :].rearrange("p (h m) -> p h m", h=H)
                own_a(a, V.tensor_reduce(mx[:, t, :], okh, AX_X, ALU.max))
                V.tensor_tensor(okh, okh, mx[:, t, :].unsqueeze(2).broadcast_to([128, H, M]), ALU.subtract)\
                    .then_inc(s_sub_ready, 1)

            def softmax(a, t):
                dve.wait_ge(s_exp_ready, nth(a, T, t + 1))
                last = V.tensor_reduce(sm[:, t, :], okE[:, t, :].rearrange("p (h m) -> p h m", h=H), AX_X, ALU.add)
                if t == T - 1:
                    own_a(a, last)
                    own_a(a, V.reciprocal(rs[:], sm[:]))

            def r(a, n):
                t, g = divmod(n, 2)
                dve.wait_ge(s_r_ps, nth(a, 2 * T, n + 1))
                V.scalar_tensor_tensor(PTm[:, t, 4 * g:4 * g + 4], bank[(2, 0)[g]].rearrange("p (h n) -> p h n", h=4), FMAX,
                                       causal[:].unsqueeze(1).broadcast_to([128, 4, 128]), ALU.min, ALU.mult)\
                    .then_inc(s_r_ready, 1)

            def og_(a):
                dve.wait_ge(s_ov_ps, nth(a))
                own_a(a, V.scalar_tensor_tensor(og[:], thg[:], 1.0, by_tile(bank[1][:, 0:N]), ALU.add, ALU.mult))
                ogh = og[:].rearrange("p t (h v) -> p (t h) v", h=H)
                own_a(a, V.scalar_tensor_tensor(ogh, ogh, -0.25, rs[:].rearrange("p t h -> p (t h)").unsqueeze(2)
                                                .broadcast_to([128, T * H, DK]), ALU.mult, ALU.mult))
                own_a(a, V.tensor_tensor(sq[:], og[:], og[:], ALU.mult))
                V.tensor_reduce(ms[:].rearrange("p t h -> p (t h)"), sq[:].rearrange("p t (h v) -> p (t h) v", h=H),
                                AX_X, ALU.add).then_inc(s_gvar_ready, 1)

            def ot(a):
                dve.wait_ge(s_grstd_ready, nth(a, 2, 1))
                V.tensor_tensor(og[:].rearrange("p t (h v) -> p (t h) v", h=H), og[:].rearrange("p t (h v) -> p (t h) v", h=H),
                                rstdg[:].unsqueeze(2).broadcast_to([128, T * H, DK]), ALU.mult).then_inc(s_og_ready, 1)

            def pr(a):
                dve.wait_ge(s_pr_ps, nth(a))
                dve.wait_ge(s_xt_in, nth(a, 16, 16))
                V.tensor_tensor(r1[:], by_tile(bank[0][:, 0:N]), xt[:], ALU.add).then_inc(s_r1_ready, 1)
                dve.wait_ge(s_r1_ready, nth(a))
                for t in range(T):
                    last = V.bn_stats(bng[:, t, :], r1[:, t, :])
                own_a(a, last)
                V.tensor_copy(nop[:, 0:1], neghalf[:, 0:1])
                for t in range(T):
                    last = V.bn_aggr(mvg[:, t, :], bng[:, t, :])
                last.then_inc(s_gvar_ready, 1)

            def x1_(a):
                dve.wait_ge(s_grstd_ready, nth(a, 2, 2))
                centre(x1, r1, mvg, rstdg).then_inc(s_x1_ready, 1)

            def stats_b(b, x):
                for t in range(T):
                    last = V.bn_stats(bn[:, t, :], x[:, t, :])
                own_b(b, last)
                V.tensor_copy(nop[:, 0:1], neghalf[:, 0:1])
                for t in range(T):
                    last = V.bn_aggr(mv[:, t, :], bn[:, t, :])
                last.then_inc(s_var_ready, 1)

            def x1c_(b):
                dve.wait_ge(s_x1_ready, nth(b))
                V.tensor_copy(x1c[:], x1[:]).then_inc(s_x1c_ready, 1)
                dve.wait_ge(s_x1c_ready, nth(b))
                stats_b(b, x1c)

            def nht(b):
                dve.wait_ge(s_rstd_ready, nth(b, 2, 1))
                centre(nh, x1c, mv, rstd).then_inc(s_nh_ready, 1)

            def pqk(b):
                dve.wait_ge(s_pqk_ps, nth(b))
                V.tensor_scalar(qkf[:, 0, :], bank[4][:, 0:N], b2qk[:, 0:1], HD ** -0.5, ALU.add, ALU.mult)
                V.tensor_scalar(qkf[:, 1, :], bank[4][:, N:2 * N], b2qk[:, 1:2], None, ALU.add).then_inc(s_qkf_ready, 1)
                dve.wait_ge(s_qkf_ready, nth(b))
                if not first(b):
                    dve.wait_ge(s_parts_out, nth(b - 1, 16, 16))
                own_b(b, V.tensor_copy(parts[:, 0], qkf[:]))
                own_b(b, V.tensor_tensor(resid[:], qkf[:], parts[:, 0], ALU.subtract))
                own_b(b, V.tensor_copy(parts[:, 1], resid[:]))
                own_b(b, V.tensor_tensor(resid[:], resid[:], parts[:, 1], ALU.subtract))
                V.tensor_copy(parts[:, 2], resid[:]).then_inc(s_parts_ready, 1)
                dve.wait_ge(s_pv_ps, nth(b))
                V.tensor_tensor(vaug[:, :, :, 0:HD], bank[5][:, 0:N].rearrange("p (t h v) -> p t h v", t=T, h=NH),
                                bvB[:].rearrange("p (h v) -> p h v", h=NH).unsqueeze(1).broadcast_to([128, T, NH, HD]),
                                ALU.add).then_inc(s_vaug_ready, 1)

            def sc(b, u):
                dve.wait_ge(s_s_ps, nth(b, 12, u + 1))
                if u < 4:
                    o, n = nmax[:, 0, 4 * u:4 * u + 4], 4
                else:
                    o, n = nmax[:, 1, 2 * (u - 4):2 * (u - 4) + 2], 2
                V.tensor_reduce(o, bank[3 + u % 3].rearrange("p (h n) -> p h n", h=n), AX_X, ALU.max).then_inc(s_s_max, 1)
                if u == 11:
                    dve.wait_ge(s_s_max, nth(b, 12, 12))
                    own_b(b, V.tensor_scalar(mres[:], nmax[:], -1.0, None, ALU.mult))
                    for j in range(3):
                        own_b(b, V.tensor_copy(mpb[:], mres[:]))
                        last = V.tensor_copy(mparts[:, :, j * NH:(j + 1) * NH], mpb[:])
                        if j < 2:
                            own_b(b, V.tensor_tensor(mres[:], mres[:], mpb[:], ALU.subtract))
                    last.then_inc(s_mt_in, 1)

            def tr(b, t):
                dve.wait_ge(s_tr_ps, nth(b, T, t + 1))
                o4 = bank[3 + t].rearrange("p (h w) -> p h w", h=NH)
                own_b(b, V.reciprocal(rec[:, t, :].unsqueeze(2), o4[:, :, HD:HD + 1]))
                V.tensor_tensor(at[:, t, :].rearrange("p (h v) -> p h v", h=NH), o4[:, :, 0:HD],
                                rec[:, t, :].unsqueeze(2).broadcast_to([128, NH, HD]), ALU.mult).then_inc(s_at_ready, 1)

            def pr2(b):
                dve.wait_ge(s_pr2_ps, nth(b))
                own_b(b, V.tensor_tensor(x2[:], by_tile(bank[3][:, 0:N]), boB[:].unsqueeze(1).broadcast_to([128, T, 128]),
                                         ALU.add))
                V.tensor_tensor(x2[:], x2[:], x1c[:], ALU.add).then_inc(s_x2_ready, 1)
                dve.wait_ge(s_x2_ready, nth(b))
                stats_b(b, x2)

            def nh2(b):
                V.tensor_tensor(x12[:], x2[:], x1c[:], ALU.add)
                dve.wait_ge(s_rstd_ready, nth(b, 2, 2))
                centre(nh, x2, mv, rstd).then_inc(s_nh_ready, 1)

            def lgs(b):
                dve.wait_ge(s_lg_ps, nth(b))
                own_b(b, V.tensor_copy(lg[:], bank[5][:, 0:T * NE].rearrange("p (t e) -> p t e", t=T)))
                V.tensor_copy(nop[:, 0:1], neghalf[:, 0:1])
                for t in range(T):
                    last = V.max(top[:, t, :], lg[:, t, :])
                own_b(b, last)
                V.tensor_copy(nop[:, 0:1], neghalf[:, 0:1])
                for t in range(T):
                    V.max_index(topi[:, t, :], top[:, t, :], lg[:, t, :])
                own_b(b, V.tensor_tensor(gd[:, :, 0:1], top[:, :, 1:2], top[:, :, 0:1], ALU.subtract))
                V.tensor_copy(topf[:], topi[:]).then_inc(s_gd_ready, 1)

            def gate(b):
                dve.wait_ge(s_gexp_ready, nth(b))
                own_b(b, V.tensor_scalar(gd[:, :, 2:3], gd[:, :, 1:2], 1.0, None, ALU.add))
                own_b(b, V.reciprocal(gd[:, :, 0:1], gd[:, :, 2:3]))
                own_b(b, V.tensor_tensor(gd[:, :, 3:4], gd[:, :, 0:1], gd[:, :, 1:2], ALU.mult))
                for t in range(T):
                    own_b(b, V.tensor_scalar(gates[:, t, 0:NE], iota[:], topf[:, t, 0:1], gd[:, t, 0:1], ALU.is_equal, ALU.mult))
                    own_b(b, V.tensor_scalar(oh[:], iota[:], topf[:, t, 1:2], gd[:, t, 3:4], ALU.is_equal, ALU.mult))
                    last = V.tensor_tensor(gates[:, t, 0:NE], gates[:, t, 0:NE], oh[:], ALU.add)
                last.then_inc(s_gates_ready, 1)

            def gt(b):
                dve.wait_ge(s_gt_ps, nth(b))
                V.tensor_copy(gT[:], by_tile(bank[3][:, 0:N])).then_inc(s_gt_ready, 1)

            def b2(m):
                dve.wait_ge(s_b2_ps, nth(m))
                if not first(m):
                    dve.wait_ge(s_out_ready, nth(m - 1))
                V.tensor_copy(gatesm[:], gates[:, :, 0:NE])
                V.tensor_tensor(acc[:], x12[:], by_tile(bank[6][:, 0:N]), ALU.add).then_inc(s_acc_ready, 1)

            def up(m, u):
                e, pair = divmod(u, 2)
                if u == 0 and first(m):
                    dve.wait_ge(s_expert_consts_in, 16 * N_EXPERT_CONSTS)
                dve.wait_ge(s_f1_ps, nth(m, NU, u + 1))
                if u == 0 and not first(m):
                    dve.wait_ge(s_y_ps, nth(m - 1, NU, NU))
                for k in range(2):
                    f = 2 * pair + k
                    last = V.tensor_scalar(hx[:, e, f, :], bank[6 + (u + 1) % 2][:, k * N:(k + 1) * N],
                                           fc1bs[:, e * FC + f:e * FC + f + 1], None, ALU.add)
                last.then_inc(s_h_raw, 1)

            def down(m, u):
                e, t = divmod(u, T)
                dve.wait_ge(s_y_ps, nth(m, NU, u + 1))
                if u >= T:
                    dve.wait_ge(s_y_acc, nth(m, NU, u - T + 1))
                else:
                    dve.wait_ge(s_acc_ready, nth(m))
                V.scalar_tensor_tensor(acc[:, t, :], bank[6 + (u + 1) % 2][:, 0:128], gatesm[:, t, e:e + 1], acc[:, t, :],
                                       ALU.mult, ALU.add).then_inc(s_y_acc, 1)

            def end(m):
                dve.wait_ge(s_y_acc, nth(m, NU, NU))
                if not first(m):
                    dve.wait_ge(s_out_stored, nth(m - 1, 16, 16))
                for t in range(T):
                    last = V.bn_stats(bnm[:, t, :], acc[:, t, :])
                own_m(m, last)
                V.tensor_copy(nop[:, 0:1], neghalf[:, 0:1])
                for t in range(T):
                    last = V.bn_aggr(mvm[:, t, :], bnm[:, t, :])
                last.then_inc(s_varm_ready, 1)

            def centre_m(m):
                dve.wait_ge(s_rstdm_ready, nth(m))
                centre(xo, acc, mvm, rstdm).then_inc(s_out_ready, 1)

            dve.wait_ge(s_consts_in, N_CONSTS * 16)
            dve.wait_ge(s_zeroed, N_ZEROED)
            V.tensor_scalar(wo[:], wo[:], nw[:, 0:1], DK ** 0.5, ALU.mult, ALU.mult).then_inc(s_wo_scaled, 1)
            over_iterations(dve, {
                "proj": ("a", proj), "kt": ("a", kt), "pt": ("a", pt), "gp": ("a", gp), "y": ("a", y_), "yt": ("a", yt),
                "kty": ("a", kty), "ht": ("a", ht), "ok": ("a", ok), "softmax": ("a", softmax), "r": ("a", r),
                "og": ("a", og_), "ot": ("a", ot), "pr": ("a", pr), "x1": ("a", x1_),
                "x1c": ("b", x1c_), "nht": ("b", nht), "pqk": ("b", pqk), "sc": ("b", sc), "tr": ("b", tr),
                "pr2": ("b", pr2), "nh2": ("b", nh2), "lg": ("b", lgs), "gate": ("b", gate), "gt": ("b", gt),
                "b2": ("m", b2), "up": ("m", up), "down": ("m", down), "end0": ("m", end), "end1": ("m", centre_m)})
            assert not any(step[k] % n for k, n in (("a", DVE_A_OWN), ("b", DVE_B_OWN), ("m", DVE_M_OWN))), step

        @block.scalar
        def _(act):
            X = nc.scalar

            def proj(a):
                act.wait_ge(s_qk_ps, nth(a))
                X.activation(thqk[:].rearrange("p j n -> p (j n)"), bank[1], ACT.Tanh, scale=0.5).then_inc(s_th_qk, 1)

            def gf(a):
                act.wait_ge(s_g_ps, nth(a))
                X.activation(thg[:].rearrange("p t n -> p (t n)"), bank[0][:, 0:N], ACT.Tanh, scale=0.5).then_inc(s_th_g, 1)
                act.wait_ge(s_f_ps, nth(a))
                X.activation(thf[:], ps[:, 1:3, :], ACT.Tanh, scale=0.5)
                X.activation(lf[:], ps[:, 1:3, :], ACT.Abs).then_inc(s_act_own, 1)
                act.wait_ge(s_act_own, nth(a, 2, 1))
                X.activation(lf[:], lf[:], ACT.Exp, scale=-1.0).then_inc(s_act_own, 1)
                act.wait_ge(s_act_own, nth(a, 2, 2))
                X.activation(lf[:], lf[:], ACT.Ln, bias=1.0).then_inc(s_lnu_ready, 1)

            def gp(a):
                act.wait_ge(s_gp_ps, nth(a))
                X.activation(EY[:], ps[:, 1:3, :], ACT.Exp, scale=-1.0)
                X.activation(E[:], ps[:, 1:3, :], ACT.Exp).then_inc(s_ey_ready, 1)

            def dv_(a):
                act.wait_ge(s_dv_ps, nth(a))
                X.activation(dv[:].rearrange("p h c -> p (h c)"), bank[0][:, 0:4 * HP], ACT.Exp).then_inc(s_dv_ready, 1)

            def yt(a, t):
                act.wait_ge(s_yt_ps, nth(a, T, t + 1))
                X.activation(YTbd[0:64, t, :, 0, :], bank[1 + t][0:64, :].rearrange("p (h n) -> p h n", h=HP), ACT.Copy)\
                    .then_inc(s_yt_lo, 1)

            def softmax(a, t):
                act.wait_ge(s_sub_ready, nth(a, T, t + 1))
                X.activation(okE[:, t, :], okE[:, t, :], ACT.Exp).then_inc(s_exp_ready, 1)

            def qet(a, t):
                act.wait_ge(s_qet_ps, nth(a, T, t + 1))
                X.activation(QET[:, t].rearrange("p h n -> p (h n)"), bank[t], ACT.Copy).then_inc(s_qet_ready, 1)

            def ot(a):
                act.wait_ge(s_ot_ps, nth(a))
                X.activation(oT[:].rearrange("p t n -> p (t n)"), bank[2][:, 0:N], ACT.Copy).then_inc(s_ot_ready, 1)

            def nht(b):
                act.wait_ge(s_nht_ps, nth(b, 2, 1))
                X.activation(nxT[:], bank[3][:, 0:N], ACT.Identity, bias=ln1c[:, 1:2], scale=ln1c[:, 0:1])\
                    .then_inc(s_nxt_ready, 1)

            def mt(b):
                act.wait_ge(s_mt_ps, nth(b))
                if not first(b):
                    act.wait_ge(s_mx_stack, nth(b - 1, 48, 48))
                X.activation(mT[:], bank[3][0:3 * NH, 0:N], ACT.Copy).then_inc(s_mt_ready, 1)

            def exps(b, u):
                act.wait_ge(s_s2_ps, nth(b, 12, u + 1))
                g, w = divmod(u, 3)
                if g >= 2 and w == 0:
                    act.wait_ge(s_o2_ps, nth(b, G4, g - 1))
                X.activation(pT[:, g % 2, w, :], bank[3 + u % 2], ACT.Exp).then_inc(s_p_ready, 1)

            def av(b, g):
                if g % 2:
                    act.wait_ge(s_o2_ps, nth(b, G4, g + 1))
                    X.activation(oT2[:, g - 1:g + 1, :].rearrange("p g n -> p (g n)"), bank[5], ACT.Copy).then_inc(s_o2_ready, 1)

            def at_(b):
                act.wait_ge(s_aat_ps, nth(b))
                X.activation(aT[:].rearrange("p t n -> p (t n)"), bank[5][:, 0:N], ACT.Copy).then_inc(s_aat_ready, 1)

            def nh2(b):
                act.wait_ge(s_nht_ps, nth(b, 2, 2))
                if not first(b):
                    act.wait_ge(s_f1_ps, nth(b - 1, NU, NU))
                X.activation(nx2T[:], bank[4][:, 0:N], ACT.Identity, bias=ln2c[:, 1:2], scale=ln2c[:, 0:1])\
                    .then_inc(s_nxt_ready, 1)

            def lgs(b):
                act.wait_ge(s_gd_ready, nth(b))
                X.activation(gd[:, :, 1:2], gd[:, :, 0:1], ACT.Exp).then_inc(s_gexp_ready, 1)

            def gelu(m, e):
                act.wait_ge(s_h_raw, nth(m, NU, 2 * e + 2))
                X.activation(hx[:, e].rearrange("p f n -> p (f n)"), hx[:, e].rearrange("p f n -> p (f n)"), ACT.Gelu)\
                    .then_inc(s_h_ready, 1)

            act.wait_ge(s_consts_in, N_CONSTS * 16)
            act.wait_ge(s_zeroed, N_ZEROED)
            over_iterations(act, {
                "proj": ("a", proj), "gf": ("a", gf), "gp": ("a", gp), "dv": ("a", dv_), "yt": ("a", yt),
                "softmax": ("a", softmax), "qet": ("a", qet), "ot": ("a", ot),
                "nht": ("b", nht), "mt": ("b", mt), "s": ("b", exps), "av": ("b", av), "at": ("b", at_), "nh2": ("b", nh2),
                "lg": ("b", lgs), "gelu": ("m", gelu)})

        @block.gpsimd
        def _(pool):
            P = nc.gpsimd
            fills = [(kvm[:], 0.0), (YTbd[:], 0.0), (gates[:], 0.0), (Qst[:], 0.0), (Kst[:], 0.0), (vaug[:], 0.0),
                     (Kst[MAXROW:MAXROW + 3], 1.0), (vaug[:, :, :, HD:HD + 1], 1.0), (neghalf[:], -0.5), (eps[:], EPS),
                     (epsdk[:], EPS * DK), (mparts[:], 0.0)]
            assert len(fills) == N_ZEROED
            for n, (z, value) in enumerate(fills):
                pool.memset(z, value).then_inc(s_zeroed, 1)
                pool.wait_ge(s_zeroed, n + 1)
            pool.wait_ge(s_consts_in, N_CONSTS * 16)

            def proj(a):
                pool.wait_ge(s_qk2_ready, nth(a))
                for n in range(2):
                    qbd_unit(a, n)
                for t in range(T):
                    for c in range(2):
                        last = P.tensor_tensor(kvm[:, t, c, 1, :, :], vtok[:, t, :].rearrange("p (h n) -> p h n", h=HP),
                                               chunkmask[:, c:c + 1].unsqueeze(2).broadcast_to([128, HP, 32]), ALU.mult)
                last.then_inc(s_v_masked, 1)

            def qbd_unit(a, n):
                t, g = divmod(n, 2)
                if n >= 2:
                    pool.wait_ge(s_pt_ps, nth(a, 2 * T, n - 1))
                P.tensor_tensor(qbd[:, g], qk2[:, 0, t * 128:(t + 1) * 128].unsqueeze(1).broadcast_to([128, 4, 128]),
                                headmask[:, 4 * g:4 * g + 4].unsqueeze(2).broadcast_to([128, 4, 128]), ALU.mult)\
                    .then_inc(s_qbd_ready, 1)

            def pt(a, n):
                if n < 2:
                    qbd_unit(a, n + 2)

            def dv_(a):
                pool.wait_ge(s_dv_ready, nth(a))
                for c in range(NC_STATES):
                    for j in range(2):
                        last = P.tensor_tensor(dvm[:, c, j], pairmask[:].unsqueeze(1).broadcast_to([128, HP, 32]),
                                               dv[:, :, c:c + 1].broadcast_to([128, HP, 32]), ALU.mult)
                last.then_inc(s_dvm_ready, 1)

            def softmax(a, t):
                pool.wait_ge(s_exp_ready, nth(a, T, t + 1))
                P.tensor_tensor(thf[:, t, :], okE[:, t, :], E[:, t, :], ALU.mult).then_inc(s_qe_ready, 1)

            def og_(a):
                pool.wait_ge(s_gvar_ready, nth(a, 2, 1))
                P.tensor_tensor(rstdg[:], ms[:].rearrange("p t h -> p (t h)"), epsdk[:], ALU.add).then_inc(s_pool_a_own, 1)
                pool.wait_ge(s_pool_a_own, nth(a, 2, 1))
                P.tensor_tensor(rstdg[:], rstdg[:], neghalf[:], ALU.pow).then_inc(s_grstd_ready, 1)

            def pr(a):
                pool.wait_ge(s_gvar_ready, nth(a, 2, 2))
                P.tensor_tensor(rstdg[:, 0:T], mvg[:, :, 1], eps[:, 0:T], ALU.add).then_inc(s_pool_a_own, 1)
                pool.wait_ge(s_pool_a_own, nth(a, 2, 2))
                P.tensor_tensor(rstdg[:, 0:T], rstdg[:, 0:T], neghalf[:, 0:T], ALU.pow).then_inc(s_grstd_ready, 1)

            def root_b(b, k):
                pool.wait_ge(s_var_ready, nth(b, 2, k))
                P.tensor_tensor(rstd[:], mv[:, :, 1], eps[:, 0:T], ALU.add).then_inc(s_pool_b_own, 1)
                pool.wait_ge(s_pool_b_own, nth(b, 2, k))
                P.tensor_tensor(rstd[:], rstd[:], neghalf[:, 0:T], ALU.pow).then_inc(s_rstd_ready, 1)

            def end(m):
                pool.wait_ge(s_varm_ready, nth(m))
                P.tensor_tensor(rstdm[:], mvm[:, :, 1], eps[:, 0:T], ALU.add).then_inc(s_pool_m_own, 1)
                pool.wait_ge(s_pool_m_own, nth(m))
                P.tensor_tensor(rstdm[:], rstdm[:], neghalf[:, 0:T], ALU.pow).then_inc(s_rstdm_ready, 1)

            over_iterations(pool, {
                "proj": ("a", proj), "pt": ("a", pt), "dv": ("a", dv_), "softmax": ("a", softmax), "og": ("a", og_),
                "pr": ("a", pr), "x1c": ("b", lambda b: root_b(b, 1)), "pr2": ("b", lambda b: root_b(b, 2)),
                "end0": ("m", end)})


N_ZEROED = 12
DVE_A_OWN = 10
DVE_B_OWN = 25
DVE_M_OWN = 1


_OUTS = [((B, N, D), "float32")]


def _constants():
    s = np.arange(128)[:, None]
    t = np.arange(128)[None, :]
    c = {}
    f = np.float32
    c["c_ident"] = (s == t).astype(f)
    middle = t // C * C + C // 2 - 1
    same = s // C == t // C
    c["c_mid"] = (same * ((s > middle) & (s <= t)).astype(f) - same * ((s <= middle) & (s > t)).astype(f)).astype(f)
    inner = ((s >= C // 2) & (s < 128 - C // 2)).astype(f)
    late = (s >= 128 - C // 2).astype(f)
    early = (s < C // 2).astype(f)
    zero = np.zeros((128, 1), f)
    c["c_wincol"] = np.stack([np.concatenate([inner, late, zero, zero], 1), np.concatenate([zero, early, inner, zero], 1)], 1)
    c["c_causal"] = (same & (s <= t)).astype(f)
    h = np.arange(H)[None, :]
    c["c_headmask"] = (s // DK == h).astype(f)
    c["c_blockmask"] = (s // (2 * DK) == np.arange(HP)[None, :]).astype(f)
    c["c_pairmask"] = (s // M == np.arange(32)[None, :] // DK).astype(f)
    up = np.where(t > s, BIG, 0.0).astype(f)
    c["c_negmask"] = np.tile(up, (1, 4))
    c["c_negmaskT"] = np.tile(up.T, (1, 4))
    c["c_chunkmask"] = (s // C == np.arange(2)[None, :]).astype(f)
    c["c_iota"] = np.repeat(np.arange(NE, dtype=f)[None, :], 128, 0)
    return {k: np.ascontiguousarray(v) for k, v in c.items()}


def _padded(a, rows, cols, r0=0, c0=0):
    out = np.zeros((rows, cols), a.dtype)
    out[r0:r0 + a.shape[0], c0:c0 + a.shape[1]] = a
    return out


def kernel(**inputs):
    import ml_dtypes
    import concourse.bacc as _bacc
    from concourse.bass_utils import run_bass_kernel_spmd as _run

    g = {k: np.asarray(v) for k, v in inputs.items()}
    x = g["L0_attn_x"]
    wqkv, bqkv = g["L0_ffn_Wqkv"], g["L0_ffn_bqkv"]
    arrays = dict(
        x_tok=x,
        x_T=x.transpose(0, 2, 1),
        w_qk=np.stack([g["L0_attn_Wq"], g["L0_attn_Wk"]], 1),
        w_v=g["L0_attn_Wv"],
        w_fg=_padded(np.concatenate([g["L0_attn_Wf1"], g["L0_attn_Wg1"]], 1), 128, 128),
        w_f2=_padded(g["L0_attn_Wf2"], 128, HM),
        w_g2=_padded(g["L0_attn_Wg2"], 128, 128, DK),
        w_o=g["L0_attn_Wo"],
        norm_w=g["L0_attn_norm_w"][:, None],
        ln1=np.stack([g["L0_ffn_ln1_w"], g["L0_ffn_ln1_b"]], 1),
        ln2=np.stack([g["L0_ffn_ln2_w"], g["L0_ffn_ln2_b"]], 1),
        w2_qk=wqkv[:, :2 * D].reshape(D, 2, D),
        w2_v=wqkv[:, 2 * D:],
        b2_qk=bqkv[:2 * D].reshape(2, D).T,
        bv=bqkv[2 * D:],
        w2_o=g["L0_ffn_Wo"],
        bo=g["L0_ffn_bo"],
        gate_w=g["L0_ffn_gate_W"],
        fc1=g["L0_ffn_fc1_w"].transpose(2, 0, 1),
        fc1_b=g["L0_ffn_fc1_b"].reshape(NE * FC, 128).T,
        fc2=g["L0_ffn_fc2_w"].reshape(NE, D, FC, 128).transpose(3, 0, 2, 1),
        fc2_b=_padded(g["L0_ffn_fc2_b"], 128, 128),
    )
    arrays.update(_constants())
    arrays["c_identb"] = arrays["c_ident"].astype(ml_dtypes.bfloat16)
    for k in ("c_negmask", "c_negmaskT"):
        arrays[k] = arrays[k].astype(ml_dtypes.bfloat16)

    nc = _bacc.Bacc("TRN2", target_bir_lowering=False, num_devices=1)
    feeds, args = {}, {}
    for name, a in arrays.items():
        a = np.ascontiguousarray(a)
        feeds[f"in_{name}"] = a
        args[name] = nc.dram_tensor(f"in_{name}", a.shape, mybir.dt.from_np(a.dtype), kind="ExternalInput").ap()
    o = nc.dram_tensor("out_0_dram", _OUTS[0][0], F32, kind="ExternalOutput").ap()
    build(nc, out=o, **args)
    r = _run(nc, [feeds], core_ids=[0])
    return r.results[0]["out_0_dram"]
```
